# Optimizing a Trainium2 kernel written in Bass

```python
import numpy as np
import jax
import jax.numpy as jnp

def _softmax(x, axis=-1):
    return jax.nn.softmax(x, axis=axis)

def _gelu(x):
    return jax.nn.gelu(x, approximate=True)

def _silu(x):
    return jax.nn.silu(x)

def _sigmoid(x):
    return jax.nn.sigmoid(x)

def _layernorm(x, axis=-1, eps=1e-05):
    m = jnp.mean(x, axis=axis, keepdims=True)
    v = jnp.var(x, axis=axis, keepdims=True)
    return (x - m) / jnp.sqrt(v + eps)

def _scatter_add(tgt, idx, src, axis=0):
    return tgt.at[idx].add(src)

def _segment_sum(src, seg, n):
    return jax.ops.segment_sum(src, seg, n)
kernel_name = 'mk_macaron_d2_jaxref_r8_ef87c6'

def setup_inputs(seed: int=0):
    np.random.seed(seed)
    _w = jnp.asarray

    def _L0_attn_setup():
        import jax, jax.numpy as jnp
        import numpy as np
        NUM_HEADS = 32
        EPS = 1e-15
        key = jax.random.key(seed)
        k1, k2, k3, k4 = jax.random.split(key, 4)
        B, N, C = (8, 512, 128)
        x = jax.random.normal(k1, (B, N, C), dtype=jnp.float32)
        qkv_weight = jax.random.normal(k2, (3 * C, C), dtype=jnp.float32) * C ** (-0.5)
        proj_weight = jax.random.normal(k3, (C, C), dtype=jnp.float32) * C ** (-0.5)
        proj_bias = jax.random.normal(k4, (C,), dtype=jnp.float32) * 0.01
        return {'x': x, 'qkv_weight': qkv_weight, 'proj_weight': proj_weight, 'proj_bias': proj_bias}
    _L0_attn_in = _L0_attn_setup()

    def _L0_ffn_setup():
        import jax, jax.numpy as jnp
        import numpy as np
        import math
        D_IN = 128
        FEATURES = (512, 512, 128)
        BATCH, SEQ = (8, 256)

        def _conn_dense(kernel_bool, x):
            w = jnp.where(kernel_bool, jnp.float32(1.0), jnp.float32(-1.0))
            return x @ w
        key = jax.random.key(seed)
        kx, kk0, kk1, kk2 = jax.random.split(key, 4)
        x = jax.random.normal(kx, (BATCH, SEQ, D_IN), dtype=jnp.float32)
        k0 = jax.random.randint(kk0, (2 * D_IN, FEATURES[0]), 0, 2).astype(jnp.bool_)
        k1 = jax.random.randint(kk1, (FEATURES[0], FEATURES[1]), 0, 2).astype(jnp.bool_)
        k2 = jax.random.randint(kk2, (FEATURES[1], FEATURES[2]), 0, 2).astype(jnp.bool_)
        s0 = jnp.asarray(1.0 / math.sqrt(2 * D_IN), dtype=jnp.float32)
        s1 = jnp.asarray(1.0 / math.sqrt(FEATURES[0]), dtype=jnp.float32)
        s2 = jnp.asarray(1.0 / math.sqrt(FEATURES[1]), dtype=jnp.float32)
        return {'x': x, 'k0': k0, 'k1': k1, 'k2': k2, 's0': s0, 's1': s1, 's2': s2}
    _L0_ffn_in = _L0_ffn_setup()

    def _L1_attn_setup():
        import jax, jax.numpy as jnp
        import numpy as np
        B, S, H, NH, P = (1, 256, 128, 16, 2)
        D = H // NH
        SCALE = 1.0 / np.sqrt(D).astype(np.float32)

        def _lin(x, W, b):
            return x @ W + b

        def _split_heads(x):
            return x.reshape(*x.shape[:-2], x.shape[-2], NH, D).swapaxes(-3, -2)

        def _merge_heads(x):
            return x.swapaxes(-3, -2).reshape(*x.shape[:-3], x.shape[-2], H)
        key = jax.random.key(seed)
        ks = jax.random.split(key, 20)
        w = lambda k, i, o: jax.random.normal(k, (i, o), jnp.float32) * 0.02
        inp = {'hidden_states': jax.random.normal(ks[0], (B, S, H), jnp.float32), 'past_states': jax.random.normal(ks[1], (P, B, S, H), jnp.float32), 'Wq': w(ks[2], H, H), 'bq': jnp.zeros((H,), jnp.float32), 'Wk': w(ks[3], H, H), 'bk': jnp.zeros((H,), jnp.float32), 'Wv': w(ks[4], H, H), 'bv': jnp.zeros((H,), jnp.float32), 'Wo': w(ks[5], H, H), 'bo': jnp.zeros((H,), jnp.float32), 'Wrq': w(ks[6], H, H), 'brq': jnp.zeros((H,), jnp.float32), 'Wrk': w(ks[7], H, H), 'brk': jnp.zeros((H,), jnp.float32), 'Wrv': w(ks[8], H, H), 'brv': jnp.zeros((H,), jnp.float32), 'Wg': w(ks[9], 2 * H, H), 'bg': jnp.zeros((H,), jnp.float32)}
        return inp
    _L1_attn_in = _L1_attn_setup()

    def _L1_ffn_setup():
        import jax, jax.numpy as jnp
        import numpy as np
        DIM = 128
        HID = 4 * DIM
        N_EXPERTS = 8
        TOP_K = 2
        key = jax.random.key(seed)
        ks = jax.random.split(key, 8)
        s = lambda fan_in: 1.0 / np.sqrt(fan_in)
        x = jax.random.normal(ks[0], (2, 256, DIM), dtype=jnp.float32)
        Wr = jax.random.uniform(ks[1], (DIM, N_EXPERTS), jnp.float32, -s(DIM), s(DIM))
        br = jnp.zeros((N_EXPERTS,), jnp.float32)
        W1 = jax.random.uniform(ks[2], (N_EXPERTS, DIM, HID), jnp.float32, -s(DIM), s(DIM))
        b1 = jnp.zeros((N_EXPERTS, HID), jnp.float32)
        W2 = jax.random.uniform(ks[3], (N_EXPERTS, HID, DIM), jnp.float32, -s(HID), s(HID))
        b2 = jnp.zeros((N_EXPERTS, DIM), jnp.float32)
        return {'x': x, 'Wr': Wr, 'br': br, 'W1': W1, 'b1': b1, 'W2': W2, 'b2': b2}
    _L1_ffn_in = _L1_ffn_setup()
    _d = {'L0_attn_x': _L0_attn_in['x'], 'L0_attn_qkv_weight': _L0_attn_in['qkv_weight'], 'L0_attn_proj_weight': _L0_attn_in['proj_weight'], 'L0_attn_proj_bias': _L0_attn_in['proj_bias'], 'L0_ffn_k0': _L0_ffn_in['k0'], 'L0_ffn_k1': _L0_ffn_in['k1'], 'L0_ffn_k2': _L0_ffn_in['k2'], 'L0_ffn_s0': _L0_ffn_in['s0'], 'L0_ffn_s1': _L0_ffn_in['s1'], 'L0_ffn_s2': _L0_ffn_in['s2'], 'L1_attn_past_states': _L1_attn_in['past_states'], 'L1_attn_Wq': _L1_attn_in['Wq'], 'L1_attn_bq': _L1_attn_in['bq'], 'L1_attn_Wk': _L1_attn_in['Wk'], 'L1_attn_bk': _L1_attn_in['bk'], 'L1_attn_Wv': _L1_attn_in['Wv'], 'L1_attn_bv': _L1_attn_in['bv'], 'L1_attn_Wo': _L1_attn_in['Wo'], 'L1_attn_bo': _L1_attn_in['bo'], 'L1_attn_Wrq': _L1_attn_in['Wrq'], 'L1_attn_brq': _L1_attn_in['brq'], 'L1_attn_Wrk': _L1_attn_in['Wrk'], 'L1_attn_brk': _L1_attn_in['brk'], 'L1_attn_Wrv': _L1_attn_in['Wrv'], 'L1_attn_brv': _L1_attn_in['brv'], 'L1_attn_Wg': _L1_attn_in['Wg'], 'L1_attn_bg': _L1_attn_in['bg'], 'L1_ffn_Wr': _L1_ffn_in['Wr'], 'L1_ffn_br': _L1_ffn_in['br'], 'L1_ffn_W1': _L1_ffn_in['W1'], 'L1_ffn_b1': _L1_ffn_in['b1'], 'L1_ffn_W2': _L1_ffn_in['W2'], 'L1_ffn_b2': _L1_ffn_in['b2']}
    _x0 = _d['L0_attn_x']
    _d['L0_attn_x'] = jax.random.normal(jax.random.fold_in(jax.random.key(seed), 1), (16, 256, 128), dtype=_x0.dtype)
    del _x0
    return _d

def reference(L0_attn_x, L0_attn_qkv_weight, L0_attn_proj_weight, L0_attn_proj_bias, L0_ffn_k0, L0_ffn_k1, L0_ffn_k2, L0_ffn_s0, L0_ffn_s1, L0_ffn_s2, L1_attn_past_states, L1_attn_Wq, L1_attn_bq, L1_attn_Wk, L1_attn_bk, L1_attn_Wv, L1_attn_bv, L1_attn_Wo, L1_attn_bo, L1_attn_Wrq, L1_attn_brq, L1_attn_Wrk, L1_attn_brk, L1_attn_Wrv, L1_attn_brv, L1_attn_Wg, L1_attn_bg, L1_ffn_Wr, L1_ffn_br, L1_ffn_W1, L1_ffn_b1, L1_ffn_W2, L1_ffn_b2):

    def _L0_attn_ref(x, qkv_weight, proj_weight, proj_bias):
        import jax, jax.numpy as jnp
        import numpy as np
        NUM_HEADS = 32
        EPS = 1e-15
        B, N, C = x.shape
        H = NUM_HEADS
        D = C // H
        qkv = jax.nn.relu(jnp.einsum('bnc,oc->bno', x, qkv_weight))
        qkv = qkv.reshape(B, N, 3, H, D)
        q, k, v = (qkv[:, :, 0], qkv[:, :, 1], qkv[:, :, 2])
        v_pad = jnp.concatenate([v, jnp.ones((B, N, H, 1), dtype=v.dtype)], axis=-1)
        vk = jnp.einsum('bnhe,bnhd->bhed', v_pad.astype(jnp.float32), k.astype(jnp.float32))
        vk_q = jnp.einsum('bhed,bnhd->bnhe', vk, q.astype(jnp.float32))
        proj_input = (vk_q[..., :D] / (vk_q[..., D:] + EPS)).astype(qkv.dtype)
        proj_input = proj_input.reshape(B, N, C)
        y = jnp.einsum('bnc,oc->bno', proj_input, proj_weight) + proj_bias
        return y

    def _L0_ffn_ref(x, k0, k1, k2, s0, s1, s2):
        import jax, jax.numpy as jnp
        import numpy as np
        import math
        D_IN = 128
        FEATURES = (512, 512, 128)
        BATCH, SEQ = (8, 256)

        def _conn_dense(kernel_bool, x):
            w = jnp.where(kernel_bool, jnp.float32(1.0), jnp.float32(-1.0))
            return x @ w
        h = jnp.concatenate([x, -x], axis=-1)
        h = s0 * _conn_dense(k0, h)
        h = jax.nn.relu(h) * 2
        h = s1 * _conn_dense(k1, h)
        h = jax.nn.relu(h) * 2
        h = s2 * _conn_dense(k2, h)
        return h

    def _L1_attn_ref(hidden_states, past_states, Wq, bq, Wk, bk, Wv, bv, Wo, bo, Wrq, brq, Wrk, brk, Wrv, brv, Wg, bg):
        import jax, jax.numpy as jnp
        import numpy as np
        B, S, H, NH, P = (1, 256, 128, 16, 2)
        D = H // NH
        SCALE = 1.0 / np.sqrt(D).astype(np.float32)

        def _lin(x, W, b):
            return x @ W + b

        def _split_heads(x):
            return x.reshape(*x.shape[:-2], x.shape[-2], NH, D).swapaxes(-3, -2)

        def _merge_heads(x):
            return x.swapaxes(-3, -2).reshape(*x.shape[:-3], x.shape[-2], H)
        q = _split_heads(_lin(hidden_states, Wq, bq))
        k = _split_heads(_lin(hidden_states, Wk, bk))
        v = _split_heads(_lin(hidden_states, Wv, bv))
        scores = jnp.einsum('bhsd,bhtd->bhst', q, k) * SCALE
        attn = jax.nn.softmax(scores, axis=-1)
        ctx = jnp.einsum('bhst,bhtd->bhsd', attn, v)
        output = _lin(_merge_heads(ctx), Wo, bo)
        rq = _split_heads(_lin(output, Wrq, brq))
        rk = _split_heads(_lin(past_states, Wrk, brk))
        rv = _split_heads(_lin(past_states, Wrv, brv))
        rscores = jnp.einsum('bhsd,pbhtd->pbhst', rq, rk) * SCALE
        rattn = jax.nn.softmax(rscores, axis=-1)
        rctx = jnp.einsum('pbhst,pbhtd->pbhsd', rattn, rv)
        recursive_output = _merge_heads(rctx).mean(axis=0)
        gate = jax.nn.sigmoid(_lin(jnp.concatenate([output, recursive_output], axis=-1), Wg, bg))
        output = output * (1.0 - gate) + recursive_output * gate
        return output

    def _L1_ffn_ref(x, Wr, br, W1, b1, W2, b2):
        import jax, jax.numpy as jnp
        import numpy as np
        DIM = 128
        HID = 4 * DIM
        N_EXPERTS = 8
        TOP_K = 2
        B, S, D = x.shape
        xf = x.reshape(-1, D)
        T = xf.shape[0]
        logits = xf @ Wr + br
        topw, sel = jax.lax.top_k(logits, TOP_K)
        topw = jax.nn.softmax(topw, axis=-1)
        w_full = jnp.zeros((T, N_EXPERTS), xf.dtype).at[jnp.arange(T)[:, None], sel].add(topw)
        h = jax.nn.gelu(jnp.einsum('td,edh->teh', xf, W1) + b1, approximate=False)
        y = jnp.einsum('teh,ehd->ted', h, W2) + b2
        out = jnp.einsum('ted,te->td', y, w_full)
        return out.reshape(B, S, D)
    x = L0_attn_x
    x = x + 0.5 * _L0_ffn_ref(_layernorm(x, axis=-1), L0_ffn_k0, L0_ffn_k1, L0_ffn_k2, L0_ffn_s0, L0_ffn_s1, L0_ffn_s2)
    x = x + _L0_attn_ref(_layernorm(x, axis=-1), L0_attn_qkv_weight, L0_attn_proj_weight, L0_attn_proj_bias)
    x = x + 0.5 * _L0_ffn_ref(_layernorm(x, axis=-1), L0_ffn_k0, L0_ffn_k1, L0_ffn_k2, L0_ffn_s0, L0_ffn_s1, L0_ffn_s2)
    x = x + 0.5 * _L1_ffn_ref(_layernorm(x, axis=-1), L1_ffn_Wr, L1_ffn_br, L1_ffn_W1, L1_ffn_b1, L1_ffn_W2, L1_ffn_b2)
    x = x + _L1_attn_ref(_layernorm(x, axis=-1), L1_attn_past_states, L1_attn_Wq, L1_attn_bq, L1_attn_Wk, L1_attn_bk, L1_attn_Wv, L1_attn_bv, L1_attn_Wo, L1_attn_bo, L1_attn_Wrq, L1_attn_brq, L1_attn_Wrk, L1_attn_brk, L1_attn_Wrv, L1_attn_brv, L1_attn_Wg, L1_attn_bg)
    x = x + 0.5 * _L1_ffn_ref(_layernorm(x, axis=-1), L1_ffn_Wr, L1_ffn_br, L1_ffn_W1, L1_ffn_b1, L1_ffn_W2, L1_ffn_b2)
    return x

_drawn_inputs = setup_inputs


def setup_inputs(seed=0):
    import zlib

    import numpy as np

    out = dict(_drawn_inputs(seed))
    spreads = {'L1_attn_bq': (0.0, 0.8),
     'L1_attn_bk': (0.0, 0.8),
     'L1_attn_bv': (0.0, 0.8),
     'L1_attn_bo': (0.0, 0.361),
     'L1_attn_brq': (0.0, 0.8),
     'L1_attn_brk': (0.0, 0.8),
     'L1_attn_brv': (0.0, 0.323),
     'L1_attn_bg': (0.0, 0.8),
     'L1_ffn_br': (0.0, 0.305),
     'L1_ffn_b1': (0.0, 0.657),
     'L1_ffn_b2': (0.0, 0.1)}
    factors = {'L0_attn_proj_bias': 7.958,
     'L1_attn_past_states': 8.0,
     'L1_attn_Wq': 8.0,
     'L1_attn_Wk': 8.0,
     'L1_attn_Wv': 6.366,
     'L1_attn_Wo': 6.306,
     'L1_attn_Wrq': 8.0,
     'L1_attn_Wrk': 8.0,
     'L1_attn_Wrv': 8.0,
     'L1_attn_Wg': 8.0}
    for name, (base, spread) in spreads.items():
        noise = np.random.default_rng([zlib.crc32(name.encode()), seed]).standard_normal(out[name].shape)
        drawn = base * np.exp(spread * noise) if base else spread * noise
        out[name] = jnp.asarray(drawn.astype(out[name].dtype))
    for name, factor in factors.items():
        out[name] = (out[name] * factor).astype(out[name].dtype)
    return out
```

```python
from contextlib import ExitStack

import concourse.bass as bass
from concourse import mybir

F32 = mybir.dt.float32
F32R = mybir.dt.float32r
U8 = mybir.dt.uint8
U32 = mybir.dt.uint32
ALU = mybir.AluOpType
ACT = mybir.ActivationFunctionType
AX = mybir.AxisListType

P = 128
BATCH, SEQ, C = 16, 256, 128
T = BATCH * SEQ
TILES = T // P
CT = 4
CH = CT * P
NCH = T // CH
HB = 4
LN_EPS = 1e-5
LIN_EPS = 1e-15
NE = 8
NH = 16
D = C // NH
NG = 4
PAST = 2
SCALE = float(1.0 / (D ** 0.5))
BT = SEQ // P
VW = D + 1


class Buffers:
    pass


def stats_vector(v, nc, b, s, layer):
    done = s["stats"]
    n = 0
    mean, diff, var, sd, r, t = (b.ln[:, k, :] for k in range(6))
    even, odd = b.bn[:, :, 0:3], b.bn[:, :, 3:6]
    v.wait_ge(b.bn_done, TILES * (layer + 1))
    nc.vector.tensor_tensor(mean, even[:, :, 1], odd[:, :, 1], ALU.add).then_inc(done, 1)
    nc.vector.tensor_tensor(diff, even[:, :, 1], odd[:, :, 1], ALU.subtract).then_inc(done, 1)
    nc.vector.tensor_tensor(var, even[:, :, 2], odd[:, :, 2], ALU.add).then_inc(done, 1)
    v.wait_ge(done, 3)
    nc.vector.tensor_scalar(mean, mean, 0.5, None, ALU.mult).then_inc(done, 1)
    nc.vector.tensor_tensor(diff, diff, diff, ALU.mult).then_inc(done, 1)
    nc.vector.tensor_scalar(var, var, 1.0 / C, LN_EPS, ALU.mult, ALU.add).then_inc(done, 1)
    v.wait_ge(done, 6)
    nc.vector.scalar_tensor_tensor(var, diff, 0.25, var, ALU.mult, ALU.add).then_inc(s["var"], 1)
    v.wait_ge(s["sd"], 1)
    nc.vector.reciprocal(r, sd).then_inc(done, 1)
    v.wait_ge(done, 7)
    nc.vector.tensor_tensor(t, r, r, ALU.mult).then_inc(done, 1)
    v.wait_ge(done, 8)
    nc.vector.tensor_tensor(t, t, var, ALU.mult).then_inc(done, 1)
    v.wait_ge(done, 9)
    nc.vector.tensor_scalar(t, t, -0.5, 1.5, ALU.mult, ALU.add).then_inc(done, 1)
    v.wait_ge(done, 10)
    nc.vector.tensor_tensor(r, r, t, ALU.mult).then_inc(done, 1)
    v.wait_ge(done, 11)


def stats_scalar(act, nc, b, s):
    act.wait_ge(s["var"], 1)
    nc.scalar.activation(b.ln[:, 3, :], b.ln[:, 2, :], ACT.Sqrt).then_inc(s["sd"], 1)


def normalise(nc, b, out, tile):
    return nc.vector.tensor_scalar(out, b.x[:, tile, :], b.ln[:, 0, tile], b.ln[:, 4, tile],
                                   ALU.subtract, ALU.mult)


STATS_SEMS = ["stats", "var", "sd", "passed"]


FFN_SEMS = STATS_SEMS + ["xn_ready", "xt_full", "x_hi", "x_split", "z_full", "z_hi", "z_split", "y_full",
                         "y_copied", "yt_full", "x_added"]
FFN_XT, FFN_Y, FFN_YT = 4, 5, 6


def ffn_tensor(pe, nc, b, s):
    bank = b.banks

    def turn_x(c):
        pe.wait_ge(s["xn_ready"], c + 1)
        if not (isinstance(c, int) and c == 0):
            pe.wait_ge(s["x_split"], c)
        for j in range(CT):
            mm = pe.transpose(bank[:, FFN_XT, P * j:P * j + P], b.xn[:, j, :], b.ident[:, :])
        mm.then_inc(s["xt_full"], 1)

    def first(c):
        pe.wait_ge(s["x_split"], c + 1)
        for m in range(HB):
            if not (isinstance(c, int) and c == 0):
                pe.wait_ge(s["z_split"], 8 * c + m - 3)
            w = b.k0[:, P * m:P * m + P]
            pe.matmul(bank[:, m, :], w, b.xh[:, :], start=True, stop=False)
            pe.matmul(bank[:, m, :], w, b.xl[:, :], start=False, stop=True).then_inc(s["z_full"], 1)

    def middle(c, m):
        for k in range(HB):
            if m == 0:
                pe.wait_ge(s["z_split"], 8 * c + k + 1)
            w = b.k1[:, k, P * m:P * m + P]
            pe.matmul(bank[:, m, :], w, b.h_hi[:, k, :], start=k == 0, stop=False)
            mm = pe.matmul(bank[:, m, :], w, b.h_lo[:, k, :], start=False, stop=k == HB - 1)
        mm.then_inc(s["z_full"], 1)

    def last(c):
        pe.wait_ge(s["y_copied"], c + 1)
        for k in range(HB):
            pe.wait_ge(s["z_split"], 8 * c + 5 + k)
            pe.matmul(bank[:, FFN_Y, :], b.k2[:, k, :], b.g_hi[:, k, :], start=k == 0, stop=False)
            mm = pe.matmul(bank[:, FFN_Y, :], b.k2[:, k, :], b.g_lo[:, k, :], start=False, stop=k == HB - 1)
        mm.then_inc(s["y_full"], 1)

    def turn_y(c):
        pe.wait_ge(s["y_copied"], c + 2)
        pe.wait_ge(s["x_added"], c + 1)
        for j in range(CT):
            mm = pe.transpose(bank[:, FFN_YT, P * j:P * j + P], b.y[:, P * j:P * j + P], b.ident[:, :])
        mm.then_inc(s["yt_full"], 1)

    turn_x(0)
    first(0)
    for m in range(HB):
        middle(0, m)
    turn_x(1)
    first(1)
    with pe.Fori(0, NCH - 2) as i:
        last(i)
        middle(i + 1, 0)
        turn_y(i)
        for m in range(1, HB):
            middle(i + 1, m)
        turn_x(i + 2)
        first(i + 2)
    last(NCH - 2)
    middle(NCH - 1, 0)
    turn_y(NCH - 2)
    for m in range(1, HB):
        middle(NCH - 1, m)
    last(NCH - 1)
    turn_y(NCH - 1)


def ffn_scalar(act, nc, b, s):
    bank = b.banks
    stats_scalar(act, nc, b, s)
    act.sem_inc(s["y_copied"], 1)

    def x_hi(c):
        act.wait_ge(s["xt_full"], c + 1)
        nc.scalar.copy(b.xh[:, :], bank[:, FFN_XT, :]).then_inc(s["x_hi"], 1)

    def relu(n, m, out):
        act.wait_ge(s["z_full"], n + 1)
        nc.scalar.activation(out[:, m, :], bank[:, m, :], ACT.Relu).then_inc(s["z_hi"], 1)

    def y_copy(c):
        act.wait_ge(s["y_full"], c + 1)
        nc.scalar.activation(b.y[:, :], bank[:, FFN_Y, :], ACT.Identity,
                             scale=b.ffn_scale[:, 0:1]).then_inc(s["y_copied"], 1)

    x_hi(0)
    for m in range(HB):
        relu(m, m, b.h_hi)
    for m in range(HB):
        relu(HB + m, m, b.g_hi)
    x_hi(1)
    for m in range(HB):
        relu(8 + m, m, b.h_hi)
    with act.Fori(0, NCH - 2) as i:
        y_copy(i)
        for m in range(HB):
            relu(8 * i + 12 + m, m, b.g_hi)
        x_hi(i + 2)
        for m in range(HB):
            relu(8 * i + 16 + m, m, b.h_hi)
    y_copy(NCH - 2)
    for m in range(HB):
        relu(8 * (NCH - 1) + 4 + m, m, b.g_hi)
    y_copy(NCH - 1)


def ffn_vector(v, nc, b, s, layer):
    bank = b.banks
    stats_vector(v, nc, b, s, layer)
    v.sem_inc(s["x_added"], 1)

    def xn(c):
        if not (isinstance(c, int) and c == 0):
            v.wait_ge(s["xt_full"], c)
        for j in range(CT):
            ins = normalise(nc, b, b.xn[:, j, :], bass.ds(c * CT + j, 1))
        ins.then_inc(s["xn_ready"], 1)

    def x_lo(c):
        v.wait_ge(s["x_hi"], c + 1)
        nc.vector.tensor_tensor(b.xl[:, :], bank[:, FFN_XT, :], b.xh[:, :].bitcast(F32),
                                ALU.subtract).then_inc(s["x_split"], 1)

    def relu_lo(n, m, hi, lo):
        v.wait_ge(s["z_hi"], n + 1)
        nc.vector.scalar_tensor_tensor(lo[:, m, :], bank[:, m, :], 0.0, hi[:, m, :].bitcast(F32),
                                       ALU.max, ALU.subtract).then_inc(s["z_split"], 1)

    def add(c):
        v.wait_ge(s["yt_full"], c + 1)
        xs = b.xc[:, bass.ds(c, 1), :]
        nc.vector.tensor_tensor(xs, xs, bank[:, FFN_YT:FFN_YT + 1, :], ALU.add).then_inc(s["x_added"], 1)
        v.wait_ge(s["x_added"], c + 2)
        for j in range(CT):
            nc.vector.bn_stats(b.bn[:, bass.ds(c * CT + j, 1), :], b.x[:, bass.ds(c * CT + j, 1), :]).then_inc(b.bn_done, 1)

    xn(0)
    x_lo(0)
    for m in range(HB):
        relu_lo(m, m, b.h_hi, b.h_lo)
    xn(1)
    for m in range(HB):
        relu_lo(HB + m, m, b.g_hi, b.g_lo)
    x_lo(1)
    for m in range(HB):
        relu_lo(8 + m, m, b.h_hi, b.h_lo)
    with v.Fori(0, NCH - 2) as i:
        xn(i + 2)
        relu_lo(8 * i + 12, 0, b.g_hi, b.g_lo)
        add(i)
        for m in range(1, HB):
            relu_lo(8 * i + 12 + m, m, b.g_hi, b.g_lo)
        x_lo(i + 2)
        for m in range(HB):
            relu_lo(8 * i + 16 + m, m, b.h_hi, b.h_lo)
    relu_lo(8 * NCH - 4, 0, b.g_hi, b.g_lo)
    add(NCH - 2)
    for m in range(1, HB):
        relu_lo(8 * NCH - 4 + m, m, b.g_hi, b.g_lo)
    add(NCH - 1)


LIN_SEMS = STATS_SEMS + ["xn_ready", "xt_full", "xt_ready", "q_full", "q_ready", "kv_full", "kv_ready",
                         "sum_full", "sum_ready", "ratio_full", "den", "inv", "ratio_ready", "y_full", "x_added"]
LIN_XT, LIN_Q, LIN_KV, LIN_SUM, LIN_NUM = 0, 1, 2, 4, 6


def lin_tensor(pe, nc, b, s):
    bank = b.banks
    with pe.Fori(0, NCH) as c:
        pe.wait_ge(s["xn_ready"], c + 1)
        pe.wait_ge(s["x_added"], c + 1)
        for j in range(CT):
            mm = pe.transpose(bank[:, LIN_XT, P * j:P * j + P], b.xn[:, j, :], b.ident[:, :])
        mm.then_inc(s["xt_full"], 1)
        pe.wait_ge(s["xt_ready"], c + 1)
        for half in range(2):
            for j in range(2):
                t = 2 * half + j
                mm = pe.matmul(bank[:, LIN_KV + half, 256 * j:256 * j + 256], b.xT[:, P * t:P * t + P],
                               b.wkv0[:, :], start=True, stop=True)
            mm.then_inc(s["kv_full"], 1)
        pe.matmul(bank[:, LIN_Q, :], b.wq0[:, :], b.xT[:, :], start=True, stop=True).then_inc(s["q_full"], 1)
        for e in range(2):
            pe.wait_ge(s["kv_ready"], 2 * c + e + 1)
            for j in range(2):
                t = 2 * e + j
                mm = pe.matmul(bank[:, LIN_SUM + e, 0:256], b.kv[:, t, 0:P], b.kv[:, t, P:3 * P],
                               start=j == 0, stop=j == 1)
            mm.then_inc(s["sum_full"], 1)
        pe.wait_ge(s["q_ready"], c + 1)
        for e in range(2):
            pe.wait_ge(s["sum_ready"], 2 * c + e + 1)
            rhs = b.qT[:, SEQ * e:SEQ * e + SEQ]
            pe.matmul(bank[:, LIN_NUM + e, SEQ:2 * SEQ], b.kvm[:, e, P:2 * P], rhs, start=True, stop=True)
            pe.matmul(bank[:, LIN_NUM + e, 0:SEQ], b.kvm[:, e, 0:P], rhs,
                      start=True, stop=True).then_inc(s["ratio_full"], 1)
        for e in range(2):
            pe.wait_ge(s["ratio_ready"], 2 * c + e + 1)
            for j in range(2):
                t = 2 * e + j
                pe.matmul(bank[:, LIN_XT, P * t:P * t + P], b.ratio[:, P * t:P * t + P], b.wp0[:, :],
                          start=True, stop=False)
                mm = pe.matmul(bank[:, LIN_XT, P * t:P * t + P], b.ones[0:1, 0:P], b.pb0[0:1, :],
                               start=False, stop=True)
        mm.then_inc(s["y_full"], 1)


def lin_scalar(act, nc, b, s):
    bank = b.banks
    stats_scalar(act, nc, b, s)
    with act.Fori(0, NCH) as c:
        act.wait_ge(s["xt_full"], c + 1)
        nc.scalar.copy(b.xT[:, :], bank[:, LIN_XT, :]).then_inc(s["xt_ready"], 1)
        for half in range(2):
            act.wait_ge(s["kv_full"], 2 * c + half + 1)
            nc.scalar.activation(b.kv[:, 2 * half:2 * half + 2, 0:256],
                                 bank[:, LIN_KV + half, :].rearrange("p (t f) -> p t f", t=2),
                                 ACT.Relu).then_inc(s["kv_ready"], 1)
        act.wait_ge(s["q_full"], c + 1)
        nc.scalar.activation(b.qT[:, :], bank[:, LIN_Q, :], ACT.Relu).then_inc(s["q_ready"], 1)


def lin_vector(v, nc, b, s, layer):
    bank = b.banks
    stats_vector(v, nc, b, s, layer)
    v.sem_inc(s["x_added"], 1)
    for j in range(CT):
        ins = normalise(nc, b, b.xn[:, j, :], bass.ds(j, 1))
    ins.then_inc(s["xn_ready"], 1)

    def attend(c):
        for e in range(2):
            v.wait_ge(s["sum_full"], 2 * c + e + 1)
            nc.vector.tensor_tensor(b.kvm[:, e, :], bank[:, LIN_SUM + e, 0:256], b.blockmask[:, :],
                                    ALU.mult).then_inc(s["sum_ready"], 1)
        for e in range(2):
            v.wait_ge(s["ratio_full"], 2 * c + e + 1)
            sl = slice(SEQ * e, SEQ * e + SEQ)
            nc.vector.tensor_scalar(b.rec[:, sl], bank[:, LIN_NUM + e, SEQ:2 * SEQ], LIN_EPS, None, ALU.add).then_inc(s["den"], 1)
            v.wait_ge(s["den"], 2 * c + e + 1)
            nc.vector.reciprocal(b.rec[:, sl], b.rec[:, sl]).then_inc(s["inv"], 1)
            v.wait_ge(s["inv"], 2 * c + e + 1)
            nc.vector.tensor_tensor(b.ratio[:, sl], bank[:, LIN_NUM + e, 0:SEQ], b.rec[:, sl],
                                    ALU.mult).then_inc(s["ratio_ready"], 1)

    def add(c):
        v.wait_ge(s["y_full"], c + 1)
        xs = b.xc[:, bass.ds(c, 1), :]
        nc.vector.tensor_tensor(xs, xs, bank[:, LIN_XT:LIN_XT + 1, :], ALU.add).then_inc(s["x_added"], 1)
        v.wait_ge(s["x_added"], c + 2)
        for j in range(CT):
            nc.vector.bn_stats(b.bn[:, bass.ds(c * CT + j, 1), :], b.x[:, bass.ds(c * CT + j, 1), :]).then_inc(b.bn_done, 1)

    with v.Fori(0, NCH - 1) as c:
        v.wait_ge(s["xt_full"], c + 1)
        for j in range(CT):
            ins = normalise(nc, b, b.xn[:, j, :], bass.ds((c + 1) * CT + j, 1))
        ins.then_inc(s["xn_ready"], 1)
        attend(c)
        add(c)
    attend(NCH - 1)
    add(NCH - 1)


MOE_SEMS = STATS_SEMS + ["xn_ready", "xt_full", "xt_ready", "x_hi", "x_split", "lg_full", "lg_ready", "rt",
                         "rt_diff", "rt_exp", "rt_top", "rt_idx", "rt_w2", "w_ready", "weights_in", "weights_hi", "weights_split",
                         "z_full", "z_gelu", "h_hi", "h_split", "h_used", "y_copied", "yt_full",
                         "x_added"]
MOE_XT, MOE_LG = 6, 7
MOE_Y, MOE_YT = 4, 5
RT_STEPS = 8


def moe_sync(sp, nc, b, s):
    with sp.Fori(0, NE) as e:
        sp.wait_ge(s["weights_split"], 2 * e + 2)
        sp.dma_start(b.w1_raw[:, :], b.W1[bass.ds(e, 1), :, :].rearrange("o c h -> (o c) h")).then_inc(s["weights_in"], 16)
        sp.dma_start(b.w2_raw[:, :, :],
                     b.W2[bass.ds(e, 1), :, :].rearrange("o (k p) c -> p (o k) c", p=P)).then_inc(s["weights_in"], 16)


def moe_gpsimd(pool, nc, b, s):
    def split(e, half, reused):
        pool.wait_ge(s["weights_in"], 32 * e + 32)
        if reused:
            pool.wait_ge(s["h_used"], 32 * e - 28)
        pool.sem_inc(s["passed"], 1)
        w2 = b.w2_raw[:, :, :].rearrange("p k c -> p (k c)")
        nc.gpsimd.tensor_copy(b.w1h[:, half, :], b.w1_raw[:, :]).then_inc(s["weights_hi"], 1)
        nc.gpsimd.tensor_copy(b.w2h[:, half, :], w2).then_inc(s["weights_hi"], 1)
        pool.wait_ge(s["weights_hi"], 2 * e + 1)
        nc.gpsimd.tensor_tensor(b.w1l[:, half, :], b.w1_raw[:, :], b.w1h[:, half, :].bitcast(F32),
                                ALU.subtract).then_inc(s["weights_split"], 1)
        pool.wait_ge(s["weights_hi"], 2 * e + 2)
        nc.gpsimd.tensor_tensor(b.w2l[:, half, :], w2, b.w2h[:, half, :].bitcast(F32),
                                ALU.subtract).then_inc(s["weights_split"], 1)

    def hi(z, m):
        pool.wait_ge(s["z_gelu"], z + 1 + HB)
        pool.wait_ge(s["h_used"], z + 1)
        pool.sem_inc(s["passed"], 1)
        nc.gpsimd.tensor_copy(b.h_hi[:, m, :], b.h_raw[:, m, :]).then_inc(s["h_hi"], 1)

    pool.sem_inc(s["weights_split"], 2)
    split(0, 0, False)
    with pool.Fori(0, NE // 2 - 1) as pair:
        for half in range(2):
            e = 2 * pair + half
            for c in range(2):
                for m in range(HB):
                    hi(32 * e + 4 * c + m, m)
            split(e + 1, 1 - half, True)
            with pool.Fori(2, NCH) as c:
                for m in range(HB):
                    hi(32 * e + 4 * c + m, m)
    with pool.Fori(0, NCH) as c:
        for m in range(HB):
            hi(32 * (NE - 2) + 4 * c + m, m)
    split(NE - 1, 1, True)
    with pool.Fori(0, NCH) as c:
        for m in range(HB):
            hi(32 * (NE - 1) + 4 * c + m, m)


def moe_tensor(pe, nc, b, s):
    bank = b.banks
    pe.sem_inc(s["h_used"], HB)
    pe.sem_inc(s["lg_full"], 1)
    pe.sem_inc(s["yt_full"], 1)
    with pe.Fori(0, NCH) as c:
        pe.wait_ge(s["xn_ready"], c + 1)
        pe.wait_ge(s["x_split"], c + 1)
        for j in range(CT):
            mm = pe.transpose(bank[:, MOE_XT, P * j:P * j + P], b.xn[:, j, :], b.ident[:, :])
        mm.then_inc(s["xt_full"], 1)
        pe.wait_ge(s["xt_ready"], c + 1)
        pe.wait_ge(s["lg_ready"], c + 1)
        for j in range(CT):
            out = bank[:, MOE_LG, NE * j:NE * j + NE]
            pe.matmul(out, b.xT[:, P * j:P * j + P], b.wr[:, :], start=True, stop=False)
            mm = pe.matmul(out, b.ones[0:1, 0:P], b.br[0:1, :], start=False, stop=True)
        mm.then_inc(s["lg_full"], 1)

    def first(e, c, m, half):
        pe.wait_ge(s["z_gelu"], 32 * e + 4 * c + m + 1)
        wh, wl = b.w1h[:, half, P * m:P * m + P], b.w1l[:, half, P * m:P * m + P]
        xh, xl = b.xh_all[:, bass.ds(c * CH, CH)], b.xl_all[:, bass.ds(c * CH, CH)]
        pe.matmul(bank[:, m, :], wh, xh, start=True, stop=False)
        pe.matmul(bank[:, m, :], wl, xh, start=False, stop=False)
        pe.matmul(bank[:, m, :], wh, xl, start=False, stop=True).then_inc(s["z_full"], 1)

    def second(e, c, m, half):
        if m == 0:
            pe.wait_ge(s["y_copied"], 8 * e + c + 1)
        pe.wait_ge(s["h_split"], 32 * e + 4 * c + m + 1 + HB)
        wh, wl = b.w2h[:, half, P * m:P * m + P], b.w2l[:, half, P * m:P * m + P]
        pe.matmul(bank[:, MOE_Y, :], wh, b.h_hi[:, m, :], start=m == 0, stop=False)
        pe.matmul(bank[:, MOE_Y, :], wl, b.h_hi[:, m, :], start=False, stop=False)
        mm = pe.matmul(bank[:, MOE_Y, :], wh, b.h_lo[:, m, :], start=False, stop=m == HB - 1)
        mm.then_inc(s["h_used"], 1)

    def turn_y(e, c):
        pe.wait_ge(s["y_copied"], 8 * e + c + 2)
        pe.wait_ge(s["x_added"], 8 * e + c + 1)
        for j in range(CT):
            mm = pe.transpose(bank[:, MOE_YT, P * j:P * j + P], b.y[:, P * j:P * j + P], b.ident[:, :])
        mm.then_inc(s["yt_full"], 1)

    pe.wait_ge(s["x_split"], NCH + 1)
    with pe.Fori(0, NE // 2) as pair:
        for half in range(2):
            e = 2 * pair + half
            pe.wait_ge(s["weights_split"], 2 * e + 4)
            for m in range(HB):
                first(e, 0, m, half)
            for m in range(HB):
                first(e, 1, m, half)
                second(e, 0, m, half)
            with pe.Fori(1, NCH - 1) as c:
                for m in range(HB):
                    first(e, c + 1, m, half)
                    second(e, c, m, half)
                    if m == 0:
                        turn_y(e, c - 1)
            for m in range(HB):
                second(e, NCH - 1, m, half)
                if m == 0:
                    turn_y(e, NCH - 2)
            turn_y(e, NCH - 1)
        

def moe_scalar(act, nc, b, s):
    bank = b.banks
    stats_scalar(act, nc, b, s)
    act.sem_inc(s["z_gelu"], HB)
    act.sem_inc(s["y_copied"], 1)
    with act.Fori(0, NCH) as c:
        act.wait_ge(s["xt_full"], c + 1)
        act.wait_ge(s["lg_full"], c + 1)
        nc.scalar.copy(b.xT[:, :], bank[:, MOE_XT, :]).then_inc(s["xt_ready"], 1)
        nc.scalar.copy(b.xh_all[:, bass.ds(c * CH, CH)], bank[:, MOE_XT, :]).then_inc(s["x_hi"], 1)
        act.wait_ge(s["rt_diff"], c + 1)
        nc.scalar.activation(b.rt[:, 1, :], b.rt[:, 0, :], ACT.Exp).then_inc(s["rt_exp"], 1)

    def gelu(e, c, m):
        z = 32 * e + 4 * c + m
        act.wait_ge(s["z_full"], z + 1)
        act.wait_ge(s["h_split"], z + 1)
        act.sem_inc(s["passed"], 1)
        nc.scalar.activation(b.h_raw[:, m, :], bank[:, m, :], ACT.Gelu,
                             bias=b.b1[:, bass.ds(4 * e + m, 1)]).then_inc(s["z_gelu"], 1)

    def y_copy(e, c):
        act.wait_ge(s["h_used"], 32 * e + 4 * c + 4 + HB)
        act.wait_ge(s["yt_full"], 8 * e + c + 1)
        act.sem_inc(s["passed"], 1)
        nc.scalar.activation(b.y[:, :], bank[:, MOE_Y, :], ACT.Identity,
                             bias=b.b2[:, bass.ds(e, 1)]).then_inc(s["y_copied"], 1)

    with act.Fori(0, NE) as e:
        for m in range(HB):
            gelu(e, 0, m)
        with act.Fori(0, NCH - 1) as c:
            for m in range(HB):
                gelu(e, c + 1, m)
            y_copy(e, c)
        y_copy(e, NCH - 1)


def moe_vector(v, nc, b, s, layer):
    bank = b.banks
    stats_vector(v, nc, b, s, layer)
    v.sem_inc(s["h_split"], HB)
    for name in ("x_split", "lg_ready", "x_added"):
        v.sem_inc(s[name], 1)
    for j in range(CT):
        ins = normalise(nc, b, b.xn[:, j, :], bass.ds(j, 1))
    ins.then_inc(s["xn_ready"], 1)
    steps = s["rt"]
    diff, ex, w1, w2 = (b.rt[:, k, :] for k in range(4))

    def route(c):
        v.wait_ge(s["x_hi"], c + 1)
        nc.vector.tensor_tensor(b.xl_all[:, bass.ds(c * CH, CH)], bank[:, MOE_XT, :],
                                b.xh_all[:, bass.ds(c * CH, CH)].bitcast(F32), ALU.subtract).then_inc(s["x_split"], 1)
        v.wait_ge(s["lg_full"], c + 2)
        nc.vector.tensor_copy(b.lg[:, :, :], bank[:, MOE_LG, 0:CT * NE].rearrange("p (j e) -> p j e", e=NE)).then_inc(s["lg_ready"], 1)
        v.wait_ge(s["lg_ready"], c + 2)
        v.sem_inc(s["passed"], 1)
        for j in range(CT):
            nc.vector.max(b.top[:, j, :], b.lg[:, j, :]).then_inc(s["rt_top"], 1)
        v.wait_ge(s["rt_top"], CT * c + CT)
        nc.vector.tensor_tensor(diff, b.top[:, :, 1], b.top[:, :, 0], ALU.subtract).then_inc(s["rt_diff"], 1)
        for j in range(CT):
            nc.vector.max_index(b.idx[:, j, :], b.top[:, j, :], b.lg[:, j, :]).then_inc(s["rt_idx"], 1)
        v.wait_ge(s["rt_idx"], CT * c + CT)
        nc.vector.tensor_copy(b.idxf[:, :, :], b.idx[:, :, 0:2]).then_inc(steps, 1)
        v.wait_ge(s["rt_exp"], c + 1)
        nc.vector.tensor_scalar(w1, ex, 1.0, None, ALU.add).then_inc(steps, 1)
        v.wait_ge(steps, RT_STEPS * c + 2)
        nc.vector.reciprocal(w1, w1).then_inc(steps, 1)
        iota = b.iota8[:, None, :].to_broadcast([P, CT, NE])
        for k in range(2):
            nc.vector.tensor_tensor(b.oh[:, k, :, :], iota, b.idxf[:, :, k:k + 1].to_broadcast([P, CT, NE]),
                                    ALU.is_equal).then_inc(steps, 1)
        v.wait_ge(steps, RT_STEPS * c + 3)
        nc.vector.tensor_scalar(w1, w1, 0.5, None, ALU.mult).then_inc(steps, 1)
        v.wait_ge(steps, RT_STEPS * c + 6)
        nc.vector.tensor_tensor(w2, w1, ex, ALU.mult).then_inc(steps, 1)
        nc.vector.tensor_tensor(b.oh[:, 0, :, :], b.oh[:, 0, :, :], w1[:, :, None].to_broadcast([P, CT, NE]),
                                ALU.mult).then_inc(steps, 1)
        v.wait_ge(steps, RT_STEPS * c + 8)
        nc.vector.tensor_tensor(b.oh[:, 1, :, :], b.oh[:, 1, :, :], w2[:, :, None].to_broadcast([P, CT, NE]),
                                ALU.mult).then_inc(s["rt_w2"], 1)
        v.wait_ge(s["rt_w2"], c + 1)
        nc.vector.tensor_tensor(b.wf[:, bass.ds(c * CT, CT), :], b.oh[:, 0, :, :], b.oh[:, 1, :, :],
                                ALU.add).then_inc(s["w_ready"], 1)

    with v.Fori(0, NCH - 1) as c:
        v.wait_ge(s["xt_full"], c + 1)
        for j in range(CT):
            ins = normalise(nc, b, b.xn[:, j, :], bass.ds((c + 1) * CT + j, 1))
        ins.then_inc(s["xn_ready"], 1)
        route(c)
    route(NCH - 1)
    v.wait_ge(s["w_ready"], NCH)

    def lo(e, c, m):
        z = 32 * e + 4 * c + m
        v.wait_ge(s["h_hi"], z + 1)
        nc.vector.tensor_tensor(b.h_lo[:, m, :], b.h_raw[:, m, :], b.h_hi[:, m, :].bitcast(F32),
                                ALU.subtract).then_inc(s["h_split"], 1)

    def add(e, c):
        v.wait_ge(s["yt_full"], 8 * e + c + 2)
        v.wait_ge(s["x_added"], 8 * e + c + 1)
        for j in range(CT):
            xs = b.x[:, bass.ds(c * CT + j, 1), :]
            ins = nc.vector.scalar_tensor_tensor(xs, bank[:, MOE_YT:MOE_YT + 1, P * j:P * j + P],
                                                 b.wfe[:, bass.ds(c * CT * NE + j * NE + e, 1)], xs,
                                                 ALU.mult, ALU.add)
        ins.then_inc(s["x_added"], 1)

    with v.Fori(0, NE) as e:
        for m in range(HB):
            lo(e, 0, m)
        for m in range(HB):
            lo(e, 1, m)
        with v.Fori(1, NCH - 1) as c:
            lo(e, c + 1, 0)
            add(e, c - 1)
            for m in range(1, HB):
                lo(e, c + 1, m)
        add(e, NCH - 2)
        add(e, NCH - 1)
    v.wait_ge(s["x_added"], NE * NCH + 1)
    with v.Fori(0, TILES) as t:
        nc.vector.bn_stats(b.bn[:, bass.ds(t, 1), :], b.x[:, bass.ds(t, 1), :]).then_inc(b.bn_done, 1)


ATT_SEMS = STATS_SEMS + ["xn_ready", "sel_ready", "s_full", "s_hi", "s_free", "st_full", "st_free", "masked",
                         "shift_hi", "shift_cols", "pv_done", "own_inv", "own_norm",
                         "rec_inv", "rec_scaled", "rec_norm", "mix", "x_added"]
S_BANK, ST_BANK, OWN_BANK, REC_BANK = 0, 2, 6, 7
QK = 96
S_SLOTS, ST_SLOTS, P_SLOTS = 2, 2, 4


def step_order(own, rec, prep):
    def maxima(g):
        if rec:
            for h in range(4):
                for t in range(BT):
                    yield "max", "rec", g, h, t
        if own:
            for h in range(2):
                for t in range(BT):
                    yield "max", "own", g, h, t

    def units(g):
        if own:
            for u in range(2):
                yield "unit", "own", g, u, 0
        if rec:
            for u in range(4):
                yield "unit", "rec", g, u, 0

    waiting = []
    yield from maxima(0)
    for g in range(NG):
        for kind in (["own"] if own else []) + (["rec"] if rec else []):
            yield "turn", kind, g, 0, 0
        nxt = list(maxima(g + 1)) if g + 1 < NG else []
        us = list(units(g))
        for n, u in enumerate(us):
            yield u
            yield from nxt[n * len(nxt) // len(us):(n + 1) * len(nxt) // len(us)]
            waiting.append(u)
            if len(waiting) > 2:
                yield ("pv",) + waiting.pop(0)[1:]
    for u in waiting:
        yield ("pv",) + u[1:]
    if prep:
        yield "prep", "x", 0, 0, 0
    if own:
        yield "own", "ctx", 0, 0, 0
    if rec:
        yield "rec", "ctx", 0, 0, 0
    if prep:
        yield "prep", "v", 0, 0, 0
        for g in range(NG):
            yield "prep", "k", g, 0, 0
    if rec:
        yield "rec", "gate", 0, 0, 0
    if own:
        yield "own", "out", 0, 0, 0
    if prep:
        for g in range(NG):
            yield "prep", "q", g, 0, 0
    if own:
        for g in range(NG):
            yield "own", "rq", g, 0, 0


class Counts:
    def __init__(self):
        self.base = {}
        self.n = {}
        self.mark = {}

    def add(self, key, k=1):
        self.n[key] = self.n.get(key, 0) + k

    def at(self, key):
        return self.base.get(key, 0) + self.n.get(key, 0)

    def slot(self, key, slots):
        return self.n.get(key, 0) % slots


def count_event(k, what, kind):
    if what == "max":
        k.add("s")
    elif what == "turn":
        k.add("st")
        k.add("turn")
    elif what == "unit":
        k.add("st")
        k.add("unit")
    elif what == "pv":
        k.add("pv")
    elif kind in ("k", "q", "rq"):
        k.add("s")
        k.add("split")
        if kind == "k":
            k.add("masked")
    else:
        k.add("st")


def walk(k, own, rec, prep, body, be=0, br=0):
    k.own, k.rec = own, rec
    k.mark = {"s_start": k.at("s"), "st_start": k.at("st")}
    for what, kind, g, u, t in step_order(own, rec, prep):
        body(what, kind, g, u, t, be, br)
        count_event(k, what, kind)
    k.add("own", int(own))
    k.add("rec", int(rec))
    k.add("prep", int(prep))


def run_steps(eng, k, body):
    walk(k, True, False, True, body, 0, 0)
    per = Counts()
    walk(per, True, True, True, lambda *ev: None)
    before = dict(k.n)
    with eng.Fori(0, BATCH - 2) as i:
        k.base = {key: i * n for key, n in per.n.items()}
        walk(k, True, True, True, body, i + 1, i)
    k.base = {}
    k.n = {key: before.get(key, 0) + (BATCH - 2) * n for key, n in per.n.items()}
    walk(k, True, True, False, body, BATCH - 1, BATCH - 2)
    walk(k, False, True, False, body, BATCH, BATCH - 1)


def run_prologue(k, body):
    for g in range(NG):
        body("past", "k", g, 0, 0, 0, 0)
        count_event(k, "past", "k")
    body("past", "v", 0, 0, 0, 0, 0)
    count_event(k, "past", "v")
    for kind, groups in (("x", 1), ("v", 1), ("k", NG), ("q", NG)):
        for g in range(groups):
            body("prep", kind, g, 0, 0, 0, 0)
            count_event(k, "prep", kind)
    k.add("prep")


def att_tensor(pe, nc, b, s):
    bank = b.banks
    k = Counts()
    pe.sem_inc(s["pv_done"], P_SLOTS)
    pe.wait_ge(b.loaded["att"], 16 * b.n_loads["att"])
    pe.wait_ge(s["sel_ready"], 2)
    pending = []

    def turned_row(out, lhs_tiles, last_row):
        for n, (lhs, rhs) in enumerate(lhs_tiles):
            pe.matmul(out, lhs, rhs, start=n == 0, stop=False)
        return pe.matmul(out, b.ones[0:1, 0:P], last_row, start=False, stop=True)

    def body(what, kind, g, u, t, be, br):
        uses_s = what == "max" or kind in ("k", "q", "rq")
        uses_st = what in ("turn", "unit", "prep", "own", "rec", "past") and not uses_s
        if uses_s:
            pe.wait_ge(s["s_free"], k.at("s") + 1)
            out_s = bank[:, S_BANK + k.slot("s", S_SLOTS), :]
        if uses_st:
            pe.wait_ge(s["st_free"], k.at("st") + 1)
            st = ST_BANK + 2 * k.slot("st", ST_SLOTS)
        tiles = [slice(P * j, P * j + P) for j in range(BT)]

        if what == "max":
            if "started" not in k.mark:
                k.mark["started"] = True
                pe.wait_ge(s["s_free"], k.mark["s_start"] + S_SLOTS)
            if kind == "own":
                if u == 0 and t == 0:
                    pe.wait_ge(s["masked"], NG * k.at("prep") + g + 1)
                lhs, rhs = b.q_own[0:QK, g, tiles[t]], b.k_own[0:QK, 4 * g + 2 * u:4 * g + 2 * u + 2, :]
            else:
                lhs, rhs = b.q_rec[0:QK, g, tiles[t]], b.k_rec[0:QK, 4 * g + u, :]
            pe.matmul(out_s, lhs, rhs, start=True, stop=True).then_inc(s["s_full"], 1)
        elif what == "turn":
            pe.wait_ge(s["shift_cols"], k.at("turn") + 1)
            cols = b.m_own if kind == "own" else b.m_rec
            for j in range(BT):
                mm = pe.transpose(bank[:, st, tiles[j]], cols[:, j, 32 * g:32 * g + P].bitcast(F32), b.ident[:, :])
            mm.then_inc(s["st_full"], 1)
            k.mark["turn_" + kind] = k.at("st")
        elif what == "unit":
            if u == 0:
                pe.wait_ge(s["st_free"], k.mark["turn_" + kind] + 1 + ST_SLOTS)
            for n in range(4):
                if kind == "own":
                    lhs, rhs = b.k_own[:, 4 * g + 2 * u + n // 2, tiles[n % 2]], b.q_own[:, g, :]
                else:
                    lhs, rhs = b.k_rec[:, 4 * g + u, P * n:P * n + P], b.q_rec[:, g, :]
                mm = pe.matmul(bank[:, st + n // 2, SEQ * (n % 2):SEQ * (n % 2) + SEQ], lhs, rhs,
                               start=True, stop=True)
            mm.then_inc(s["st_full"], 1)
            pending.append(k.at("st"))
        elif what == "pv":
            slot = k.slot("pv", P_SLOTS)
            pe.wait_ge(s["st_free"], pending.pop(0) + 1 + ST_SLOTS)
            if kind == "own" and g == 0 and u == 0:
                pe.wait_ge(s["st_free"], k.mark["st_start"] + ST_SLOTS)
                pe.wait_ge(s["own_norm"], k.at("own"))
            if kind == "rec" and g % 2 == 0 and u == 0:
                pe.wait_ge(s["rec_norm"], 2 * k.at("rec") + g // 2 + 1)
            for x in range(2):
                for j in range(BT):
                    if kind == "own":
                        h = 4 * g + 2 * u + x
                        at = NH * j + h
                        out = bank[:, OWN_BANK, at * VW:(at + 1) * VW]
                    else:
                        h = 4 * g + u
                        at = (8 * j + h % 8) * PAST + x
                        out = bank[:, REC_BANK, at * VW:(at + 1) * VW]
                    for tc in range(BT):
                        val = b.v_own[:, tc, h, :] if kind == "own" else b.v_rec[:, BT * x + tc, h, :]
                        at = (BT * x + tc) * SEQ + P * j
                        mm = pe.matmul(out, b.p[:, slot, at:at + P], val, start=tc == 0, stop=tc == BT - 1)
            mm.then_inc(s["pv_done"], 1)
        elif what == "past" and kind == "k":
            pe.matmul(out_s[0:QK, :], b.wrk[:, g, :], b.pastT[:, :], start=True, stop=True).then_inc(s["s_full"], 1)
        elif what == "past":
            for n in range(PAST * BT):
                mm = turned_row(bank[:, st, P * n:P * n + P], [(b.pastT[:, P * n:P * n + P], b.wrv[:, :])],
                                b.brv[0:1, :])
            mm.then_inc(s["st_full"], 1)
        elif kind in ("k", "q", "rq"):
            if kind == "rq":
                pe.wait_ge(s["st_free"], k.mark["out"] + 1 + ST_SLOTS)
            elif kind == "k":
                pe.wait_ge(s["st_free"], k.mark["xT"] + 1 + ST_SLOTS)
            w = {"k": b.wk, "q": b.wq, "rq": b.wrq}[kind]
            rhs = b.outT[:, :] if kind == "rq" else b.xT[:, 0:SEQ]
            pe.matmul(out_s[0:QK, 0:SEQ], w[:, g, :], rhs, start=True, stop=True).then_inc(s["s_full"], 1)
        elif what == "prep" and kind == "x":
            pe.wait_ge(s["xn_ready"], k.at("prep") + 1)
            for j in range(BT):
                mm = pe.transpose(bank[:, st, tiles[j]], b.xn[:, j, :], b.ident[:, :])
            mm.then_inc(s["st_full"], 1)
            k.mark["xT"] = k.at("st")
        elif what == "prep" and kind == "v":
            pe.wait_ge(s["st_free"], k.mark["xT"] + 1 + ST_SLOTS)
            for j in range(BT):
                mm = turned_row(bank[:, st, tiles[j]], [(b.xT[:, tiles[j]], b.wv[:, :])], b.bv[0:1, :])
            mm.then_inc(s["st_full"], 1)
        elif what == "own" and kind == "ctx":
            pe.wait_ge(s["own_norm"], k.at("own") + 1)
            for j in range(BT):
                mm = pe.transpose(bank[:, st, tiles[j]], b.ctx[:, j, :], b.ident[:, :])
            mm.then_inc(s["st_full"], 1)
            k.mark["ctx"] = k.at("st")
        elif what == "own" and kind == "out":
            pe.wait_ge(s["st_free"], k.mark["ctx"] + 1 + ST_SLOTS)
            pe.matmul(bank[:, st, 0:SEQ], b.wo[:, :], b.ctxT[:, :], start=True, stop=True)
            for j in range(BT):
                mm = turned_row(bank[:, st + 1, tiles[j]], [(b.ctxT[:, tiles[j]], b.wo[:, :])], b.bo_row[0:1, :])
            mm.then_inc(s["st_full"], 1)
            k.mark["out"] = k.at("st")
        elif what == "rec" and kind == "ctx":
            pe.wait_ge(s["rec_norm"], 2 * k.at("rec") + 3)
            for j in range(BT):
                mm = pe.transpose(bank[:, st, tiles[j]], b.rctx[:, j, :], b.ident[:, :])
            mm.then_inc(s["st_full"], 1)
            k.mark["rctx"] = k.at("st")
        elif what == "rec" and kind == "gate":
            pe.wait_ge(s["st_free"], k.mark["rctx"] + 1 + ST_SLOTS)
            for j in range(BT):
                mm = turned_row(bank[:, st, tiles[j]],
                                [(b.outT[:, tiles[j]], b.wg[:, 0, :]), (b.rcT[:, tiles[j]], b.wg[:, 1, :])],
                                b.bg[0:1, :])
            mm.then_inc(s["st_full"], 1)

    run_prologue(k, body)
    run_steps(pe, k, body)


def att_scalar(act, nc, b, s):
    bank = b.banks
    stats_scalar(act, nc, b, s)
    act.sem_inc(s["st_free"], ST_SLOTS)
    k = Counts()

    def body(what, kind, g, u, t, be, br):
        if what in ("max", "pv"):
            return
        if kind in ("k", "q", "rq"):
            act.wait_ge(s["s_full"], k.at("s") + 1)
            width = PAST * SEQ if what == "past" else SEQ
            if what == "prep" and kind == "k":
                act.wait_ge(s["masked"], k.at("masked") - NG + 1)
            dst = {"k": b.k_parts, "q": b.q_own, "rq": b.q_rec}[kind]
            bias = b.brk if what == "past" else {"k": b.bk, "q": b.bq, "rq": b.brq}[kind]
            nc.scalar.activation(dst[0:QK, g, 0:width], bank[0:QK, S_BANK + k.slot("s", S_SLOTS), 0:width],
                                 ACT.Identity, bias=bias[0:QK, g:g + 1]).then_inc(s["s_hi"], 1)
            return
        st = ST_BANK + 2 * k.slot("st", ST_SLOTS)
        act.wait_ge(s["st_full"], k.at("st") + 1)
        if what == "turn":
            q = b.q_own if kind == "own" else b.q_rec
            nc.scalar.copy(q[QK:P, g, :], bank[QK:P, st, 0:SEQ]).then_inc(s["st_free"], 1)
        elif what == "unit":
            act.wait_ge(s["pv_done"], k.at("unit") + 1)
            nc.scalar.activation(b.p[:, k.slot("unit", P_SLOTS), :].rearrange("p (a n) -> p a n", a=2),
                                 bank[:, st:st + 2, :], ACT.Exp, scale=SCALE).then_inc(s["st_free"], 1)
        elif what == "past":
            nc.scalar.copy(b.v_rec[:, :, :, 0:D],
                           bank[:, st, :].rearrange("p (n h d) -> p n h d", h=NH, d=D)).then_inc(s["st_free"], 1)
        elif kind == "v":
            nc.scalar.copy(b.v_own[:, :, :, 0:D],
                           bank[:, st, 0:SEQ].rearrange("p (n h d) -> p n h d", h=NH, d=D)).then_inc(s["st_free"], 1)
        elif kind == "x":
            nc.scalar.copy(b.xT[:, 0:SEQ], bank[:, st, 0:SEQ]).then_inc(s["st_free"], 1)
        elif what == "own" and kind == "ctx":
            nc.scalar.copy(b.ctxT[:, :], bank[:, st, 0:SEQ]).then_inc(s["st_free"], 1)
        elif what == "rec" and kind == "ctx":
            nc.scalar.copy(b.rcT[:, :], bank[:, st, 0:SEQ]).then_inc(s["st_free"], 1)
        elif what == "rec" and kind == "gate":
            nc.scalar.activation(b.th[:, :], bank[:, st, 0:SEQ], ACT.Tanh, scale=0.5).then_inc(s["st_free"], 1)
        elif what == "own" and kind == "out":
            if k.rec:
                act.wait_ge(s["mix"], 3 * k.at("rec") + 3)
            nc.scalar.activation(b.outT[:, :], bank[:, st, 0:SEQ], ACT.Identity, bias=b.bo_col[:, 0:1])
            nc.scalar.copy(b.out_tm[:, :], bank[:, st + 1, 0:SEQ]).then_inc(s["st_free"], 1)

    run_prologue(k, body)
    run_steps(act, k, body)


def att_gpsimd(pool, nc, b, s):
    pool.wait_ge(b.loaded["att"], 16 * b.n_loads["att"])
    pool.wait_ge(s["var"], 1)
    nc.gpsimd.tensor_copy(b.k_own[QK:P, :, :], b.sel[QK:P, 0:NH, None].to_broadcast([32, NH, SEQ])).then_inc(s["sel_ready"], 1)
    nc.gpsimd.tensor_copy(b.k_rec[QK:P, :, :].rearrange("p h (a n) -> p (h a) n", a=PAST),
                          b.sel[QK:P, NH:NH + NH * PAST, None].to_broadcast([32, NH * PAST, SEQ])).then_inc(s["sel_ready"], 1)
    k = Counts()

    def body(what, kind, g, u, t, be, br):
        if kind != "k":
            return
        pool.wait_ge(s["s_free"], k.at("s") + 1 + S_SLOTS)
        pool.sem_inc(s["passed"], 1)
        for h in range(4):
            out = b.k_rec[0:QK, 4 * g + h, :] if what == "past" else b.k_own[0:QK, 4 * g + h, :]
            width = PAST * SEQ if what == "past" else SEQ
            ins = nc.gpsimd.tensor_scalar(out, b.k_parts[0:QK, g, 0:width].bitcast(F32), b.headmask[0:QK, h:h + 1],
                                          1.0, ALU.mult, ALU.mult)
        ins.then_inc(s["masked"], 1)

    run_prologue(k, body)
    run_steps(pool, k, body)


def att_vector(v, nc, b, s, layer):
    bank = b.banks
    stats_vector(v, nc, b, s, layer)
    v.sem_inc(s["s_free"], S_SLOTS)
    v.sem_inc(s["rec_norm"], 1)
    v.wait_ge(b.loaded["att"], 16 * b.n_loads["att"])
    k = Counts()

    def xn(entry):
        for j in range(BT):
            ins = normalise(nc, b, b.xn[:, j, :], bass.ds(entry * BT + j, 1))
        ins.then_inc(s["xn_ready"], 1)

    xn(0)

    def body(what, kind, g, u, t, be, br):
        src = bank[:, S_BANK + k.slot("s", S_SLOTS), :]
        if what == "max":
            v.wait_ge(s["s_full"], k.at("s") + 1)
            out = b.mx_own if kind == "own" else b.mx_rec
            nc.vector.reduce_max(out[:, t, 2 * u:2 * u + 2], src.rearrange("p (a n) -> p a n", a=2),
                                 AX.X).then_inc(s["s_free"], 1)
        elif what == "turn":
            v.wait_ge(s["s_free"], k.at("s") + S_SLOTS)
            mx, cols = (b.mx_own, b.m_own) if kind == "own" else (b.mx_rec, b.m_rec)
            at, step = QK + 32 * g, 4 if kind == "own" else 2
            hi, lo = cols[:, :, at:at + 16:step], cols[:, :, at + 1:at + 16:step]
            nc.vector.tensor_copy(hi, mx[:, :, :]).then_inc(s["shift_hi"], 1)
            v.wait_ge(s["shift_hi"], k.at("turn") + 1)
            nc.vector.tensor_tensor(lo, mx[:, :, :], hi.bitcast(F32), ALU.subtract).then_inc(s["shift_cols"], 1)
            if g == 2 and kind == "own" and not (isinstance(be, int) and be == BATCH - 1):
                xn(be + 1)
        elif kind in ("k", "q", "rq"):
            v.wait_ge(s["s_hi"], k.at("split") + 1)
            width = PAST * SEQ if what == "past" else SEQ
            dst = {"k": b.k_parts, "q": b.q_own, "rq": b.q_rec}[kind]
            bias = b.brk if what == "past" else {"k": b.bk, "q": b.bq, "rq": b.brq}[kind]
            rows = slice(32, 64) if kind == "k" else slice(64, 96)
            part = dst[rows, g, 0:width]
            nc.vector.scalar_tensor_tensor(part, src[rows, 0:width], bias[rows, g:g + 1], part.bitcast(F32),
                                           ALU.add, ALU.subtract).then_inc(s["s_free"], 1)
        elif what == "pv" and kind == "own" and g == NG - 1 and u == 1:
            v.wait_ge(s["pv_done"], k.at("pv") + 1 + P_SLOTS)
            acc = bank[:, OWN_BANK, 0:BT * NH * VW].rearrange("p (n w) -> p n w", w=VW)
            nc.vector.reciprocal(b.own_inv[:, :, None], acc[:, :, D:VW]).then_inc(s["own_inv"], 1)
            v.wait_ge(s["own_inv"], k.at("own") + 1)
            nc.vector.tensor_tensor(b.ctx[:, :, :].rearrange("p j (h d) -> p (j h) d", d=D), acc[:, :, 0:D],
                                    b.own_inv[:, :, None].to_broadcast([P, BT * NH, D]),
                                    ALU.mult).then_inc(s["own_norm"], 1)
        elif what == "pv" and kind == "rec" and g % 2 == 1 and u == 3:
            half = g // 2
            v.wait_ge(s["pv_done"], k.at("pv") + 1 + P_SLOTS)
            acc = bank[:, REC_BANK, 0:BT * 8 * PAST * VW].rearrange("p (n w) -> p n w", w=VW)
            nc.vector.reciprocal(b.rec_inv[:, :, None], acc[:, :, D:VW]).then_inc(s["rec_inv"], 1)
            v.wait_ge(s["rec_inv"], 2 * k.at("rec") + half + 1)
            nc.vector.scalar_tensor_tensor(b.rec_tmp[:, :, :], acc[:, :, 0:D], 1.0 / PAST,
                                           b.rec_inv[:, :, None].to_broadcast([P, BT * 8 * PAST, D]),
                                           ALU.mult, ALU.mult).then_inc(s["rec_scaled"], 1)
            v.wait_ge(s["rec_scaled"], 2 * k.at("rec") + half + 1)
            tmp = b.rec_tmp[:, :, :].rearrange("p (j h a) d -> p j h a d", j=BT, a=PAST)
            for j in range(BT):
                ins = nc.vector.tensor_tensor(b.rctx[:, j, 64 * half:64 * half + 64].rearrange("p (h d) -> p h d", d=D),
                                              tmp[:, j, :, 0, :], tmp[:, j, :, 1, :], ALU.add)
            ins.then_inc(s["rec_norm"], 1)
        elif what == "rec" and kind == "gate":
            rctx = b.rctx[:, :, :].rearrange("p j f -> p (j f)")
            v.wait_ge(s["rec_norm"], 2 * k.at("rec") + 3)
            nc.vector.tensor_tensor(b.mixd[:, :], rctx, b.out_tm[:, :], ALU.subtract).then_inc(s["mix"], 1)
            v.wait_ge(s["mix"], 3 * k.at("rec") + 1)
            v.wait_ge(s["st_free"], k.at("st") + 1 + ST_SLOTS)
            nc.vector.scalar_tensor_tensor(b.mixd[:, :], b.th[:, :], 1.0, b.mixd[:, :],
                                           ALU.add, ALU.mult).then_inc(s["mix"], 1)
            v.wait_ge(s["mix"], 3 * k.at("rec") + 2)
            nc.vector.scalar_tensor_tensor(b.mixd[:, :], b.mixd[:, :], 0.5, b.out_tm[:, :],
                                           ALU.mult, ALU.add).then_inc(s["mix"], 1)
            v.wait_ge(s["mix"], 3 * k.at("rec") + 3)
            xs = b.xb[:, bass.ds(br, 1), :]
            nc.vector.tensor_tensor(xs, xs, b.mixd[:, None, :], ALU.add).then_inc(s["x_added"], 1)
            v.wait_ge(s["x_added"], k.at("rec") + 1)
            for j in range(BT):
                nc.vector.bn_stats(b.bn[:, bass.ds(br * BT + j, 1), :],
                                   b.x[:, bass.ds(br * BT + j, 1), :]).then_inc(b.bn_done, 1)

    run_prologue(k, body)
    run_steps(v, k, body)


def macaron(nc, a, out):
    with ExitStack() as ctx:
        def sb(name, shape, dt=F32):
            return ctx.enter_context(nc.sbuf_tensor(name, shape, dt))

        def sems(prefix, names):
            return {n: ctx.enter_context(nc.semaphore(f"{prefix}_{n}")) for n in names}

        b = Buffers()
        b.banks = ctx.enter_context(nc.psum_tensor("banks", [P, 8, 512], F32))
        x = sb("x", [P, T])
        b.x = x[:, :].rearrange("p (t f) -> p t f", f=C)
        b.xc = x[:, :].rearrange("p (c n) -> p c n", n=CH)
        b.xb = x[:, :].rearrange("p (c n) -> p c n", n=SEQ)
        b.xn = sb("xn", [P, CT, C])
        b.xT = sb("xT", [P, CH])
        b.bn = sb("bn", [P, TILES, 6])
        b.ln = sb("ln", [P, 6, TILES])
        b.ident = sb("ident", [P, P])
        b.ones = sb("ones", [1, P])
        parts = sb("parts", [P, 4 * HB * CH], F32R)
        quarter = [parts[:, HB * CH * n:HB * CH * (n + 1)].rearrange("p (k n) -> p k n", n=CH) for n in range(4)]
        b.h_hi, b.h_lo, b.g_hi, b.g_lo = quarter
        b.k_own = parts[:, 0:NH * SEQ].rearrange("p (h n) -> p h n", n=SEQ)
        wide = sb("wide", [P, 2 * T], F32R)
        b.xh_all, b.xl_all = wide[:, 0:T], wide[:, T:2 * T]
        b.k_rec = wide[:, 0:NH * PAST * SEQ].rearrange("p (h n) -> p h n", n=PAST * SEQ)
        raw = sb("raw", [P, HB * CH])
        b.h_raw = raw[:, :].rearrange("p (k n) -> p k n", n=CH)
        b.y = sb("y", [P, CH])
        b.xh = sb("xh", [P, CH], F32R)
        b.xl = sb("xl", [P, CH], F32R)
        b.k0u = sb("k0u", [P, 2, 512], U8)
        b.k1u = sb("k1u", [P, HB, 512], U8)
        b.k2u = sb("k2u", [P, HB, C], U8)
        b.k0f = b.y
        b.k0 = sb("k0", [P, 512], F32R)
        b.k1 = sb("k1", [P, HB, 512], F32R)
        b.k2 = sb("k2", [P, HB, C], F32R)
        b.sc = sb("sc", [P, 16])
        b.ffn_scale = b.sc[:, 15:16]
        b.wq0 = sb("wq0", [P, C])
        b.wkv0 = sb("wkv0", [P, 2 * C])
        b.wp0 = sb("wp0", [P, C])
        b.pb0 = sb("pb0", [1, C])
        b.blockmask = sb("blockmask", [P, 2 * C])
        work = sb("work", [P, P_SLOTS * 4 * SEQ])
        b.kv = work[:, 0:3 * CH].rearrange("p (t n) -> p t n", t=CT)
        b.kvm = work[:, 3 * CH:4 * CH].rearrange("p (e n) -> p e n", e=2)
        b.rec, b.ratio, b.qT = (work[:, n * CH:(n + 1) * CH] for n in (4, 5, 6))
        b.wr = sb("wr", [P, NE])
        b.br = sb("br", [1, NE])
        b.b1 = sb("b1", [P, NE * HB])
        b.b2 = sb("b2", [P, NE])
        b.iota8 = sb("iota8", [P, NE])
        b.w1_raw = sb("w1_raw", [P, 512])
        b.w2_raw = sb("w2_raw", [P, HB, C])
        b.w1h, b.w1l, b.w2h, b.w2l = (sb(n, [P, 2, 512], F32R) for n in ("w1h", "w1l", "w2h", "w2l"))
        b.lg = sb("lg", [P, CT, NE])
        b.top = sb("top", [P, CT, 8])
        b.idx = sb("idx", [P, CT, 8], U32)
        b.idxf = sb("idxf", [P, CT, 2])
        b.rt = sb("rt", [P, 4, CT])
        b.oh = sb("oh", [P, 2, CT, NE])
        b.wfe = sb("wfe", [P, TILES * NE])
        b.wf = b.wfe[:, :].rearrange("p (t e) -> p t e", e=NE)
        b.wq, b.wk, b.wrq, b.wrk = (sb(n, [P, NG, QK]) for n in ("wq", "wk", "wrq", "wrk"))
        b.bq, b.bk, b.brq, b.brk = (sb(n, [QK, NG]) for n in ("bq", "bk", "brq", "brk"))
        b.wv, b.wrv, b.wo = (sb(n, [P, C]) for n in ("wv", "wrv", "wo"))
        b.wg = sb("wg", [P, 2, C])
        b.bv, b.brv, b.bo_row, b.bg = (sb(n, [1, C]) for n in ("bv", "brv", "bo_row", "bg"))
        b.bo_col = sb("bo_col", [P, 1])
        b.pastT = sb("pastT", [P, PAST * SEQ])
        b.headmask = sb("headmask", [QK, 4])
        b.sel = sb("sel", [P, NH + NH * PAST])
        b.q_own, b.q_rec = (sb(n, [P, NG, SEQ], F32R) for n in ("q_own", "q_rec"))
        b.k_parts = sb("k_parts", [QK, NG, PAST * SEQ], F32R)
        b.m_own, b.m_rec = (sb(n, [P, BT, QK + P], F32R) for n in ("m_own", "m_rec"))
        b.mx_own = sb("mx_own", [P, BT, 4])
        b.mx_rec = sb("mx_rec", [P, BT, 8])
        b.p = work[:, :].rearrange("p (k n) -> p k n", k=P_SLOTS)
        b.v_own = sb("v_own", [P, BT, NH, VW])
        b.v_rec = sb("v_rec", [P, PAST * BT, NH, VW])
        b.own_inv, b.rec_inv = sb("own_inv", [P, BT * NH]), sb("rec_inv", [P, BT * 8 * PAST])
        b.rec_tmp = sb("rec_tmp", [P, BT * 8 * PAST, D])
        b.ctx, b.rctx = sb("ctx", [P, BT, C]), sb("rctx", [P, BT, C])
        b.ctxT, b.rcT, b.outT, b.out_tm, b.th, b.mixd = (sb(n, [P, SEQ]) for n in
                                                         ("ctxT", "rcT", "outT", "out_tm", "th", "mixd"))

        loads = {
            "ffn": [(b.k0u[:, :, :], a["L0_ffn_k0"].rearrange("(h p) n -> p h n", p=P)),
                    (b.k1u[:, :, :], a["L0_ffn_k1"].rearrange("(k p) n -> p k n", p=P)),
                    (b.k2u[:, :, :], a["L0_ffn_k2"].rearrange("(k p) n -> p k n", p=P)),
                    (b.sc[:, 0:3], a["s_cols"]), (b.ident[:, :], a["ident"])],
            "lin": [(b.wq0[:, :], a["wqkv0_t"][:, 0:C]), (b.wkv0[:, :], a["wqkv0_t"][:, C:3 * C]),
                    (b.wp0[:, :], a["wproj0_t"]), (b.pb0[:, :], a["L0_attn_proj_bias"].rearrange("(o f) -> o f", o=1)),
                    (b.blockmask[:, :], a["blockmask"])],
            "moe": [(b.wr[:, :], a["L1_ffn_Wr"]), (b.br[:, :], a["L1_ffn_br"].rearrange("(o f) -> o f", o=1)),
                    (b.b1[:, :], a["b1_t"]), (b.b2[:, :], a["b2_t"]), (b.iota8[:, :], a["iota8"])],
            "att": [(b.wq[:, :, :], a["wq_rep"]), (b.wk[:, :, :], a["wk_rep"]), (b.wrq[:, :, :], a["wrq_rep"]),
                    (b.wrk[:, :, :], a["wrk_rep"]), (b.bq[:, :], a["bq_rep"]), (b.bk[:, :], a["bk_rep"]),
                    (b.brq[:, :], a["brq_rep"]), (b.brk[:, :], a["brk_rep"]),
                    (b.wv[:, :], a["L1_attn_Wv"]), (b.wrv[:, :], a["L1_attn_Wrv"]), (b.wo[:, :], a["L1_attn_Wo"]),
                    (b.wg[:, :, :], a["L1_attn_Wg"].rearrange("(h p) n -> p h n", p=P)),
                    (b.bo_col[:, :], a["L1_attn_bo"].rearrange("(p o) -> p o", o=1)),
                    (b.pastT[:, :], a["past_t"]), (b.headmask[:, :], a["headmask"]),
                    (b.sel[QK:P, :], a["sel"])]
                   + [(dst[:, :], a[n].rearrange("(o f) -> o f", o=1)) for dst, n in
                      ((b.bv, "L1_attn_bv"), (b.brv, "L1_attn_brv"), (b.bo_row, "L1_attn_bo"), (b.bg, "L1_attn_bg"))],
        }
        b.n_loads = {name: len(group) for name, group in loads.items()}
        b.loaded = sems("loaded", loads)
        b.W1, b.W2 = a["L1_ffn_W1"], a["L1_ffn_W2"]
        x_in = [ctx.enter_context(nc.semaphore(f"x_in{c}")) for c in range(NCH)]
        b.bn_done = ctx.enter_context(nc.semaphore("bn_done"))
        x_out = ctx.enter_context(nc.semaphore("x_out"))
        setup = sems("setup", ["signs", "abs", "diff", "weights", "fills"])
        layer_sems = [sems("ffn_a", FFN_SEMS), sems("lin", LIN_SEMS), sems("ffn_b", FFN_SEMS),
                      sems("moe_a", MOE_SEMS), sems("att", ATT_SEMS), sems("moe_b", MOE_SEMS)]
        ffn_a, lin, ffn_b, moe_a, att, moe_b = layer_sems
        block = ctx.enter_context(nc.Block())
        x_dram = a["L0_attn_x"].rearrange("e (j p) f -> p (e j) f", p=P)
        out_dram = out.rearrange("e (j p) f -> p (e j) f", p=P)

        @block.sync
        def _(sp):
            for c in range(NCH):
                sp.dma_start(b.x[:, CT * c:CT * c + CT, :], x_dram[:, CT * c:CT * c + CT, :]).then_inc(x_in[c], 16)
            for name in ("lin", "moe", "att"):
                for dst, src in loads[name]:
                    sp.dma_start(dst, src).then_inc(b.loaded[name], 16)
            moe_sync(sp, nc, b, moe_a)
            sp.wait_ge(moe_a["weights_split"], 2 * NE + 2)
            moe_sync(sp, nc, b, moe_b)
            sp.wait_ge(moe_b["x_added"], NE * NCH + 1)
            for c in range(NCH):
                sp.dma_start(out_dram[:, CT * c:CT * c + CT, :], b.x[:, CT * c:CT * c + CT, :]).then_inc(x_out, 16)
            sp.wait_ge(x_out, 16 * NCH)

        @block.scalar
        def _(act):
            for dst, src in loads["ffn"]:
                act.dma_start(dst, src).then_inc(b.loaded["ffn"], 16)
            ffn_scalar(act, nc, b, ffn_a)
            lin_scalar(act, nc, b, lin)
            ffn_scalar(act, nc, b, ffn_b)
            act.wait_ge(b.loaded["moe"], 16 * b.n_loads["moe"])
            moe_scalar(act, nc, b, moe_a)
            act.wait_ge(b.loaded["att"], 16 * b.n_loads["att"])
            att_scalar(act, nc, b, att)
            moe_scalar(act, nc, b, moe_b)

        @block.gpsimd
        def _(pool):
            nc.gpsimd.memset(b.ones[:, :], 1.0).then_inc(setup["fills"], 1)
            nc.gpsimd.memset(b.kv[:, :, 2 * C:3 * C], 1.0).then_inc(setup["fills"], 1)
            nc.gpsimd.memset(b.v_own[:, :, :, D:VW], 1.0).then_inc(setup["fills"], 1)
            nc.gpsimd.memset(b.v_rec[:, :, :, D:VW], 1.0).then_inc(setup["fills"], 1)
            nc.gpsimd.memset(b.m_own[:, :, :].bitcast(F32), 0.0).then_inc(setup["fills"], 1)
            nc.gpsimd.memset(b.m_rec[:, :, :].bitcast(F32), 0.0).then_inc(setup["fills"], 1)
            moe_gpsimd(pool, nc, b, moe_a)
            att_gpsimd(pool, nc, b, att)
            pool.wait_ge(moe_b["var"], 1)
            moe_gpsimd(pool, nc, b, moe_b)

        @block.tensor
        def _(pe):
            pe.wait_ge(b.loaded["ffn"], 16 * b.n_loads["ffn"])
            pe.wait_ge(setup["weights"], 3)
            ffn_tensor(pe, nc, b, ffn_a)
            pe.wait_ge(b.loaded["lin"], 16 * b.n_loads["lin"])
            pe.wait_ge(setup["fills"], 6)
            lin_tensor(pe, nc, b, lin)
            ffn_tensor(pe, nc, b, ffn_b)
            pe.wait_ge(b.loaded["moe"], 16 * b.n_loads["moe"])
            moe_tensor(pe, nc, b, moe_a)
            att_tensor(pe, nc, b, att)
            moe_tensor(pe, nc, b, moe_b)

        @block.vector
        def _(v):
            v.wait_ge(b.loaded["ffn"], 16 * b.n_loads["ffn"])
            pos, neg, sign, twice, minus = (b.sc[:, n:n + 2] for n in (3, 5, 7, 9, 11))
            s01 = b.sc[:, 0:2]
            nc.vector.tensor_scalar(pos, s01, 0.0, None, ALU.is_gt).then_inc(setup["signs"], 1)
            nc.vector.tensor_scalar(neg, s01, 0.0, None, ALU.is_lt).then_inc(setup["signs"], 1)
            v.wait_ge(setup["signs"], 2)
            nc.vector.tensor_tensor(sign, pos, neg, ALU.subtract).then_inc(setup["signs"], 1)
            v.wait_ge(setup["signs"], 3)
            nc.vector.tensor_scalar(twice, sign, 2.0, None, ALU.mult).then_inc(setup["signs"], 1)
            nc.vector.tensor_scalar(minus, sign, -1.0, None, ALU.mult).then_inc(setup["signs"], 1)
            nc.vector.tensor_tensor(b.sc[:, 13:15], s01, sign, ALU.mult).then_inc(setup["abs"], 1)
            nc.vector.tensor_tensor(b.k0f[:, :], b.k0u[:, 0, :], b.k0u[:, 1, :], ALU.subtract).then_inc(setup["diff"], 1)
            v.wait_ge(setup["signs"], 5)
            v.wait_ge(setup["abs"], 1)
            nc.vector.scalar_tensor_tensor(b.sc[:, 13:14], b.sc[:, 13:14], 2.0, b.sc[:, 14:15],
                                           ALU.mult, ALU.mult).then_inc(setup["abs"], 1)
            v.wait_ge(setup["abs"], 2)
            nc.vector.tensor_tensor(b.ffn_scale, b.sc[:, 13:14], b.sc[:, 2:3], ALU.mult).then_inc(setup["abs"], 1)
            v.wait_ge(setup["diff"], 1)
            nc.vector.tensor_scalar(b.k0[:, :], b.k0f[:, :], twice[:, 0:1], None, ALU.mult).then_inc(setup["weights"], 1)
            nc.vector.tensor_scalar(b.k1[:, :, :], b.k1u[:, :, :], twice[:, 1:2], minus[:, 1:2],
                                    ALU.mult, ALU.add).then_inc(setup["weights"], 1)
            nc.vector.tensor_scalar(b.k2[:, :, :], b.k2u[:, :, :], 2.0, -1.0, ALU.mult, ALU.add).then_inc(setup["weights"], 1)
            v.wait_ge(setup["abs"], 3)
            for c in range(NCH):
                v.wait_ge(x_in[c], 16)
                for t in range(CT * c, CT * c + CT):
                    nc.vector.bn_stats(b.bn[:, t, :], b.x[:, t, :]).then_inc(b.bn_done, 1)
            ffn_vector(v, nc, b, ffn_a, 0)
            v.wait_ge(b.loaded["lin"], 16 * b.n_loads["lin"])
            lin_vector(v, nc, b, lin, 1)
            ffn_vector(v, nc, b, ffn_b, 2)
            v.wait_ge(b.loaded["moe"], 16 * b.n_loads["moe"])
            moe_vector(v, nc, b, moe_a, 3)
            v.wait_ge(setup["fills"], 6)
            att_vector(v, nc, b, att, 4)
            moe_vector(v, nc, b, moe_b, 5)


def kernel(**inputs):
    import numpy as np
    import concourse.bacc as bacc
    from concourse.bass_utils import run_bass_kernel_spmd

    def grouped(w):
        w = np.asarray(w).reshape(C, NG, 32)
        return np.concatenate([w, w, w], axis=2)

    def grouped_bias(v):
        v = np.asarray(v).reshape(NG, 32).T
        return np.concatenate([v, v, v], axis=0)

    given = {n: np.asarray(v) for n, v in inputs.items()}
    arrays = {n: given[n] for n in (
        "L0_attn_x", "L0_attn_proj_bias", "L0_ffn_k0", "L0_ffn_k1", "L0_ffn_k2", "L1_attn_Wv", "L1_attn_bv",
        "L1_attn_Wo", "L1_attn_bo", "L1_attn_Wrv", "L1_attn_brv", "L1_attn_Wg", "L1_attn_bg", "L1_ffn_Wr",
        "L1_ffn_br", "L1_ffn_W1", "L1_ffn_W2")}
    arrays["wqkv0_t"] = given["L0_attn_qkv_weight"].T
    arrays["wproj0_t"] = given["L0_attn_proj_weight"].T
    arrays["s_cols"] = np.tile(np.stack([given["L0_ffn_s0"], given["L0_ffn_s1"], given["L0_ffn_s2"]]).reshape(1, 3), (P, 1))
    arrays["b1_t"] = given["L1_ffn_b1"].reshape(NE * HB, P).T
    arrays["b2_t"] = given["L1_ffn_b2"].T
    arrays["past_t"] = given["L1_attn_past_states"].reshape(PAST * SEQ, C).T
    for name, w, bias in (("q", "Wq", "bq"), ("k", "Wk", "bk"), ("rq", "Wrq", "brq"), ("rk", "Wrk", "brk")):
        arrays[f"w{name}_rep"] = grouped(given["L1_attn_" + w])
        arrays[f"b{name}_rep"] = grouped_bias(given["L1_attn_" + bias])
    f = np.arange(P)
    arrays["ident"] = np.eye(P, dtype=np.float32)
    mask = (f[:, None] // 4 == f[None, :] // 4).astype(np.float32)
    arrays["blockmask"] = np.concatenate([mask, mask], axis=1)
    arrays["iota8"] = np.tile(np.arange(NE, dtype=np.float32), (P, 1))
    arrays["headmask"] = (f[:QK, None] % 32 // D == np.arange(4)[None, :]).astype(np.float32)
    sel = np.zeros((32, NH + NH * PAST), np.float32)
    for h in range(NH):
        for a in range(PAST):
            rows = slice(4 * (h % 4) + 2 * a, 4 * (h % 4) + 2 * a + 2)
            if a == 0:
                sel[rows, h] = -1.0
            sel[rows, NH + h * PAST + a] = -1.0
    arrays["sel"] = sel

    nc = bacc.Bacc("TRN2", target_bir_lowering=False, num_devices=1)
    feed, args = {}, {}
    for name, arr in arrays.items():
        arr = np.ascontiguousarray(arr)
        feed[f"in_{name}"] = arr
        args[name] = nc.dram_tensor(f"in_{name}", arr.shape, mybir.dt.from_np(arr.dtype), kind="ExternalInput").ap()
    out = nc.dram_tensor("out_x", (BATCH, SEQ, C), F32, kind="ExternalOutput").ap()
    macaron(nc, args, out)
    result = run_bass_kernel_spmd(nc, [feed], core_ids=[0])
    return result.results[0]["out_x"]
```

```python
from contextlib import ExitStack

import concourse.bass as bass
from concourse import mybir

F32 = mybir.dt.float32
F32R = mybir.dt.float32r
U8 = mybir.dt.uint8
U32 = mybir.dt.uint32
ALU = mybir.AluOpType
ACT = mybir.ActivationFunctionType
AX = mybir.AxisListType

P = 128
BATCH, SEQ, C = 16, 256, 128
T = BATCH * SEQ
TILES = T // P
CT = 4
CH = CT * P
NCH = T // CH
HB = 4
LN_EPS = 1e-5
LIN_EPS = 1e-15
NE = 8
NH = 16
D = C // NH
NG = 4
PAST = 2
SCALE = float(1.0 / (D ** 0.5))
BT = SEQ // P
VW = 32


class Buffers:
    pass


def stats_vector(v, nc, b, s, layer):
    done = s["stats"]
    n = 0
    mean, diff, var, sd, r, t = (b.ln[:, k, :] for k in range(6))
    even, odd = b.bn[:, :, 0:3], b.bn[:, :, 3:6]
    v.wait_ge(b.bn_done, TILES * (layer + 1))
    nc.vector.tensor_tensor(mean, even[:, :, 1], odd[:, :, 1], ALU.add).then_inc(done, 1)
    nc.vector.tensor_tensor(diff, even[:, :, 1], odd[:, :, 1], ALU.subtract).then_inc(done, 1)
    nc.vector.tensor_tensor(var, even[:, :, 2], odd[:, :, 2], ALU.add).then_inc(done, 1)
    v.wait_ge(done, 3)
    nc.vector.tensor_scalar(mean, mean, 0.5, None, ALU.mult).then_inc(done, 1)
    nc.vector.tensor_tensor(diff, diff, diff, ALU.mult).then_inc(done, 1)
    nc.vector.tensor_scalar(var, var, 1.0 / C, LN_EPS, ALU.mult, ALU.add).then_inc(done, 1)
    v.wait_ge(done, 6)
    nc.vector.scalar_tensor_tensor(var, diff, 0.25, var, ALU.mult, ALU.add).then_inc(s["var"], 1)
    v.wait_ge(s["sd"], 1)
    nc.vector.reciprocal(r, sd).then_inc(done, 1)
    v.wait_ge(done, 7)
    nc.vector.tensor_tensor(t, r, r, ALU.mult).then_inc(done, 1)
    v.wait_ge(done, 8)
    nc.vector.tensor_tensor(t, t, var, ALU.mult).then_inc(done, 1)
    v.wait_ge(done, 9)
    nc.vector.tensor_scalar(t, t, -0.5, 1.5, ALU.mult, ALU.add).then_inc(done, 1)
    v.wait_ge(done, 10)
    nc.vector.tensor_tensor(r, r, t, ALU.mult).then_inc(done, 1)
    v.wait_ge(done, 11)


def stats_scalar(act, nc, b, s):
    act.wait_ge(s["var"], 1)
    nc.scalar.activation(b.ln[:, 3, :], b.ln[:, 2, :], ACT.Sqrt).then_inc(s["sd"], 1)


def normalise(nc, b, out, tile):
    return nc.vector.tensor_scalar(out, b.x[:, tile, :], b.ln[:, 0, tile], b.ln[:, 4, tile],
                                   ALU.subtract, ALU.mult)


STATS_SEMS = ["stats", "var", "sd", "passed"]


FFN_SEMS = STATS_SEMS + ["xn_ready", "xt_full", "x_hi", "x_split", "z_full", "z_hi", "z_split", "y_full",
                         "y_copied", "yt_full", "x_added"]
FFN_XT, FFN_Y, FFN_YT = 4, 5, 6


def ffn_tensor(pe, nc, b, s):
    bank = b.banks

    def turn_x(c):
        pe.wait_ge(s["xn_ready"], c + 1)
        if not (isinstance(c, int) and c == 0):
            pe.wait_ge(s["x_split"], c)
        for j in range(CT):
            mm = pe.transpose(bank[:, FFN_XT, P * j:P * j + P], b.xn[:, j, :], b.ident[:, :])
        mm.then_inc(s["xt_full"], 1)

    def first(c):
        pe.wait_ge(s["x_split"], c + 1)
        for m in range(HB):
            if not (isinstance(c, int) and c == 0):
                pe.wait_ge(s["z_split"], 8 * c + m - 3)
            w = b.k0[:, P * m:P * m + P]
            pe.matmul(bank[:, m, :], w, b.xh[:, :], start=True, stop=False)
            pe.matmul(bank[:, m, :], w, b.xl[:, :], start=False, stop=True).then_inc(s["z_full"], 1)

    def middle(c, m):
        for k in range(HB):
            if m == 0:
                pe.wait_ge(s["z_split"], 8 * c + k + 1)
            w = b.k1[:, k, P * m:P * m + P]
            pe.matmul(bank[:, m, :], w, b.h_hi[:, k, :], start=k == 0, stop=False)
            mm = pe.matmul(bank[:, m, :], w, b.h_lo[:, k, :], start=False, stop=k == HB - 1)
        mm.then_inc(s["z_full"], 1)

    def last(c):
        pe.wait_ge(s["y_copied"], c + 1)
        for k in range(HB):
            pe.wait_ge(s["z_split"], 8 * c + 5 + k)
            pe.matmul(bank[:, FFN_Y, :], b.k2[:, k, :], b.g_hi[:, k, :], start=k == 0, stop=False)
            mm = pe.matmul(bank[:, FFN_Y, :], b.k2[:, k, :], b.g_lo[:, k, :], start=False, stop=k == HB - 1)
        mm.then_inc(s["y_full"], 1)

    def turn_y(c):
        pe.wait_ge(s["y_copied"], c + 2)
        pe.wait_ge(s["x_added"], c + 1)
        for j in range(CT):
            mm = pe.transpose(bank[:, FFN_YT, P * j:P * j + P], b.y[:, P * j:P * j + P], b.ident[:, :])
        mm.then_inc(s["yt_full"], 1)

    turn_x(0)
    first(0)
    for m in range(HB):
        middle(0, m)
    turn_x(1)
    first(1)
    with pe.Fori(0, NCH - 2) as i:
        last(i)
        middle(i + 1, 0)
        turn_y(i)
        for m in range(1, HB):
            middle(i + 1, m)
        turn_x(i + 2)
        first(i + 2)
    last(NCH - 2)
    middle(NCH - 1, 0)
    turn_y(NCH - 2)
    for m in range(1, HB):
        middle(NCH - 1, m)
    last(NCH - 1)
    turn_y(NCH - 1)


def ffn_scalar(act, nc, b, s):
    bank = b.banks
    stats_scalar(act, nc, b, s)
    act.sem_inc(s["y_copied"], 1)

    def x_hi(c):
        act.wait_ge(s["xt_full"], c + 1)
        nc.scalar.copy(b.xh[:, :], bank[:, FFN_XT, :]).then_inc(s["x_hi"], 1)

    def relu(n, m, out):
        act.wait_ge(s["z_full"], n + 1)
        nc.scalar.activation(out[:, m, :], bank[:, m, :], ACT.Relu).then_inc(s["z_hi"], 1)

    def y_copy(c):
        act.wait_ge(s["y_full"], c + 1)
        nc.scalar.activation(b.y[:, :], bank[:, FFN_Y, :], ACT.Identity,
                             scale=b.ffn_scale[:, 0:1]).then_inc(s["y_copied"], 1)

    x_hi(0)
    for m in range(HB):
        relu(m, m, b.h_hi)
    for m in range(HB):
        relu(HB + m, m, b.g_hi)
    x_hi(1)
    for m in range(HB):
        relu(8 + m, m, b.h_hi)
    with act.Fori(0, NCH - 2) as i:
        y_copy(i)
        for m in range(HB):
            relu(8 * i + 12 + m, m, b.g_hi)
        x_hi(i + 2)
        for m in range(HB):
            relu(8 * i + 16 + m, m, b.h_hi)
    y_copy(NCH - 2)
    for m in range(HB):
        relu(8 * (NCH - 1) + 4 + m, m, b.g_hi)
    y_copy(NCH - 1)


def ffn_vector(v, nc, b, s, layer):
    bank = b.banks
    stats_vector(v, nc, b, s, layer)
    v.sem_inc(s["x_added"], 1)

    def xn(c):
        if not (isinstance(c, int) and c == 0):
            v.wait_ge(s["xt_full"], c)
        for j in range(CT):
            ins = normalise(nc, b, b.xn[:, j, :], bass.ds(c * CT + j, 1))
        ins.then_inc(s["xn_ready"], 1)

    def x_lo(c):
        v.wait_ge(s["x_hi"], c + 1)
        nc.vector.tensor_tensor(b.xl[:, :], bank[:, FFN_XT, :], b.xh[:, :].bitcast(F32),
                                ALU.subtract).then_inc(s["x_split"], 1)

    def relu_lo(n, m, hi, lo):
        v.wait_ge(s["z_hi"], n + 1)
        nc.vector.scalar_tensor_tensor(lo[:, m, :], bank[:, m, :], 0.0, hi[:, m, :].bitcast(F32),
                                       ALU.max, ALU.subtract).then_inc(s["z_split"], 1)

    def add(c):
        v.wait_ge(s["yt_full"], c + 1)
        xs = b.xc[:, bass.ds(c, 1), :]
        nc.vector.tensor_tensor(xs, xs, bank[:, FFN_YT:FFN_YT + 1, :], ALU.add).then_inc(s["x_added"], 1)
        v.wait_ge(s["x_added"], c + 2)
        for j in range(CT):
            nc.vector.bn_stats(b.bn[:, bass.ds(c * CT + j, 1), :], b.x[:, bass.ds(c * CT + j, 1), :]).then_inc(b.bn_done, 1)

    xn(0)
    x_lo(0)
    for m in range(HB):
        relu_lo(m, m, b.h_hi, b.h_lo)
    xn(1)
    for m in range(HB):
        relu_lo(HB + m, m, b.g_hi, b.g_lo)
    x_lo(1)
    for m in range(HB):
        relu_lo(8 + m, m, b.h_hi, b.h_lo)
    with v.Fori(0, NCH - 2) as i:
        xn(i + 2)
        relu_lo(8 * i + 12, 0, b.g_hi, b.g_lo)
        add(i)
        for m in range(1, HB):
            relu_lo(8 * i + 12 + m, m, b.g_hi, b.g_lo)
        x_lo(i + 2)
        for m in range(HB):
            relu_lo(8 * i + 16 + m, m, b.h_hi, b.h_lo)
    relu_lo(8 * NCH - 4, 0, b.g_hi, b.g_lo)
    add(NCH - 2)
    for m in range(1, HB):
        relu_lo(8 * NCH - 4 + m, m, b.g_hi, b.g_lo)
    add(NCH - 1)


LIN_SEMS = STATS_SEMS + ["xn_ready", "xt_full", "xt_ready", "q_full", "q_ready", "kv_full", "kv_ready",
                         "sum_full", "sum_ready", "ratio_full", "den", "inv", "ratio_ready", "y_full", "x_added"]
LIN_XT, LIN_Q, LIN_KV, LIN_SUM, LIN_NUM = 0, 1, 2, 4, 6


def lin_tensor(pe, nc, b, s):
    bank = b.banks
    with pe.Fori(0, NCH) as c:
        pe.wait_ge(s["xn_ready"], c + 1)
        pe.wait_ge(s["x_added"], c + 1)
        for j in range(CT):
            mm = pe.transpose(bank[:, LIN_XT, P * j:P * j + P], b.xn[:, j, :], b.ident[:, :])
        mm.then_inc(s["xt_full"], 1)
        pe.wait_ge(s["xt_ready"], c + 1)
        for half in range(2):
            for j in range(2):
                t = 2 * half + j
                mm = pe.matmul(bank[:, LIN_KV + half, 256 * j:256 * j + 256], b.xT[:, P * t:P * t + P],
                               b.wkv0[:, :], start=True, stop=True)
            mm.then_inc(s["kv_full"], 1)
        pe.matmul(bank[:, LIN_Q, :], b.wq0[:, :], b.xT[:, :], start=True, stop=True).then_inc(s["q_full"], 1)
        for e in range(2):
            pe.wait_ge(s["kv_ready"], 2 * c + e + 1)
            for j in range(2):
                t = 2 * e + j
                mm = pe.matmul(bank[:, LIN_SUM + e, 0:256], b.kv[:, t, 0:P], b.kv[:, t, P:3 * P],
                               start=j == 0, stop=j == 1)
            mm.then_inc(s["sum_full"], 1)
        pe.wait_ge(s["q_ready"], c + 1)
        for e in range(2):
            pe.wait_ge(s["sum_ready"], 2 * c + e + 1)
            rhs = b.qT[:, SEQ * e:SEQ * e + SEQ]
            pe.matmul(bank[:, LIN_NUM + e, SEQ:2 * SEQ], b.kvm[:, e, P:2 * P], rhs, start=True, stop=True)
            pe.matmul(bank[:, LIN_NUM + e, 0:SEQ], b.kvm[:, e, 0:P], rhs,
                      start=True, stop=True).then_inc(s["ratio_full"], 1)
        for e in range(2):
            pe.wait_ge(s["ratio_ready"], 2 * c + e + 1)
            for j in range(2):
                t = 2 * e + j
                pe.matmul(bank[:, LIN_XT, P * t:P * t + P], b.ratio[:, P * t:P * t + P], b.wp0[:, :],
                          start=True, stop=False)
                mm = pe.matmul(bank[:, LIN_XT, P * t:P * t + P], b.ones[0:1, 0:P], b.pb0[0:1, :],
                               start=False, stop=True)
        mm.then_inc(s["y_full"], 1)


def lin_scalar(act, nc, b, s):
    bank = b.banks
    stats_scalar(act, nc, b, s)
    with act.Fori(0, NCH) as c:
        act.wait_ge(s["xt_full"], c + 1)
        nc.scalar.copy(b.xT[:, :], bank[:, LIN_XT, :]).then_inc(s["xt_ready"], 1)
        for half in range(2):
            act.wait_ge(s["kv_full"], 2 * c + half + 1)
            nc.scalar.activation(b.kv[:, 2 * half:2 * half + 2, 0:256],
                                 bank[:, LIN_KV + half, :].rearrange("p (t f) -> p t f", t=2),
                                 ACT.Relu).then_inc(s["kv_ready"], 1)
        act.wait_ge(s["q_full"], c + 1)
        nc.scalar.activation(b.qT[:, :], bank[:, LIN_Q, :], ACT.Relu).then_inc(s["q_ready"], 1)


def lin_vector(v, nc, b, s, layer):
    bank = b.banks
    stats_vector(v, nc, b, s, layer)
    v.sem_inc(s["x_added"], 1)
    for j in range(CT):
        ins = normalise(nc, b, b.xn[:, j, :], bass.ds(j, 1))
    ins.then_inc(s["xn_ready"], 1)

    def attend(c):
        for e in range(2):
            v.wait_ge(s["sum_full"], 2 * c + e + 1)
            nc.vector.tensor_tensor(b.kvm[:, e, :], bank[:, LIN_SUM + e, 0:256], b.blockmask[:, :],
                                    ALU.mult).then_inc(s["sum_ready"], 1)
        for e in range(2):
            v.wait_ge(s["ratio_full"], 2 * c + e + 1)
            sl = slice(SEQ * e, SEQ * e + SEQ)
            nc.vector.tensor_scalar(b.rec[:, sl], bank[:, LIN_NUM + e, SEQ:2 * SEQ], LIN_EPS, None, ALU.add).then_inc(s["den"], 1)
            v.wait_ge(s["den"], 2 * c + e + 1)
            nc.vector.reciprocal(b.rec[:, sl], b.rec[:, sl]).then_inc(s["inv"], 1)
            v.wait_ge(s["inv"], 2 * c + e + 1)
            nc.vector.tensor_tensor(b.ratio[:, sl], bank[:, LIN_NUM + e, 0:SEQ], b.rec[:, sl],
                                    ALU.mult).then_inc(s["ratio_ready"], 1)

    def add(c):
        v.wait_ge(s["y_full"], c + 1)
        xs = b.xc[:, bass.ds(c, 1), :]
        nc.vector.tensor_tensor(xs, xs, bank[:, LIN_XT:LIN_XT + 1, :], ALU.add).then_inc(s["x_added"], 1)
        v.wait_ge(s["x_added"], c + 2)
        for j in range(CT):
            nc.vector.bn_stats(b.bn[:, bass.ds(c * CT + j, 1), :], b.x[:, bass.ds(c * CT + j, 1), :]).then_inc(b.bn_done, 1)

    with v.Fori(0, NCH - 1) as c:
        v.wait_ge(s["xt_full"], c + 1)
        for j in range(CT):
            ins = normalise(nc, b, b.xn[:, j, :], bass.ds((c + 1) * CT + j, 1))
        ins.then_inc(s["xn_ready"], 1)
        attend(c)
        add(c)
    attend(NCH - 1)
    add(NCH - 1)


MOE_SEMS = STATS_SEMS + ["xn_ready", "xt_full", "xt_ready", "x_hi", "x_split", "lg_full", "lg_ready", "rt",
                         "rt_diff", "rt_exp", "rt_top", "rt_idx", "rt_w2", "w_ready", "weights_in", "weights_hi", "weights_split",
                         "z_full", "z_gelu", "h_hi", "h_split", "h_used", "y_copied", "yt_full",
                         "x_added"]
MOE_XT, MOE_LG = 6, 7
MOE_Y, MOE_YT = 4, 5
RT_STEPS = 8


def moe_sync(sp, nc, b, s):
    with sp.Fori(0, NE) as e:
        sp.wait_ge(s["weights_split"], 2 * e + 2)
        sp.dma_start(b.w1_raw[:, :], b.W1[bass.ds(e, 1), :, :].rearrange("o c h -> (o c) h")).then_inc(s["weights_in"], 16)
        sp.dma_start(b.w2_raw[:, :, :],
                     b.W2[bass.ds(e, 1), :, :].rearrange("o (k p) c -> p (o k) c", p=P)).then_inc(s["weights_in"], 16)


def moe_gpsimd(pool, nc, b, s):
    def split(e, half, reused):
        pool.wait_ge(s["weights_in"], 32 * e + 32)
        if reused:
            pool.wait_ge(s["h_used"], 32 * e - 28)
        pool.sem_inc(s["passed"], 1)
        w2 = b.w2_raw[:, :, :].rearrange("p k c -> p (k c)")
        nc.gpsimd.tensor_copy(b.w1h[:, half, :], b.w1_raw[:, :]).then_inc(s["weights_hi"], 1)
        nc.gpsimd.tensor_copy(b.w2h[:, half, :], w2).then_inc(s["weights_hi"], 1)
        pool.wait_ge(s["weights_hi"], 2 * e + 1)
        nc.gpsimd.tensor_tensor(b.w1l[:, half, :], b.w1_raw[:, :], b.w1h[:, half, :].bitcast(F32),
                                ALU.subtract).then_inc(s["weights_split"], 1)
        pool.wait_ge(s["weights_hi"], 2 * e + 2)
        nc.gpsimd.tensor_tensor(b.w2l[:, half, :], w2, b.w2h[:, half, :].bitcast(F32),
                                ALU.subtract).then_inc(s["weights_split"], 1)

    def hi(z, m):
        pool.wait_ge(s["z_gelu"], z + 1 + HB)
        pool.wait_ge(s["h_used"], z + 1)
        pool.sem_inc(s["passed"], 1)
        nc.gpsimd.tensor_copy(b.h_hi[:, m, :], b.h_raw[:, m, :]).then_inc(s["h_hi"], 1)

    pool.sem_inc(s["weights_split"], 2)
    split(0, 0, False)
    with pool.Fori(0, NE // 2 - 1) as pair:
        for half in range(2):
            e = 2 * pair + half
            for c in range(2):
                for m in range(HB):
                    hi(32 * e + 4 * c + m, m)
            split(e + 1, 1 - half, True)
            with pool.Fori(2, NCH) as c:
                for m in range(HB):
                    hi(32 * e + 4 * c + m, m)
    with pool.Fori(0, NCH) as c:
        for m in range(HB):
            hi(32 * (NE - 2) + 4 * c + m, m)
    split(NE - 1, 1, True)
    with pool.Fori(0, NCH) as c:
        for m in range(HB):
            hi(32 * (NE - 1) + 4 * c + m, m)


def moe_tensor(pe, nc, b, s):
    bank = b.banks
    pe.sem_inc(s["h_used"], HB)
    pe.sem_inc(s["lg_full"], 1)
    pe.sem_inc(s["yt_full"], 1)
    with pe.Fori(0, NCH) as c:
        pe.wait_ge(s["xn_ready"], c + 1)
        pe.wait_ge(s["x_split"], c + 1)
        for j in range(CT):
            mm = pe.transpose(bank[:, MOE_XT, P * j:P * j + P], b.xn[:, j, :], b.ident[:, :])
        mm.then_inc(s["xt_full"], 1)
        pe.wait_ge(s["xt_ready"], c + 1)
        pe.wait_ge(s["lg_ready"], c + 1)
        for j in range(CT):
            out = bank[:, MOE_LG, NE * j:NE * j + NE]
            pe.matmul(out, b.xT[:, P * j:P * j + P], b.wr[:, :], start=True, stop=False)
            mm = pe.matmul(out, b.ones[0:1, 0:P], b.br[0:1, :], start=False, stop=True)
        mm.then_inc(s["lg_full"], 1)

    def first(e, c, m, half):
        pe.wait_ge(s["z_gelu"], 32 * e + 4 * c + m + 1)
        wh, wl = b.w1h[:, half, P * m:P * m + P], b.w1l[:, half, P * m:P * m + P]
        xh, xl = b.xh_all[:, bass.ds(c * CH, CH)], b.xl_all[:, bass.ds(c * CH, CH)]
        pe.matmul(bank[:, m, :], wh, xh, start=True, stop=False)
        pe.matmul(bank[:, m, :], wl, xh, start=False, stop=False)
        pe.matmul(bank[:, m, :], wh, xl, start=False, stop=True).then_inc(s["z_full"], 1)

    def second(e, c, m, half):
        if m == 0:
            pe.wait_ge(s["y_copied"], 8 * e + c + 1)
        pe.wait_ge(s["h_split"], 32 * e + 4 * c + m + 1 + HB)
        wh, wl = b.w2h[:, half, P * m:P * m + P], b.w2l[:, half, P * m:P * m + P]
        pe.matmul(bank[:, MOE_Y, :], wh, b.h_hi[:, m, :], start=m == 0, stop=False)
        pe.matmul(bank[:, MOE_Y, :], wl, b.h_hi[:, m, :], start=False, stop=False)
        mm = pe.matmul(bank[:, MOE_Y, :], wh, b.h_lo[:, m, :], start=False, stop=m == HB - 1)
        mm.then_inc(s["h_used"], 1)

    def turn_y(e, c):
        pe.wait_ge(s["y_copied"], 8 * e + c + 2)
        pe.wait_ge(s["x_added"], 8 * e + c + 1)
        for j in range(CT):
            mm = pe.transpose(bank[:, MOE_YT, P * j:P * j + P], b.y[:, P * j:P * j + P], b.ident[:, :])
        mm.then_inc(s["yt_full"], 1)

    pe.wait_ge(s["x_split"], NCH + 1)
    with pe.Fori(0, NE // 2) as pair:
        for half in range(2):
            e = 2 * pair + half
            pe.wait_ge(s["weights_split"], 2 * e + 4)
            for m in range(HB):
                first(e, 0, m, half)
            for m in range(HB):
                first(e, 1, m, half)
                second(e, 0, m, half)
            with pe.Fori(1, NCH - 1) as c:
                for m in range(HB):
                    first(e, c + 1, m, half)
                    second(e, c, m, half)
                    if m == 0:
                        turn_y(e, c - 1)
            for m in range(HB):
                second(e, NCH - 1, m, half)
                if m == 0:
                    turn_y(e, NCH - 2)
            turn_y(e, NCH - 1)
        

def moe_scalar(act, nc, b, s):
    bank = b.banks
    stats_scalar(act, nc, b, s)
    act.sem_inc(s["z_gelu"], HB)
    act.sem_inc(s["y_copied"], 1)
    with act.Fori(0, NCH) as c:
        act.wait_ge(s["xt_full"], c + 1)
        act.wait_ge(s["lg_full"], c + 1)
        nc.scalar.copy(b.xT[:, :], bank[:, MOE_XT, :]).then_inc(s["xt_ready"], 1)
        nc.scalar.copy(b.xh_all[:, bass.ds(c * CH, CH)], bank[:, MOE_XT, :]).then_inc(s["x_hi"], 1)
        act.wait_ge(s["rt_diff"], c + 1)
        nc.scalar.activation(b.rt[:, 1, :], b.rt[:, 0, :], ACT.Exp).then_inc(s["rt_exp"], 1)

    def gelu(e, c, m):
        z = 32 * e + 4 * c + m
        act.wait_ge(s["z_full"], z + 1)
        act.wait_ge(s["h_split"], z + 1)
        act.sem_inc(s["passed"], 1)
        nc.scalar.activation(b.h_raw[:, m, :], bank[:, m, :], ACT.Gelu,
                             bias=b.b1[:, bass.ds(4 * e + m, 1)]).then_inc(s["z_gelu"], 1)

    def y_copy(e, c):
        act.wait_ge(s["h_used"], 32 * e + 4 * c + 4 + HB)
        act.wait_ge(s["yt_full"], 8 * e + c + 1)
        act.sem_inc(s["passed"], 1)
        nc.scalar.activation(b.y[:, :], bank[:, MOE_Y, :], ACT.Identity,
                             bias=b.b2[:, bass.ds(e, 1)]).then_inc(s["y_copied"], 1)

    with act.Fori(0, NE) as e:
        for m in range(HB):
            gelu(e, 0, m)
        with act.Fori(0, NCH - 1) as c:
            for m in range(HB):
                gelu(e, c + 1, m)
            y_copy(e, c)
        y_copy(e, NCH - 1)


def moe_vector(v, nc, b, s, layer):
    bank = b.banks
    stats_vector(v, nc, b, s, layer)
    v.sem_inc(s["h_split"], HB)
    for name in ("x_split", "lg_ready", "x_added"):
        v.sem_inc(s[name], 1)
    for j in range(CT):
        ins = normalise(nc, b, b.xn[:, j, :], bass.ds(j, 1))
    ins.then_inc(s["xn_ready"], 1)
    steps = s["rt"]
    diff, ex, w1, w2 = (b.rt[:, k, :] for k in range(4))

    def route(c):
        v.wait_ge(s["x_hi"], c + 1)
        nc.vector.tensor_tensor(b.xl_all[:, bass.ds(c * CH, CH)], bank[:, MOE_XT, :],
                                b.xh_all[:, bass.ds(c * CH, CH)].bitcast(F32), ALU.subtract).then_inc(s["x_split"], 1)
        v.wait_ge(s["lg_full"], c + 2)
        nc.vector.tensor_copy(b.lg[:, :, :], bank[:, MOE_LG, 0:CT * NE].rearrange("p (j e) -> p j e", e=NE)).then_inc(s["lg_ready"], 1)
        v.wait_ge(s["lg_ready"], c + 2)
        v.sem_inc(s["passed"], 1)
        for j in range(CT):
            nc.vector.max(b.top[:, j, :], b.lg[:, j, :]).then_inc(s["rt_top"], 1)
        v.wait_ge(s["rt_top"], CT * c + CT)
        nc.vector.tensor_tensor(diff, b.top[:, :, 1], b.top[:, :, 0], ALU.subtract).then_inc(s["rt_diff"], 1)
        for j in range(CT):
            nc.vector.max_index(b.idx[:, j, :], b.top[:, j, :], b.lg[:, j, :]).then_inc(s["rt_idx"], 1)
        v.wait_ge(s["rt_idx"], CT * c + CT)
        nc.vector.tensor_copy(b.idxf[:, :, :], b.idx[:, :, 0:2]).then_inc(steps, 1)
        v.wait_ge(s["rt_exp"], c + 1)
        nc.vector.tensor_scalar(w1, ex, 1.0, None, ALU.add).then_inc(steps, 1)
        v.wait_ge(steps, RT_STEPS * c + 2)
        nc.vector.reciprocal(w1, w1).then_inc(steps, 1)
        iota = b.iota8[:, None, :].to_broadcast([P, CT, NE])
        for k in range(2):
            nc.vector.tensor_tensor(b.oh[:, k, :, :], iota, b.idxf[:, :, k:k + 1].to_broadcast([P, CT, NE]),
                                    ALU.is_equal).then_inc(steps, 1)
        v.wait_ge(steps, RT_STEPS * c + 3)
        nc.vector.tensor_scalar(w1, w1, 0.5, None, ALU.mult).then_inc(steps, 1)
        v.wait_ge(steps, RT_STEPS * c + 6)
        nc.vector.tensor_tensor(w2, w1, ex, ALU.mult).then_inc(steps, 1)
        nc.vector.tensor_tensor(b.oh[:, 0, :, :], b.oh[:, 0, :, :], w1[:, :, None].to_broadcast([P, CT, NE]),
                                ALU.mult).then_inc(steps, 1)
        v.wait_ge(steps, RT_STEPS * c + 8)
        nc.vector.tensor_tensor(b.oh[:, 1, :, :], b.oh[:, 1, :, :], w2[:, :, None].to_broadcast([P, CT, NE]),
                                ALU.mult).then_inc(s["rt_w2"], 1)
        v.wait_ge(s["rt_w2"], c + 1)
        nc.vector.tensor_tensor(b.wf[:, bass.ds(c * CT, CT), :], b.oh[:, 0, :, :], b.oh[:, 1, :, :],
                                ALU.add).then_inc(s["w_ready"], 1)

    with v.Fori(0, NCH - 1) as c:
        v.wait_ge(s["xt_full"], c + 1)
        for j in range(CT):
            ins = normalise(nc, b, b.xn[:, j, :], bass.ds((c + 1) * CT + j, 1))
        ins.then_inc(s["xn_ready"], 1)
        route(c)
    route(NCH - 1)
    v.wait_ge(s["w_ready"], NCH)

    def lo(e, c, m):
        z = 32 * e + 4 * c + m
        v.wait_ge(s["h_hi"], z + 1)
        nc.vector.tensor_tensor(b.h_lo[:, m, :], b.h_raw[:, m, :], b.h_hi[:, m, :].bitcast(F32),
                                ALU.subtract).then_inc(s["h_split"], 1)

    def add(e, c):
        v.wait_ge(s["yt_full"], 8 * e + c + 2)
        v.wait_ge(s["x_added"], 8 * e + c + 1)
        for j in range(CT):
            xs = b.x[:, bass.ds(c * CT + j, 1), :]
            ins = nc.vector.scalar_tensor_tensor(xs, bank[:, MOE_YT:MOE_YT + 1, P * j:P * j + P],
                                                 b.wfe[:, bass.ds(c * CT * NE + j * NE + e, 1)], xs,
                                                 ALU.mult, ALU.add)
        ins.then_inc(s["x_added"], 1)

    with v.Fori(0, NE) as e:
        for m in range(HB):
            lo(e, 0, m)
        for m in range(HB):
            lo(e, 1, m)
        with v.Fori(1, NCH - 1) as c:
            lo(e, c + 1, 0)
            add(e, c - 1)
            for m in range(1, HB):
                lo(e, c + 1, m)
        add(e, NCH - 2)
        add(e, NCH - 1)
    v.wait_ge(s["x_added"], NE * NCH + 1)
    with v.Fori(0, TILES) as t:
        nc.vector.bn_stats(b.bn[:, bass.ds(t, 1), :], b.x[:, bass.ds(t, 1), :]).then_inc(b.bn_done, 1)


ATT_SEMS = STATS_SEMS + ["xn_ready", "sel_ready", "s_full", "s_hi", "s_free", "st_full", "st_free", "masked",
                         "shift_hi", "shift_cols", "pv_done", "pv_saved", "flipped", "inv", "scaled", "normed",
                         "half_bg", "kept", "mix"]
S_BANK, ST_BANK, PV_BANK = 0, 2, 6
QK = 96
S_SLOTS, ST_SLOTS, PV_SLOTS = 2, 2, 2
P_SLOTS = 6


def step_order(own, rec, prep, fin):
    kinds = (["own"] if own else []) + (["rec"] if rec else [])

    def maxima(g):
        if own:
            for h in range(2):
                for t in range(BT):
                    yield "max", "own", g, h, t
        if rec:
            for h in range(4):
                for t in range(BT):
                    yield "max", "rec", g, h, t

    pairs = [(kind, g, half) for g in range(NG) for kind in kinds for half in range(PAST if kind == "rec" else 1)]
    if pairs:
        yield from maxima(0)
    if fin:
        yield "fin", "ctx", 0, 0, 0
    if pairs:
        yield "turn", kinds[0], 0, 0, 0
    if fin:
        yield "fin", "gate", 0, 0, 0
        if not pairs:
            yield "fin", "mix", 0, 0, 0
            yield "fin", "mix", 1, 0, 0
    per_group = len(pairs) // NG
    for n, (kind, g, half) in enumerate(pairs):
        nxt = list(maxima(g + 1)) if g + 1 < NG else []
        in_group = n % per_group
        for u in range(2):
            yield "unit", kind, g, 2 * half + u, 0
            at = 2 * in_group + u
            if n == 0 and u == 0 and len(kinds) == 2:
                yield "turn", kinds[1], 0, 0, 0
            elif g > 0 and at == 0 and len(kinds) == 2:
                yield "turn", kinds[1], g, 0, 0
            if n > 1 and u == 0:
                yield ("save",) + pairs[n - 2] + (0,)
            turns = 2 * per_group - 1
            yield from nxt[at * len(nxt) // turns:(at + 1) * len(nxt) // turns]
            if u == 1:
                if n > 1:
                    yield ("flip",) + pairs[n - 2] + (0,)
                if n > 0:
                    yield ("pv",) + pairs[n - 1] + (0,)
            if nxt and at == 2 * per_group - 2:
                yield "turn", kinds[0], g + 1, 0, 0
            if prep:
                if g == 0 and at == 1:
                    yield "prep", "x", 0, 0, 0
                if g > 0 and at == 0:
                    yield "prep", "k", g - 1, 0, 0
                if g > 0 and at == 1:
                    yield "prep", "q", g - 1, 0, 0
            if fin and g == 1 and at in (2, 3):
                yield "fin", "mix", at - 2, 0, 0
            if rec and g == 1 and at == 3:
                yield "keep", "out", 0, 0, 0
    if not pairs:
        return
    before, last = pairs[-2] + (0,), pairs[-1] + (0,)
    own_early = own and rec
    last_k, last_q = ((("prep", "k", NG - 1, 0, 0), ("prep", "q", NG - 1, 0, 0)) if prep else (None, None))
    tail = [last_k, ("own", "ctx", 0, 0, 0) if own_early else None, ("save",) + before, ("pv",) + last,
            ("own", "out", 0, 0, 0) if own_early else None, last_q, ("flip",) + before, ("save",) + last,
            ("prep", "v", 0, 0, 0) if prep else None, ("flip",) + last]
    if own and not own_early:
        tail += [("own", "ctx", 0, 0, 0), ("own", "out", 0, 0, 0)]
    if own:
        tail += [("own", "rq", g, 0, 0) for g in range(NG)]
    yield from (event for event in tail if event)


class Counts:
    def __init__(self):
        self.base = {}
        self.n = {}
        self.mark = {}

    def add(self, key, k=1):
        self.n[key] = self.n.get(key, 0) + k

    def at(self, key):
        return self.base.get(key, 0) + self.n.get(key, 0)

    def slot(self, key, slots):
        return self.n.get(key, 0) % slots


def count_event(k, what, kind, u):
    if what == "max":
        k.add("s")
    elif what == "turn":
        k.add("st")
        k.add("turn")
    elif what == "unit":
        k.add("st")
        k.add("unit")
        k.add("unit_pair", u % 2)
    elif what in ("pv", "save", "flip"):
        k.add(what)
        if what == "flip" and kind == "rec" and u == 1:
            k.add("scaled")
    elif what == "keep":
        pass
    elif kind in ("k", "q", "rq"):
        k.add("s")
        k.add("split")
        if kind == "k":
            k.add("masked")
    elif kind == "mix":
        k.add("s")
    else:
        k.add("st")


def walk(k, kinds, body, e=0):
    own, rec, prep, fin = (name in kinds for name in ("own", "rec", "prep", "fin"))
    k.own, k.rec, k.prep, k.fin = own, rec, prep, fin
    k.mark = {"s_start": k.at("s"), "st_start": k.at("st"), "flip_start": k.at("flip")}
    for what, kind, g, u, t in step_order(own, rec, prep, fin):
        body(what, kind, g, u, t, e)
        count_event(k, what, kind, u)
    for name in ("own", "rec", "prep", "fin"):
        k.add(name, int(name in kinds))


STEADY = ("own", "rec", "prep", "fin")


def run_steps(eng, k, body):
    walk(k, ("own", "prep"), body, 0)
    walk(k, ("own", "rec", "prep"), body, 1)
    per = Counts()
    walk(per, STEADY, lambda *event: None)
    before = dict(k.n)
    with eng.Fori(0, BATCH - 3) as i:
        k.base = {key: i * n for key, n in per.n.items()}
        walk(k, STEADY, body, i + 2)
    k.base = {}
    k.n = {key: before.get(key, 0) + (BATCH - 3) * n for key, n in per.n.items()}
    walk(k, ("own", "rec", "fin"), body, BATCH - 1)
    walk(k, ("rec", "fin"), body, BATCH)
    walk(k, ("fin",), body, BATCH + 1)


def run_prologue(k, body):
    for g in range(NG):
        body("past", "k", g, 0, 0, 0)
        count_event(k, "past", "k", 0)
    body("past", "v", 0, 0, 0, 0)
    count_event(k, "past", "v", 0)
    for kind, groups in (("x", 1), ("k", NG), ("q", NG), ("v", 1)):
        for g in range(groups):
            body("prep", kind, g, 0, 0, 0)
            count_event(k, "prep", kind, 0)
    k.add("prep")


def att_tensor(pe, nc, b, s):
    bank = b.banks
    k = Counts()
    pe.sem_inc(s["pv_done"], P_SLOTS // 2)
    pe.sem_inc(s["flipped"], PV_SLOTS)
    pe.wait_ge(b.loaded["att"], 16 * b.n_loads["att"])
    pe.wait_ge(s["sel_ready"], 2)
    units = []
    tiles = [slice(P * j, P * j + P) for j in range(BT)]

    def body(what, kind, g, u, t, e):
        uses_s = what == "max" or kind in ("k", "q", "rq", "mix")
        uses_st = what in ("turn", "unit", "prep", "own", "past", "fin") and not uses_s
        if uses_s:
            pe.wait_ge(s["s_free"], k.at("s") + 1)
            out_s = bank[:, S_BANK + k.slot("s", S_SLOTS), :]
        if uses_st:
            pe.wait_ge(s["st_free"], k.at("st") + 1)
            st = ST_BANK + 2 * k.slot("st", ST_SLOTS)
        pv_bank = PV_BANK + k.slot(what, PV_SLOTS)

        if what == "max":
            if kind == "own":
                if g == 0 and u == 0 and t == 0:
                    pe.wait_ge(s["s_free"], k.mark["s_start"] + S_SLOTS - (NG if k.rec else 0))
                if u == 0 and t == 0:
                    pe.wait_ge(s["masked"], NG * k.at("prep") + g + 1)
                lhs, rhs = b.q_own[0:QK, g, tiles[t]], b.k_own[0:QK, 4 * g + 2 * u:4 * g + 2 * u + 2, :]
            else:
                if g == 0 and u == 0 and t == 0:
                    pe.wait_ge(s["s_free"], k.mark["s_start"] + S_SLOTS)
                lhs, rhs = b.q_rec[0:QK, g, tiles[t]], b.k_rec[0:QK, 4 * g + u, :]
            pe.matmul(out_s, lhs, rhs, start=True, stop=True).then_inc(s["s_full"], 1)
        elif what == "turn":
            pe.wait_ge(s["shift_cols"], k.at("turn") + 1)
            cols = b.m_own if kind == "own" else b.m_rec
            for j in range(BT):
                mm = pe.transpose(bank[:, st, tiles[j]], cols[:, j, 32 * g:32 * g + P].bitcast(F32), b.ident[:, :])
            mm.then_inc(s["st_full"], 1)
            k.mark["turn_" + kind, g] = k.at("st")
        elif what == "unit":
            if u == 0:
                pe.wait_ge(s["st_free"], k.mark["turn_" + kind, g] + 1 + ST_SLOTS)
            for n in range(4):
                h = 4 * g + 2 * (u % 2) + n // 2
                if kind == "own":
                    lhs, rhs = b.k_own[:, h, tiles[n % 2]], b.q_own[:, g, :]
                else:
                    at = SEQ * (u // 2) + P * (n % 2)
                    lhs, rhs = b.k_rec[:, h, at:at + P], b.q_rec[:, g, :]
                mm = pe.matmul(bank[:, st + n // 2, SEQ * (n % 2):SEQ * (n % 2) + SEQ], lhs, rhs,
                               start=True, stop=True)
            mm.then_inc(s["st_full"], 1)
            units.append(k.at("st"))
        elif what == "pv":
            pe.wait_ge(s["st_free"], units[1] + 1 + ST_SLOTS)
            del units[0:2]
            pe.wait_ge(s["normed"], k.at("pv") + 1)
            if kind == "own" and g == 0:
                pe.wait_ge(s["st_free"], k.mark["st_start"] + ST_SLOTS)
            first = 2 * k.n.get("pv", 0) % P_SLOTS
            for tc in range(BT):
                for j in range(4):
                    h = 4 * g + j
                    val = b.v_own[:, tc, h, :] if kind == "own" else b.v_rec[:, BT * u + tc, h, :]
                    at = ((j % 2) * BT + tc) * SEQ
                    mm = pe.matmul(bank[32 * j:32 * j + 32, pv_bank, 0:SEQ], val, b.p[:, first + j // 2, at:at + SEQ],
                                   start=tc == 0, stop=tc == BT - 1)
            mm.then_inc(s["pv_done"], 1)
        elif what == "flip":
            pe.wait_ge(s["pv_saved"], k.at("flip") + 1)
            for j in range(BT):
                mm = pe.transpose(bank[:, pv_bank, SEQ + P * j:SEQ + P * j + P],
                                  b.pvs[:, k.slot("flip", PV_SLOTS), tiles[j]], b.ident[:, :])
            mm.then_inc(s["flipped"], 1)
            k.mark["flip_" + kind] = k.at("flip")
        elif what == "past" and kind == "k":
            pe.matmul(out_s[0:QK, :], b.wrk[:, g, :], b.pastT[:, :], start=True, stop=True).then_inc(s["s_full"], 1)
        elif what == "past":
            for n in range(PAST * BT):
                out = bank[:, st, P * n:P * n + P]
                pe.matmul(out, b.pastT[:, P * n:P * n + P], b.wrv[:, :], start=True, stop=False)
                mm = pe.matmul(out, b.ones[0:1, 0:P], b.brv[0:1, :], start=False, stop=True)
            mm.then_inc(s["st_full"], 1)
        elif kind in ("k", "q", "rq"):
            if kind == "rq":
                pe.wait_ge(s["st_free"], k.mark["out"] + 1 + ST_SLOTS)
            elif kind == "k":
                pe.wait_ge(s["st_free"], k.mark["xT"] + 1 + ST_SLOTS)
            w = {"k": b.wk, "q": b.wq, "rq": b.wrq}[kind]
            rhs = b.outT[:, :] if kind == "rq" else b.xT[:, 0:SEQ]
            pe.matmul(out_s[0:QK, 0:SEQ], w[:, g, :], rhs, start=True, stop=True).then_inc(s["s_full"], 1)
        elif what == "prep" and kind == "x":
            pe.wait_ge(s["xn_ready"], k.at("prep") + 1)
            for j in range(BT):
                mm = pe.transpose(bank[:, st, tiles[j]], b.xn[:, j, :], b.ident[:, :])
            mm.then_inc(s["st_full"], 1)
            k.mark["xT"] = k.at("st")
        elif what == "prep" and kind == "v":
            for j in range(BT):
                mm = pe.matmul(bank[:, st, tiles[j]], b.xT[:, tiles[j]], b.wv[:, :], start=True, stop=True)
            mm.then_inc(s["st_full"], 1)
        elif what == "own" and kind == "ctx":
            pe.wait_ge(s["normed"], k.mark["flip_own"] + 1 + PV_SLOTS)
            for j in range(BT):
                mm = pe.transpose(bank[:, st, tiles[j]], b.ctx[:, j, :], b.ident[:, :])
            mm.then_inc(s["st_full"], 1)
            k.mark["ctx"] = k.at("st")
        elif what == "own" and kind == "out":
            pe.wait_ge(s["st_free"], k.mark["ctx"] + 1 + ST_SLOTS)
            pe.matmul(bank[:, st, 0:SEQ], b.wo[:, :], b.ctxT[:, :], start=True, stop=True).then_inc(s["st_full"], 1)
            k.mark["out"] = k.at("st")
        elif what == "fin" and kind == "ctx":
            pe.wait_ge(s["normed"], k.mark["flip_start"] + PV_SLOTS)
            for j in range(BT):
                mm = pe.transpose(bank[:, st, tiles[j]], b.rctx[:, j, :], b.ident[:, :])
            mm.then_inc(s["st_full"], 1)
            k.mark["rctx"] = k.at("st")
        elif what == "fin" and kind == "gate":
            pe.wait_ge(s["kept"], k.at("fin") + 1)
            pe.wait_ge(s["st_free"], k.mark["rctx"] + 1 + ST_SLOTS)
            pe.matmul(bank[:, st, 0:SEQ], b.wg[:, 0, :], b.out_kept[:, :], start=True, stop=False)
            pe.matmul(bank[:, st, 0:SEQ], b.wg[:, 1, :], b.rcT[:, :], start=False, stop=True).then_inc(s["st_full"], 1)
        elif what == "fin" and kind == "mix":
            pe.wait_ge(s["mix"], 3 * k.at("fin") + 3)
            pe.transpose(out_s[:, 0:P], b.mixd[:, tiles[g]], b.ident[:, :]).then_inc(s["s_full"], 1)

    run_prologue(k, body)
    run_steps(pe, k, body)


def att_scalar(act, nc, b, s):
    bank = b.banks
    stats_scalar(act, nc, b, s)
    act.sem_inc(s["st_free"], ST_SLOTS)
    k = Counts()

    def body(what, kind, g, u, t, e):
        if what in ("max", "pv", "flip", "keep") or kind == "mix":
            return
        if what == "save":
            pv_bank = PV_BANK + k.slot("save", PV_SLOTS)
            act.wait_ge(s["pv_done"], k.at("save") + 1 + P_SLOTS // 2)
            act.wait_ge(s["flipped"], k.at("save") + 1)
            nc.scalar.copy(b.pvs[:, k.slot("save", PV_SLOTS), :], bank[:, pv_bank, 0:SEQ]).then_inc(s["pv_saved"], 1)
            return
        if kind in ("k", "q", "rq"):
            act.wait_ge(s["s_full"], k.at("s") + 1)
            width = PAST * SEQ if what == "past" else SEQ
            if what == "prep" and kind == "k":
                act.wait_ge(s["masked"], k.at("masked") - NG + 1)
            dst = {"k": b.k_parts, "q": b.q_own, "rq": b.q_rec}[kind]
            bias = b.brk if what == "past" else {"k": b.bk, "q": b.bq, "rq": b.brq}[kind]
            nc.scalar.activation(dst[0:QK, g, 0:width], bank[0:QK, S_BANK + k.slot("s", S_SLOTS), 0:width],
                                 ACT.Identity, bias=bias[0:QK, g:g + 1]).then_inc(s["s_hi"], 1)
            return
        st = ST_BANK + 2 * k.slot("st", ST_SLOTS)
        act.wait_ge(s["st_full"], k.at("st") + 1)
        if what == "turn":
            q = b.q_own if kind == "own" else b.q_rec
            nc.scalar.copy(q[QK:P, g, :], bank[QK:P, st, 0:SEQ]).then_inc(s["st_free"], 1)
        elif what == "unit":
            act.wait_ge(s["pv_done"], k.at("unit_pair") + 1)
            nc.scalar.activation(b.p[:, k.slot("unit", P_SLOTS), :].rearrange("p (a n) -> p a n", a=2),
                                 bank[:, st:st + 2, :], ACT.Exp, scale=SCALE).then_inc(s["st_free"], 1)
        elif what == "past":
            nc.scalar.copy(b.v_rec[:, :, :, 0:D],
                           bank[:, st, :].rearrange("p (n h d) -> p n h d", h=NH, d=D)).then_inc(s["st_free"], 1)
        elif kind == "v":
            nc.scalar.copy(b.v_own[:, :, :, 0:D],
                           bank[:, st, 0:SEQ].rearrange("p (n h d) -> p n h d", h=NH, d=D)).then_inc(s["st_free"], 1)
        elif kind == "x":
            nc.scalar.copy(b.xT[:, 0:SEQ], bank[:, st, 0:SEQ]).then_inc(s["st_free"], 1)
        elif what == "own" and kind == "ctx":
            nc.scalar.activation(b.ctxT[:, :], bank[:, st, 0:SEQ], ACT.Identity,
                                 bias=b.bv[:, 0:1]).then_inc(s["st_free"], 1)
        elif what == "fin" and kind == "ctx":
            nc.scalar.activation(b.rcT[:, :], bank[:, st, 0:SEQ], ACT.Identity,
                                 scale=1.0 / PAST).then_inc(s["st_free"], 1)
        elif what == "fin" and kind == "gate":
            nc.scalar.activation(b.th[:, :], bank[:, st, 0:SEQ], ACT.Tanh, bias=b.bg[:, 0:1],
                                 scale=0.5).then_inc(s["st_free"], 1)
        elif what == "own" and kind == "out":
            if k.rec:
                act.wait_ge(s["kept"], k.at("rec") + 1)
            nc.scalar.activation(b.outT[:, :], bank[:, st, 0:SEQ], ACT.Identity,
                                 bias=b.bo[:, 0:1]).then_inc(s["st_free"], 1)

    act.wait_ge(s["half_bg"], 1)
    run_prologue(k, body)
    run_steps(act, k, body)


def att_gpsimd(pool, nc, b, s):
    pool.wait_ge(b.loaded["att"], 16 * b.n_loads["att"])
    pool.wait_ge(s["var"], 1)
    nc.gpsimd.tensor_copy(b.k_own[QK:P, :, :], b.sel[QK:P, 0:NH, None].to_broadcast([32, NH, SEQ])).then_inc(s["sel_ready"], 1)
    nc.gpsimd.tensor_copy(b.k_rec[QK:P, :, :].rearrange("p h (a n) -> p (h a) n", a=PAST),
                          b.sel[QK:P, NH:NH + NH * PAST, None].to_broadcast([32, NH * PAST, SEQ])).then_inc(s["sel_ready"], 1)
    k = Counts()

    def body(what, kind, g, u, t, e):
        if what == "keep":
            pool.wait_ge(s["st_free"], k.mark["st_start"] + ST_SLOTS)
            if k.fin:
                pool.wait_ge(s["mix"], 3 * k.at("fin") + 3)
            pool.sem_inc(s["passed"], 1)
            nc.gpsimd.tensor_copy(b.out_kept[:, :], b.outT[:, :]).then_inc(s["kept"], 1)
        elif kind == "k":
            pool.wait_ge(s["s_free"], k.at("s") + 1 + S_SLOTS)
            pool.sem_inc(s["passed"], 1)
            for h in range(4):
                out = b.k_rec[0:QK, 4 * g + h, :] if what == "past" else b.k_own[0:QK, 4 * g + h, :]
                width = PAST * SEQ if what == "past" else SEQ
                ins = nc.gpsimd.tensor_scalar(out, b.k_parts[0:QK, g, 0:width].bitcast(F32), b.headmask[0:QK, h:h + 1],
                                              1.0, ALU.mult, ALU.mult)
            ins.then_inc(s["masked"], 1)

    run_prologue(k, body)
    run_steps(pool, k, body)


def att_vector(v, nc, b, s, layer):
    bank = b.banks
    stats_vector(v, nc, b, s, layer)
    v.sem_inc(s["s_free"], S_SLOTS)
    v.sem_inc(s["normed"], PV_SLOTS)
    v.wait_ge(b.loaded["att"], 16 * b.n_loads["att"])
    nc.vector.tensor_scalar(b.bg[:, :], b.bg[:, :], 0.5, None, ALU.mult).then_inc(s["half_bg"], 1)
    k = Counts()

    def xn(entry):
        for j in range(BT):
            ins = normalise(nc, b, b.xn[:, j, :], bass.ds(entry * BT + j, 1))
        ins.then_inc(s["xn_ready"], 1)

    xn(0)

    def body(what, kind, g, u, t, e):
        src = bank[:, S_BANK + k.slot("s", S_SLOTS), :]
        if what == "max":
            v.wait_ge(s["s_full"], k.at("s") + 1)
            out = b.mx_own if kind == "own" else b.mx_rec
            nc.vector.reduce_max(out[:, t, 2 * u:2 * u + 2], src.rearrange("p (a n) -> p a n", a=2),
                                 AX.X).then_inc(s["s_free"], 1)
            k.mark["max_" + kind] = k.at("s")
        elif what == "turn":
            v.wait_ge(s["s_free"], k.mark["max_" + kind] + 1 + S_SLOTS)
            mx, cols = (b.mx_own, b.m_own) if kind == "own" else (b.mx_rec, b.m_rec)
            at, step = QK + 32 * g, 4 if kind == "own" else 2
            hi, lo = cols[:, :, at:at + 16:step], cols[:, :, at + 1:at + 16:step]
            nc.vector.tensor_copy(hi, mx[:, :, :]).then_inc(s["shift_hi"], 1)
            v.wait_ge(s["shift_hi"], k.at("turn") + 1)
            nc.vector.tensor_tensor(lo, mx[:, :, :], hi.bitcast(F32), ALU.subtract).then_inc(s["shift_cols"], 1)
            if k.prep and g == 0 and kind == "own":
                xn(e + 1)
        elif kind in ("k", "q", "rq"):
            v.wait_ge(s["s_hi"], k.at("split") + 1)
            width = PAST * SEQ if what == "past" else SEQ
            dst = {"k": b.k_parts, "q": b.q_own, "rq": b.q_rec}[kind]
            bias = b.brk if what == "past" else {"k": b.bk, "q": b.bq, "rq": b.brq}[kind]
            rows = slice(32, 64) if kind == "k" else slice(64, 96)
            part = dst[rows, g, 0:width]
            nc.vector.scalar_tensor_tensor(part, src[rows, 0:width], bias[rows, g:g + 1], part.bitcast(F32),
                                           ALU.add, ALU.subtract).then_inc(s["s_free"], 1)
        elif what == "flip":
            n = k.at("flip")
            slot = k.slot("flip", PV_SLOTS)
            v.wait_ge(s["flipped"], n + 1 + PV_SLOTS)
            acc = bank[:, PV_BANK + slot, SEQ:2 * SEQ].rearrange("p (j h w) -> p j h w", j=BT, w=VW)
            inv = b.inv[:, slot, :, :]
            nc.vector.reciprocal(inv[:, :, :, None], acc[:, :, :, D:D + 1]).then_inc(s["inv"], 1)
            v.wait_ge(s["inv"], n + 1)
            ctx = b.ctx if kind == "own" else b.rctx
            out = ctx[:, :, 32 * g:32 * g + 32].rearrange("p j (h d) -> p j h d", d=D)
            inv = inv[:, :, :, None].to_broadcast([P, BT, 4, D])
            if kind == "own" or u == 0:
                nc.vector.tensor_tensor(out, acc[:, :, :, 0:D], inv, ALU.mult).then_inc(s["normed"], 1)
            else:
                nc.vector.tensor_tensor(b.rec_tmp[:, :, :, :], acc[:, :, :, 0:D], inv, ALU.mult).then_inc(s["scaled"], 1)
                v.wait_ge(s["scaled"], k.at("scaled") + 1)
                nc.vector.tensor_tensor(out, out, b.rec_tmp[:, :, :, :], ALU.add).then_inc(s["normed"], 1)
        elif what == "fin" and kind == "ctx":
            k.mark["rcT"] = k.at("st")
        elif what == "fin" and kind == "gate":
            n = 3 * k.at("fin")
            v.wait_ge(s["kept"], k.at("fin") + 1)
            v.wait_ge(s["st_free"], k.mark["rcT"] + 1 + ST_SLOTS)
            nc.vector.tensor_tensor(b.mixd[:, :], b.rcT[:, :], b.out_kept[:, :], ALU.subtract).then_inc(s["mix"], 1)
            v.wait_ge(s["mix"], n + 1)
            v.wait_ge(s["st_free"], k.at("st") + 1 + ST_SLOTS)
            nc.vector.scalar_tensor_tensor(b.mixd[:, :], b.th[:, :], 1.0, b.mixd[:, :],
                                           ALU.add, ALU.mult).then_inc(s["mix"], 1)
            v.wait_ge(s["mix"], n + 2)
            nc.vector.scalar_tensor_tensor(b.mixd[:, :], b.mixd[:, :], 0.5, b.out_kept[:, :],
                                           ALU.mult, ALU.add).then_inc(s["mix"], 1)
        elif what == "fin" and kind == "mix":
            v.wait_ge(s["s_full"], k.at("s") + 1)
            tile = (e - 2) * BT + g
            xs = b.x[:, bass.ds(tile, 1), :]
            nc.vector.tensor_tensor(xs, xs, src[:, None, 0:P], ALU.add).then_inc(s["s_free"], 1)
            v.wait_ge(s["s_free"], k.at("s") + 1 + S_SLOTS)
            nc.vector.bn_stats(b.bn[:, bass.ds(tile, 1), :], xs).then_inc(b.bn_done, 1)

    run_prologue(k, body)
    run_steps(v, k, body)


def macaron(nc, a, out):
    with ExitStack() as ctx:
        def sb(name, shape, dt=F32):
            return ctx.enter_context(nc.sbuf_tensor(name, shape, dt))

        def sems(prefix, names):
            return {n: ctx.enter_context(nc.semaphore(f"{prefix}_{n}")) for n in names}

        b = Buffers()
        b.banks = ctx.enter_context(nc.psum_tensor("banks", [P, 8, 512], F32))
        x = sb("x", [P, T])
        b.x = x[:, :].rearrange("p (t f) -> p t f", f=C)
        b.xc = x[:, :].rearrange("p (c n) -> p c n", n=CH)
        b.xb = x[:, :].rearrange("p (c n) -> p c n", n=SEQ)
        b.xn = sb("xn", [P, CT, C])
        b.xT = sb("xT", [P, CH])
        b.bn = sb("bn", [P, TILES, 6])
        b.ln = sb("ln", [P, 6, TILES])
        b.ident = sb("ident", [P, P])
        b.ones = sb("ones", [1, P])
        parts = sb("parts", [P, 4 * HB * CH], F32R)
        quarter = [parts[:, HB * CH * n:HB * CH * (n + 1)].rearrange("p (k n) -> p k n", n=CH) for n in range(4)]
        b.h_hi, b.h_lo, b.g_hi, b.g_lo = quarter
        b.k_own = parts[:, 0:NH * SEQ].rearrange("p (h n) -> p h n", n=SEQ)
        wide = sb("wide", [P, 2 * T], F32R)
        b.xh_all, b.xl_all = wide[:, 0:T], wide[:, T:2 * T]
        b.k_rec = wide[:, 0:NH * PAST * SEQ].rearrange("p (h n) -> p h n", n=PAST * SEQ)
        b.y = sb("y", [P, CH])
        b.xh = sb("xh", [P, CH], F32R)
        b.xl = sb("xl", [P, CH], F32R)
        b.k0u = sb("k0u", [P, 2, 512], U8)
        b.k1u = sb("k1u", [P, HB, 512], U8)
        b.k2u = sb("k2u", [P, HB, C], U8)
        b.k0f = b.y
        b.k0 = sb("k0", [P, 512], F32R)
        b.k1 = sb("k1", [P, HB, 512], F32R)
        b.k2 = sb("k2", [P, HB, C], F32R)
        b.sc = sb("sc", [P, 16])
        b.ffn_scale = b.sc[:, 15:16]
        b.wq0 = sb("wq0", [P, C])
        b.wkv0 = sb("wkv0", [P, 2 * C])
        b.wp0 = sb("wp0", [P, C])
        b.pb0 = sb("pb0", [1, C])
        b.blockmask = sb("blockmask", [P, 2 * C])
        work = sb("work", [P, P_SLOTS * 4 * SEQ])
        b.h_raw = work[:, P_SLOTS * 4 * SEQ - HB * CH:].rearrange("p (k n) -> p k n", n=CH)
        b.kv = work[:, 0:3 * CH].rearrange("p (t n) -> p t n", t=CT)
        b.kvm = work[:, 3 * CH:4 * CH].rearrange("p (e n) -> p e n", e=2)
        b.rec, b.ratio, b.qT = (work[:, n * CH:(n + 1) * CH] for n in (4, 5, 6))
        b.wr = sb("wr", [P, NE])
        b.br = sb("br", [1, NE])
        b.b1 = sb("b1", [P, NE * HB])
        b.b2 = sb("b2", [P, NE])
        b.iota8 = sb("iota8", [P, NE])
        b.w1_raw = sb("w1_raw", [P, 512])
        b.w2_raw = sb("w2_raw", [P, HB, C])
        b.w1h, b.w1l, b.w2h, b.w2l = (sb(n, [P, 2, 512], F32R) for n in ("w1h", "w1l", "w2h", "w2l"))
        b.lg = sb("lg", [P, CT, NE])
        b.top = sb("top", [P, CT, 8])
        b.idx = sb("idx", [P, CT, 8], U32)
        b.idxf = sb("idxf", [P, CT, 2])
        b.rt = sb("rt", [P, 4, CT])
        b.oh = sb("oh", [P, 2, CT, NE])
        b.wfe = sb("wfe", [P, TILES * NE])
        b.wf = b.wfe[:, :].rearrange("p (t e) -> p t e", e=NE)
        b.wq, b.wk, b.wrq, b.wrk = (sb(n, [P, NG, QK]) for n in ("wq", "wk", "wrq", "wrk"))
        b.bq, b.bk, b.brq, b.brk = (sb(n, [QK, NG]) for n in ("bq", "bk", "brq", "brk"))
        b.wv, b.wrv, b.wo = (sb(n, [P, C]) for n in ("wv", "wrv", "wo"))
        b.wg = sb("wg", [P, 2, C])
        b.brv = sb("brv", [1, C])
        b.bv, b.bo, b.bg = (sb(n, [P, 1]) for n in ("bv", "bo", "bg"))
        b.pastT = sb("pastT", [P, PAST * SEQ])
        b.headmask = sb("headmask", [QK, 4])
        b.sel = sb("sel", [P, NH + NH * PAST])
        b.q_own, b.q_rec = (sb(n, [P, NG, SEQ], F32R) for n in ("q_own", "q_rec"))
        b.k_parts = sb("k_parts", [QK, NG, PAST * SEQ], F32R)
        b.m_own, b.m_rec = (sb(n, [P, BT, QK + P], F32R) for n in ("m_own", "m_rec"))
        b.mx_own = sb("mx_own", [P, BT, 4])
        b.mx_rec = sb("mx_rec", [P, BT, 8])
        b.p = work[:, :].rearrange("p (k n) -> p k n", k=P_SLOTS)
        b.v_own = sb("v_own", [P, BT, NH, VW])
        b.v_rec = sb("v_rec", [P, PAST * BT, NH, VW])
        b.pvs = sb("pvs", [P, 2, SEQ])
        b.inv = sb("inv", [P, 2, BT, 4])
        b.rec_tmp = sb("rec_tmp", [P, BT, 4, D])
        b.ctx, b.rctx = sb("ctx", [P, BT, C]), sb("rctx", [P, BT, C])
        b.outT, b.out_kept = (sb(n, [P, SEQ]) for n in ("outT", "out_kept"))
        b.th, b.mixd, b.ctxT = b.y[:, 0:SEQ], b.y[:, SEQ:2 * SEQ], b.xT[:, SEQ:2 * SEQ]
        b.rcT = b.xn[:, BT:2 * BT, :].rearrange("p j f -> p (j f)")

        loads = {
            "ffn": [(b.k0u[:, :, :], a["L0_ffn_k0"].rearrange("(h p) n -> p h n", p=P)),
                    (b.k1u[:, :, :], a["L0_ffn_k1"].rearrange("(k p) n -> p k n", p=P)),
                    (b.k2u[:, :, :], a["L0_ffn_k2"].rearrange("(k p) n -> p k n", p=P)),
                    (b.sc[:, 0:3], a["s_cols"]), (b.ident[:, :], a["ident"])],
            "lin": [(b.wq0[:, :], a["wqkv0_t"][:, 0:C]), (b.wkv0[:, :], a["wqkv0_t"][:, C:3 * C]),
                    (b.wp0[:, :], a["wproj0_t"]), (b.pb0[:, :], a["L0_attn_proj_bias"].rearrange("(o f) -> o f", o=1)),
                    (b.blockmask[:, :], a["blockmask"])],
            "moe": [(b.wr[:, :], a["L1_ffn_Wr"]), (b.br[:, :], a["L1_ffn_br"].rearrange("(o f) -> o f", o=1)),
                    (b.b1[:, :], a["b1_t"]), (b.b2[:, :], a["b2_t"]), (b.iota8[:, :], a["iota8"])],
            "att": [(b.wq[:, :, :], a["wq_rep"]), (b.wk[:, :, :], a["wk_rep"]), (b.wrq[:, :, :], a["wrq_rep"]),
                    (b.wrk[:, :, :], a["wrk_rep"]), (b.bq[:, :], a["bq_rep"]), (b.bk[:, :], a["bk_rep"]),
                    (b.brq[:, :], a["brq_rep"]), (b.brk[:, :], a["brk_rep"]),
                    (b.wv[:, :], a["L1_attn_Wv"]), (b.wrv[:, :], a["L1_attn_Wrv"]), (b.wo[:, :], a["L1_attn_Wo"]),
                    (b.wg[:, :, :], a["L1_attn_Wg"].rearrange("(h p) n -> p h n", p=P)),
                    (b.brv[:, :], a["L1_attn_brv"].rearrange("(o f) -> o f", o=1)),
                    (b.pastT[:, :], a["past_t"]), (b.headmask[:, :], a["headmask"]),
                    (b.sel[QK:P, :], a["sel"])]
                   + [(dst[:, :], a[n].rearrange("(p o) -> p o", o=1)) for dst, n in
                      ((b.bv, "L1_attn_bv"), (b.bo, "L1_attn_bo"), (b.bg, "L1_attn_bg"))],
        }
        b.n_loads = {name: len(group) for name, group in loads.items()}
        b.loaded = sems("loaded", loads)
        b.W1, b.W2 = a["L1_ffn_W1"], a["L1_ffn_W2"]
        x_in = [ctx.enter_context(nc.semaphore(f"x_in{c}")) for c in range(NCH)]
        b.bn_done = ctx.enter_context(nc.semaphore("bn_done"))
        x_out = ctx.enter_context(nc.semaphore("x_out"))
        setup = sems("setup", ["signs", "abs", "diff", "weights", "fills"])
        layer_sems = [sems("ffn_a", FFN_SEMS), sems("lin", LIN_SEMS), sems("ffn_b", FFN_SEMS),
                      sems("moe_a", MOE_SEMS), sems("att", ATT_SEMS), sems("moe_b", MOE_SEMS)]
        ffn_a, lin, ffn_b, moe_a, att, moe_b = layer_sems
        block = ctx.enter_context(nc.Block())
        x_dram = a["L0_attn_x"].rearrange("e (j p) f -> p (e j) f", p=P)
        out_dram = out.rearrange("e (j p) f -> p (e j) f", p=P)

        @block.sync
        def _(sp):
            for c in range(NCH):
                sp.dma_start(b.x[:, CT * c:CT * c + CT, :], x_dram[:, CT * c:CT * c + CT, :]).then_inc(x_in[c], 16)
            for name in ("lin", "moe", "att"):
                for dst, src in loads[name]:
                    sp.dma_start(dst, src).then_inc(b.loaded[name], 16)
            moe_sync(sp, nc, b, moe_a)
            sp.wait_ge(moe_a["weights_split"], 2 * NE + 2)
            moe_sync(sp, nc, b, moe_b)
            sp.wait_ge(moe_b["x_added"], NE * NCH + 1)
            for c in range(NCH):
                sp.dma_start(out_dram[:, CT * c:CT * c + CT, :], b.x[:, CT * c:CT * c + CT, :]).then_inc(x_out, 16)
            sp.wait_ge(x_out, 16 * NCH)

        @block.scalar
        def _(act):
            for dst, src in loads["ffn"]:
                act.dma_start(dst, src).then_inc(b.loaded["ffn"], 16)
            ffn_scalar(act, nc, b, ffn_a)
            lin_scalar(act, nc, b, lin)
            ffn_scalar(act, nc, b, ffn_b)
            act.wait_ge(b.loaded["moe"], 16 * b.n_loads["moe"])
            moe_scalar(act, nc, b, moe_a)
            act.wait_ge(b.loaded["att"], 16 * b.n_loads["att"])
            att_scalar(act, nc, b, att)
            moe_scalar(act, nc, b, moe_b)

        @block.gpsimd
        def _(pool):
            nc.gpsimd.memset(b.ones[:, :], 1.0).then_inc(setup["fills"], 1)
            nc.gpsimd.memset(b.kv[:, :, 2 * C:3 * C], 1.0).then_inc(setup["fills"], 1)
            nc.gpsimd.memset(b.v_own[:, :, :, D:D + 1], 1.0).then_inc(setup["fills"], 1)
            nc.gpsimd.memset(b.v_rec[:, :, :, D:D + 1], 1.0).then_inc(setup["fills"], 1)
            nc.gpsimd.memset(b.v_own[:, :, :, D + 1:VW], 0.0).then_inc(setup["fills"], 1)
            nc.gpsimd.memset(b.v_rec[:, :, :, D + 1:VW], 0.0).then_inc(setup["fills"], 1)
            nc.gpsimd.memset(b.m_own[:, :, :].bitcast(F32), 0.0).then_inc(setup["fills"], 1)
            nc.gpsimd.memset(b.m_rec[:, :, :].bitcast(F32), 0.0).then_inc(setup["fills"], 1)
            moe_gpsimd(pool, nc, b, moe_a)
            att_gpsimd(pool, nc, b, att)
            pool.wait_ge(moe_b["var"], 1)
            moe_gpsimd(pool, nc, b, moe_b)

        @block.tensor
        def _(pe):
            pe.wait_ge(b.loaded["ffn"], 16 * b.n_loads["ffn"])
            pe.wait_ge(setup["weights"], 3)
            ffn_tensor(pe, nc, b, ffn_a)
            pe.wait_ge(b.loaded["lin"], 16 * b.n_loads["lin"])
            pe.wait_ge(setup["fills"], 8)
            lin_tensor(pe, nc, b, lin)
            ffn_tensor(pe, nc, b, ffn_b)
            pe.wait_ge(b.loaded["moe"], 16 * b.n_loads["moe"])
            moe_tensor(pe, nc, b, moe_a)
            att_tensor(pe, nc, b, att)
            moe_tensor(pe, nc, b, moe_b)

        @block.vector
        def _(v):
            v.wait_ge(b.loaded["ffn"], 16 * b.n_loads["ffn"])
            pos, neg, sign, twice, minus = (b.sc[:, n:n + 2] for n in (3, 5, 7, 9, 11))
            s01 = b.sc[:, 0:2]
            nc.vector.tensor_scalar(pos, s01, 0.0, None, ALU.is_gt).then_inc(setup["signs"], 1)
            nc.vector.tensor_scalar(neg, s01, 0.0, None, ALU.is_lt).then_inc(setup["signs"], 1)
            v.wait_ge(setup["signs"], 2)
            nc.vector.tensor_tensor(sign, pos, neg, ALU.subtract).then_inc(setup["signs"], 1)
            v.wait_ge(setup["signs"], 3)
            nc.vector.tensor_scalar(twice, sign, 2.0, None, ALU.mult).then_inc(setup["signs"], 1)
            nc.vector.tensor_scalar(minus, sign, -1.0, None, ALU.mult).then_inc(setup["signs"], 1)
            nc.vector.tensor_tensor(b.sc[:, 13:15], s01, sign, ALU.mult).then_inc(setup["abs"], 1)
            nc.vector.tensor_tensor(b.k0f[:, :], b.k0u[:, 0, :], b.k0u[:, 1, :], ALU.subtract).then_inc(setup["diff"], 1)
            v.wait_ge(setup["signs"], 5)
            v.wait_ge(setup["abs"], 1)
            nc.vector.scalar_tensor_tensor(b.sc[:, 13:14], b.sc[:, 13:14], 2.0, b.sc[:, 14:15],
                                           ALU.mult, ALU.mult).then_inc(setup["abs"], 1)
            v.wait_ge(setup["abs"], 2)
            nc.vector.tensor_tensor(b.ffn_scale, b.sc[:, 13:14], b.sc[:, 2:3], ALU.mult).then_inc(setup["abs"], 1)
            v.wait_ge(setup["diff"], 1)
            nc.vector.tensor_scalar(b.k0[:, :], b.k0f[:, :], twice[:, 0:1], None, ALU.mult).then_inc(setup["weights"], 1)
            nc.vector.tensor_scalar(b.k1[:, :, :], b.k1u[:, :, :], twice[:, 1:2], minus[:, 1:2],
                                    ALU.mult, ALU.add).then_inc(setup["weights"], 1)
            nc.vector.tensor_scalar(b.k2[:, :, :], b.k2u[:, :, :], 2.0, -1.0, ALU.mult, ALU.add).then_inc(setup["weights"], 1)
            v.wait_ge(setup["abs"], 3)
            for c in range(NCH):
                v.wait_ge(x_in[c], 16)
                for t in range(CT * c, CT * c + CT):
                    nc.vector.bn_stats(b.bn[:, t, :], b.x[:, t, :]).then_inc(b.bn_done, 1)
            ffn_vector(v, nc, b, ffn_a, 0)
            v.wait_ge(b.loaded["lin"], 16 * b.n_loads["lin"])
            lin_vector(v, nc, b, lin, 1)
            ffn_vector(v, nc, b, ffn_b, 2)
            v.wait_ge(b.loaded["moe"], 16 * b.n_loads["moe"])
            moe_vector(v, nc, b, moe_a, 3)
            v.wait_ge(setup["fills"], 8)
            att_vector(v, nc, b, att, 4)
            moe_vector(v, nc, b, moe_b, 5)


def kernel(**inputs):
    import numpy as np
    import concourse.bacc as bacc
    from concourse.bass_utils import run_bass_kernel_spmd

    def grouped(w):
        w = np.asarray(w).reshape(C, NG, 32)
        return np.concatenate([w, w, w], axis=2)

    def grouped_bias(v):
        v = np.asarray(v).reshape(NG, 32).T
        return np.concatenate([v, v, v], axis=0)

    given = {n: np.asarray(v) for n, v in inputs.items()}
    arrays = {n: given[n] for n in (
        "L0_attn_x", "L0_attn_proj_bias", "L0_ffn_k0", "L0_ffn_k1", "L0_ffn_k2", "L1_attn_Wv", "L1_attn_bv",
        "L1_attn_Wo", "L1_attn_bo", "L1_attn_Wrv", "L1_attn_brv", "L1_attn_Wg", "L1_attn_bg", "L1_ffn_Wr",
        "L1_ffn_br", "L1_ffn_W1", "L1_ffn_W2")}
    arrays["wqkv0_t"] = given["L0_attn_qkv_weight"].T
    arrays["wproj0_t"] = given["L0_attn_proj_weight"].T
    arrays["s_cols"] = np.tile(np.stack([given["L0_ffn_s0"], given["L0_ffn_s1"], given["L0_ffn_s2"]]).reshape(1, 3), (P, 1))
    arrays["b1_t"] = given["L1_ffn_b1"].reshape(NE * HB, P).T
    arrays["b2_t"] = given["L1_ffn_b2"].T
    arrays["past_t"] = given["L1_attn_past_states"].reshape(PAST * SEQ, C).T
    for name, w, bias in (("q", "Wq", "bq"), ("k", "Wk", "bk"), ("rq", "Wrq", "brq"), ("rk", "Wrk", "brk")):
        arrays[f"w{name}_rep"] = grouped(given["L1_attn_" + w])
        arrays[f"b{name}_rep"] = grouped_bias(given["L1_attn_" + bias])
    f = np.arange(P)
    arrays["ident"] = np.eye(P, dtype=np.float32)
    mask = (f[:, None] // 4 == f[None, :] // 4).astype(np.float32)
    arrays["blockmask"] = np.concatenate([mask, mask], axis=1)
    arrays["iota8"] = np.tile(np.arange(NE, dtype=np.float32), (P, 1))
    arrays["headmask"] = (f[:QK, None] % 32 // D == np.arange(4)[None, :]).astype(np.float32)
    sel = np.zeros((32, NH + NH * PAST), np.float32)
    for h in range(NH):
        for a in range(PAST):
            rows = slice(4 * (h % 4) + 2 * a, 4 * (h % 4) + 2 * a + 2)
            if a == 0:
                sel[rows, h] = -1.0
            sel[rows, NH + h * PAST + a] = -1.0
    arrays["sel"] = sel

    nc = bacc.Bacc("TRN2", target_bir_lowering=False, num_devices=1)
    feed, args = {}, {}
    for name, arr in arrays.items():
        arr = np.ascontiguousarray(arr)
        feed[f"in_{name}"] = arr
        args[name] = nc.dram_tensor(f"in_{name}", arr.shape, mybir.dt.from_np(arr.dtype), kind="ExternalInput").ap()
    out = nc.dram_tensor("out_x", (BATCH, SEQ, C), F32, kind="ExternalOutput").ap()
    macaron(nc, args, out)
    result = run_bass_kernel_spmd(nc, [feed], core_ids=[0])
    return result.results[0]["out_x"]
```

```python
from contextlib import ExitStack

import concourse.bass as bass
from concourse import mybir

F32 = mybir.dt.float32
F32R = mybir.dt.float32r
U8 = mybir.dt.uint8
U32 = mybir.dt.uint32
ALU = mybir.AluOpType
ACT = mybir.ActivationFunctionType
AX = mybir.AxisListType

P = 128
BATCH, SEQ, C = 16, 256, 128
T = BATCH * SEQ
TILES = T // P
CT = 4
CH = CT * P
NCH = T // CH
HB = 4
LN_EPS = 1e-5
LIN_EPS = 1e-15
NE = 8
NH = 16
D = C // NH
NG = 4
PAST = 2
SCALE = float(1.0 / (D ** 0.5))
BT = SEQ // P
VW = 32


class Buffers:
    pass


def stats_vector(v, nc, b, s, layer):
    done = s["stats"]
    n = 0
    mean, diff, var, sd, r, t = (b.ln[:, k, :] for k in range(6))
    even, odd = b.bn[:, :, 0:3], b.bn[:, :, 3:6]
    v.wait_ge(b.bn_done, TILES * (layer + 1))
    nc.vector.tensor_tensor(mean, even[:, :, 1], odd[:, :, 1], ALU.add).then_inc(done, 1)
    nc.vector.tensor_tensor(diff, even[:, :, 1], odd[:, :, 1], ALU.subtract).then_inc(done, 1)
    nc.vector.tensor_tensor(var, even[:, :, 2], odd[:, :, 2], ALU.add).then_inc(done, 1)
    v.wait_ge(done, 3)
    nc.vector.tensor_scalar(mean, mean, 0.5, None, ALU.mult).then_inc(done, 1)
    nc.vector.tensor_tensor(diff, diff, diff, ALU.mult).then_inc(done, 1)
    nc.vector.tensor_scalar(var, var, 1.0 / C, LN_EPS, ALU.mult, ALU.add).then_inc(done, 1)
    v.wait_ge(done, 6)
    nc.vector.scalar_tensor_tensor(var, diff, 0.25, var, ALU.mult, ALU.add).then_inc(s["var"], 1)
    v.wait_ge(s["sd"], 1)
    nc.vector.reciprocal(r, sd).then_inc(done, 1)
    v.wait_ge(done, 7)
    nc.vector.tensor_tensor(t, r, r, ALU.mult).then_inc(done, 1)
    v.wait_ge(done, 8)
    nc.vector.tensor_tensor(t, t, var, ALU.mult).then_inc(done, 1)
    v.wait_ge(done, 9)
    nc.vector.tensor_scalar(t, t, -0.5, 1.5, ALU.mult, ALU.add).then_inc(done, 1)
    v.wait_ge(done, 10)
    nc.vector.tensor_tensor(r, r, t, ALU.mult).then_inc(done, 1)
    v.wait_ge(done, 11)


def stats_scalar(act, nc, b, s, layer):
    nc.scalar.activation(b.warm[0:1, layer:layer + 1], b.ident[0:1, 0:1], ACT.Sqrt)
    act.wait_ge(s["var"], 1)
    nc.scalar.activation(b.ln[:, 3, :], b.ln[:, 2, :], ACT.Sqrt).then_inc(s["sd"], 1)


def normalise(nc, b, out, tile):
    return nc.vector.tensor_scalar(out, b.x[:, tile, :], b.ln[:, 0, tile], b.ln[:, 4, tile],
                                   ALU.subtract, ALU.mult)


STATS_SEMS = ["stats", "var", "sd"]


FFN_SEMS = STATS_SEMS + ["xn_ready", "xt_full", "x_hi", "x_split", "z_full", "z_hi", "z_split", "y_full",
                         "y_copied", "yt_full", "x_added"]
FFN_XT, FFN_Y, FFN_YT = 4, 5, 6


def ffn_tensor(pe, nc, b, s):
    bank = b.banks

    def turn_x(c):
        pe.wait_ge(s["xn_ready"], c + 1)
        if not (isinstance(c, int) and c == 0):
            pe.wait_ge(s["x_split"], c)
        for j in range(CT):
            mm = pe.transpose(bank[:, FFN_XT, P * j:P * j + P], b.xn[:, j, :], b.ident[:, :])
        mm.then_inc(s["xt_full"], 1)

    def first(c):
        pe.wait_ge(s["x_split"], c + 1)
        for m in range(HB):
            if not (isinstance(c, int) and c == 0):
                pe.wait_ge(s["z_split"], 8 * c + m - 3)
            w = b.k0[:, P * m:P * m + P]
            pe.matmul(bank[:, m, :], w, b.xh[:, :], start=True, stop=False)
            pe.matmul(bank[:, m, :], w, b.xl[:, :], start=False, stop=True).then_inc(s["z_full"], 1)

    def middle(c, m):
        for k in range(HB):
            if m == 0:
                pe.wait_ge(s["z_split"], 8 * c + k + 1)
            w = b.k1[:, k, P * m:P * m + P]
            pe.matmul(bank[:, m, :], w, b.h_hi[:, k, :], start=k == 0, stop=False)
            mm = pe.matmul(bank[:, m, :], w, b.h_lo[:, k, :], start=False, stop=k == HB - 1)
        mm.then_inc(s["z_full"], 1)

    def last(c):
        pe.wait_ge(s["y_copied"], c + 1)
        for k in range(HB):
            pe.wait_ge(s["z_split"], 8 * c + 5 + k)
            pe.matmul(bank[:, FFN_Y, :], b.k2[:, k, :], b.g_hi[:, k, :], start=k == 0, stop=False)
            mm = pe.matmul(bank[:, FFN_Y, :], b.k2[:, k, :], b.g_lo[:, k, :], start=False, stop=k == HB - 1)
        mm.then_inc(s["y_full"], 1)

    def turn_y(c):
        pe.wait_ge(s["y_copied"], c + 2)
        pe.wait_ge(s["x_added"], c + 1)
        for j in range(CT):
            mm = pe.transpose(bank[:, FFN_YT, P * j:P * j + P], b.y[:, P * j:P * j + P], b.ident[:, :])
        mm.then_inc(s["yt_full"], 1)

    turn_x(0)
    first(0)
    pe.wait_ge(b.weights_ready, 3)
    for m in range(HB - 1):
        middle(0, m)
    turn_x(1)
    middle(0, HB - 1)
    first(1)
    with pe.Fori(0, NCH - 2) as i:
        last(i)
        middle(i + 1, 0)
        turn_y(i)
        for m in range(1, HB - 1):
            middle(i + 1, m)
        turn_x(i + 2)
        middle(i + 1, HB - 1)
        first(i + 2)
    last(NCH - 2)
    middle(NCH - 1, 0)
    turn_y(NCH - 2)
    for m in range(1, HB):
        middle(NCH - 1, m)
    last(NCH - 1)
    turn_y(NCH - 1)


def ffn_scalar(act, nc, b, s, layer):
    bank = b.banks
    stats_scalar(act, nc, b, s, layer)
    act.sem_inc(s["y_copied"], 1)

    def x_hi(c):
        act.wait_ge(s["xt_full"], c + 1)
        nc.scalar.copy(b.xh[:, :], bank[:, FFN_XT, :]).then_inc(s["x_hi"], 1)

    def relu(n, m, out):
        act.wait_ge(s["z_full"], n + 1)
        nc.scalar.activation(out[:, m, :], bank[:, m, :], ACT.Relu).then_inc(s["z_hi"], 1)

    def y_copy(c):
        act.wait_ge(s["y_full"], c + 1)
        nc.scalar.activation(b.y[:, :], bank[:, FFN_Y, :], ACT.Identity,
                             scale=b.ffn_scale[:, 0:1]).then_inc(s["y_copied"], 1)

    x_hi(0)
    for m in range(HB):
        relu(m, m, b.h_hi)
    for m in range(HB - 1):
        relu(HB + m, m, b.g_hi)
    x_hi(1)
    relu(2 * HB - 1, HB - 1, b.g_hi)
    for m in range(HB):
        relu(8 + m, m, b.h_hi)
    with act.Fori(0, NCH - 2) as i:
        y_copy(i)
        for m in range(HB - 1):
            relu(8 * i + 12 + m, m, b.g_hi)
        x_hi(i + 2)
        relu(8 * i + 15, HB - 1, b.g_hi)
        for m in range(HB):
            relu(8 * i + 16 + m, m, b.h_hi)
    y_copy(NCH - 2)
    for m in range(HB):
        relu(8 * (NCH - 1) + 4 + m, m, b.g_hi)
    y_copy(NCH - 1)


def ffn_vector(v, nc, b, s, layer):
    bank = b.banks
    stats_vector(v, nc, b, s, layer)
    v.sem_inc(s["x_added"], 1)

    def xn(c):
        if not (isinstance(c, int) and c == 0):
            v.wait_ge(s["xt_full"], c)
        for j in range(CT):
            ins = normalise(nc, b, b.xn[:, j, :], bass.ds(c * CT + j, 1))
        ins.then_inc(s["xn_ready"], 1)

    def x_lo(c):
        v.wait_ge(s["x_hi"], c + 1)
        nc.vector.tensor_tensor(b.xl[:, :], bank[:, FFN_XT, :], b.xh[:, :].bitcast(F32),
                                ALU.subtract).then_inc(s["x_split"], 1)

    def relu_lo(n, m, hi, lo):
        v.wait_ge(s["z_hi"], n + 1)
        nc.vector.scalar_tensor_tensor(lo[:, m, :], bank[:, m, :], 0.0, hi[:, m, :].bitcast(F32),
                                       ALU.max, ALU.subtract).then_inc(s["z_split"], 1)

    def add(c):
        v.wait_ge(s["yt_full"], c + 1)
        xs = b.xc[:, bass.ds(c, 1), :]
        nc.vector.tensor_tensor(xs, xs, bank[:, FFN_YT:FFN_YT + 1, :], ALU.add).then_inc(s["x_added"], 1)
        v.wait_ge(s["x_added"], c + 2)
        for j in range(CT):
            nc.vector.bn_stats(b.bn[:, bass.ds(c * CT + j, 1), :], b.x[:, bass.ds(c * CT + j, 1), :]).then_inc(b.bn_done, 1)

    xn(0)
    x_lo(0)
    for m in range(HB):
        relu_lo(m, m, b.h_hi, b.h_lo)
    xn(1)
    for m in range(HB - 1):
        relu_lo(HB + m, m, b.g_hi, b.g_lo)
    x_lo(1)
    relu_lo(2 * HB - 1, HB - 1, b.g_hi, b.g_lo)
    for m in range(HB):
        relu_lo(8 + m, m, b.h_hi, b.h_lo)
    with v.Fori(0, NCH - 2) as i:
        xn(i + 2)
        relu_lo(8 * i + 12, 0, b.g_hi, b.g_lo)
        add(i)
        for m in range(1, HB - 1):
            relu_lo(8 * i + 12 + m, m, b.g_hi, b.g_lo)
        x_lo(i + 2)
        relu_lo(8 * i + 15, HB - 1, b.g_hi, b.g_lo)
        for m in range(HB):
            relu_lo(8 * i + 16 + m, m, b.h_hi, b.h_lo)
    relu_lo(8 * NCH - 4, 0, b.g_hi, b.g_lo)
    add(NCH - 2)
    for m in range(1, HB):
        relu_lo(8 * NCH - 4 + m, m, b.g_hi, b.g_lo)
    add(NCH - 1)


LIN_SEMS = STATS_SEMS + ["xn_ready", "xt_full", "xt_ready", "q_full", "q_ready", "kv_full", "kv_ready",
                         "sum_full", "sum_ready", "ratio_full", "den", "inv", "ratio_ready", "y_full", "biased",
                         "x_added"]
LIN_XT, LIN_Q, LIN_KV, LIN_SUM, LIN_NUM = 0, 1, 2, 4, 6


def lin_tensor(pe, nc, b, s):
    bank = b.banks

    def turn_x(c):
        pe.wait_ge(s["xn_ready"], c + 1)
        if not (isinstance(c, int) and c == 0):
            pe.wait_ge(s["x_added"], c)
        for j in range(CT):
            mm = pe.transpose(bank[:, LIN_XT, P * j:P * j + P], b.xn[:, j, :], b.ident[:, :])
        mm.then_inc(s["xt_full"], 1)

    def keys_values(c):
        pe.wait_ge(s["xt_ready"], c + 1)
        for half in range(2):
            for j in range(2):
                t = 2 * half + j
                mm = pe.matmul(bank[:, LIN_KV + half, 256 * j:256 * j + 256], b.xT[:, P * t:P * t + P],
                               b.wkv0[:, :], start=True, stop=True)
            mm.then_inc(s["kv_full"], 1)

    def queries():
        pe.matmul(bank[:, LIN_Q, :], b.wq0[:, :], b.xT[:, :], start=True, stop=True).then_inc(s["q_full"], 1)

    def sums(c):
        for e in range(2):
            pe.wait_ge(s["kv_ready"], 2 * c + e + 1)
            for j in range(2):
                t = 2 * e + j
                mm = pe.matmul(bank[:, LIN_SUM + e, 0:256], b.kv[:, t, 0:P], b.kv[:, t, P:3 * P],
                               start=j == 0, stop=j == 1)
            mm.then_inc(s["sum_full"], 1)

    def attend(c):
        pe.wait_ge(s["q_ready"], c + 1)
        for e in range(2):
            pe.wait_ge(s["sum_ready"], 2 * c + e + 1)
            rhs = b.qT[:, SEQ * e:SEQ * e + SEQ]
            pe.matmul(bank[:, LIN_NUM + e, SEQ:2 * SEQ], b.kvm[:, e, P:2 * P], rhs, start=True, stop=True)
            mm = pe.matmul(bank[:, LIN_NUM + e, 0:SEQ], b.kvm[:, e, 0:P], rhs, start=True, stop=True)
        mm.then_inc(s["ratio_full"], 1)

    def project(c):
        pe.wait_ge(s["ratio_ready"], c + 1)
        for t in range(CT):
            mm = pe.matmul(bank[:, LIN_XT, P * t:P * t + P], b.ratio[:, P * t:P * t + P], b.wp0[:, :],
                           start=True, stop=True)
        mm.then_inc(s["y_full"], 1)

    turn_x(0)
    keys_values(0)
    queries()
    turn_x(1)
    sums(0)
    keys_values(1)
    attend(0)
    queries()
    with pe.Fori(1, NCH - 1) as c:
        turn_x(c + 1)
        sums(c)
        keys_values(c + 1)
        project(c - 1)
        attend(c)
        queries()
    sums(NCH - 1)
    project(NCH - 2)
    attend(NCH - 1)
    project(NCH - 1)


def lin_scalar(act, nc, b, s, layer):
    bank = b.banks
    stats_scalar(act, nc, b, s, layer)
    with act.Fori(0, NCH) as c:
        act.wait_ge(s["xt_full"], c + 1)
        nc.scalar.copy(b.xT[:, :], bank[:, LIN_XT, :]).then_inc(s["xt_ready"], 1)
        for half in range(2):
            act.wait_ge(s["kv_full"], 2 * c + half + 1)
            nc.scalar.activation(b.kv[:, 2 * half:2 * half + 2, 0:256],
                                 bank[:, LIN_KV + half, :].rearrange("p (t f) -> p t f", t=2),
                                 ACT.Relu).then_inc(s["kv_ready"], 1)
        act.wait_ge(s["q_full"], c + 1)
        nc.scalar.activation(b.qT[:, :], bank[:, LIN_Q, :], ACT.Relu).then_inc(s["q_ready"], 1)


def lin_gpsimd(pool, nc, b, s):
    with pool.Fori(0, NCH) as c:
        pool.wait_ge(s["xn_ready"], c + 1)
        pool.sem_inc(s["passed"], 1)
        xs = b.x[:, bass.ds(c * CT, CT), :]
        nc.gpsimd.tensor_tensor(xs, xs, b.pb0[:, None, :].to_broadcast([P, CT, C]), ALU.add).then_inc(s["biased"], 1)


def lin_vector(v, nc, b, s, layer):
    bank = b.banks
    stats_vector(v, nc, b, s, layer)
    v.sem_inc(s["x_added"], 2)

    def xn(c):
        if not (isinstance(c, int) and c == 0):
            v.wait_ge(s["xt_full"], c)
        for j in range(CT):
            ins = normalise(nc, b, b.xn[:, j, :], bass.ds(c * CT + j, 1))
        ins.then_inc(s["xn_ready"], 1)

    def mask(c):
        for e in range(2):
            v.wait_ge(s["sum_full"], 2 * c + e + 1)
            nc.vector.tensor_tensor(b.kvm[:, e, :], bank[:, LIN_SUM + e, 0:256], b.blockmask[:, :],
                                    ALU.mult).then_inc(s["sum_ready"], 1)

    def divide(c):
        v.wait_ge(s["ratio_full"], c + 1)
        den, ratio = (t.rearrange("p (e n) -> p e n", e=2) for t in (b.den, b.ratio))
        nc.vector.tensor_scalar(den, bank[:, LIN_NUM:LIN_NUM + 2, SEQ:2 * SEQ], LIN_EPS, None, ALU.add).then_inc(s["den"], 1)
        v.wait_ge(s["den"], c + 1)
        nc.vector.reciprocal(den, den).then_inc(s["inv"], 1)
        v.wait_ge(s["inv"], c + 1)
        nc.vector.tensor_tensor(ratio, bank[:, LIN_NUM:LIN_NUM + 2, 0:SEQ], den, ALU.mult).then_inc(s["ratio_ready"], 1)

    def add(c):
        v.wait_ge(s["y_full"], c + 1)
        v.wait_ge(s["biased"], c + 1)
        xs = b.xc[:, bass.ds(c, 1), :]
        nc.vector.tensor_tensor(xs, xs, bank[:, LIN_XT:LIN_XT + 1, :], ALU.add).then_inc(s["x_added"], 1)
        v.wait_ge(s["x_added"], c + 3)
        for j in range(CT):
            nc.vector.bn_stats(b.bn[:, bass.ds(c * CT + j, 1), :], b.x[:, bass.ds(c * CT + j, 1), :]).then_inc(b.bn_done, 1)

    xn(0)
    xn(1)
    mask(0)
    xn(2)
    divide(0)
    with v.Fori(1, NCH - 2) as c:
        mask(c)
        xn(c + 2)
        add(c - 1)
        divide(c)
    for c in (NCH - 2, NCH - 1):
        mask(c)
        add(c - 1)
        divide(c)
    add(NCH - 1)


MOE_SEMS = STATS_SEMS + ["xn_ready", "xt_full", "xt_ready", "x_hi", "x_split", "lg_full", "lg_ready", "rt",
                         "rt_diff", "rt_exp", "rt_top", "rt_idx", "rt_place", "weights_in", "weights_hi",
                         "weights_split", "z_full", "z_gelu", "hi_scalar", "hi_vector", "hi_gpsimd", "h_split",
                         "h_used", "y_copied", "yt_full", "x_added"]
MOE_XT, MOE_LG = (6, 5), 7
MOE_Y, MOE_YT = (4, 6), (5, 7)
HI_SCALAR, HI_VECTOR, HI_GPSIMD = (0, 1), 2, 3


def moe_sync(sp, nc, b, s):
    with sp.Fori(0, NE) as e:
        sp.wait_ge(s["weights_split"], 2 * e + 2)
        sp.dma_start(b.w1_raw[:, :], b.W1[bass.ds(e, 1), :, :].rearrange("o c h -> (o c) h")).then_inc(s["weights_in"], 16)
        sp.dma_start(b.w2_raw[:, :, :],
                     b.W2[bass.ds(e, 1), :, :].rearrange("o (k p) c -> p (o k) c", p=P)).then_inc(s["weights_in"], 16)


def moe_gpsimd(pool, nc, b, s):
    w2 = b.w2_raw[:, :, :].rearrange("p k c -> p (k c)")

    def split(e, half, part):
        raw, w_hi, w_lo = ((b.w1_raw[:, :], b.w1h[:, half, :], b.w1l[:, half, :]) if part % 2 == 0 else
                           (w2, b.w2h[:, half, :], b.w2l[:, half, :]))
        if part < 2:
            nc.gpsimd.tensor_copy(w_hi, raw).then_inc(s["weights_hi"], 1)
        else:
            pool.wait_ge(s["weights_hi"], 2 * e + part - 1)
            nc.gpsimd.tensor_tensor(w_lo, raw, w_hi.bitcast(F32), ALU.subtract).then_inc(s["weights_split"], 1)

    def hi(n):
        pool.wait_ge(s["z_gelu"], HB * n + HI_GPSIMD + 1 + HB)
        pool.wait_ge(s["h_used"], HB * n + HI_GPSIMD + 1)
        pool.sem_inc(s["passed"], 1)
        nc.gpsimd.tensor_copy(b.h_hi[:, HI_GPSIMD, :], b.h_raw[:, HI_GPSIMD, :]).then_inc(s["hi_gpsimd"], 1)

    def expert(e, half):
        hi(NCH * e)
        pool.wait_ge(s["weights_in"], 32 * (e + 1) + 32)
        pool.wait_ge(s["h_used"], HB * NCH * e + HB)
        pool.sem_inc(s["passed"], 1)
        for part in range(4):
            split(e + 1, 1 - half, part)
            hi(NCH * e + part + 1)
        with pool.Fori(5, NCH) as c:
            hi(NCH * e + c)

    pool.sem_inc(s["weights_split"], 2)
    pool.wait_ge(s["weights_in"], 32)
    for part in range(4):
        split(0, 0, part)
    expert(0, 0)
    with pool.Fori(0, NE // 2 - 1) as pair:
        expert(2 * pair + 1, 1)
        expert(2 * pair + 2, 0)
    with pool.Fori(0, NCH) as c:
        hi(NCH * (NE - 1) + c)


def moe_tensor(pe, nc, b, s):
    bank = b.banks
    pe.sem_inc(s["h_used"], HB)
    pe.sem_inc(s["lg_full"], 1)
    pe.sem_inc(s["yt_full"], 1)

    def turn_x(c, parity):
        pe.wait_ge(s["xn_ready"], c + 1)
        pe.wait_ge(s["x_split"], c + 1)
        for j in range(CT):
            mm = pe.transpose(bank[:, MOE_XT[parity], P * j:P * j + P], b.xn[:, j, :], b.ident[:, :])
        mm.then_inc(s["xt_full"], 1)

    def logits(c):
        pe.wait_ge(s["xt_ready"], c + 1)
        pe.wait_ge(s["lg_ready"], c + 1)
        for j in range(CT):
            mm = pe.matmul(bank[:, MOE_LG, NE * j:NE * j + NE], b.xT[:, P * j:P * j + P], b.wr[:, :],
                           start=True, stop=True)
        mm.then_inc(s["lg_full"], 1)

    turn_x(0, 0)
    with pe.Fori(0, NCH // 2 - 1) as i:
        for parity in range(2):
            turn_x(2 * i + parity + 1, 1 - parity)
            logits(2 * i + parity)
    turn_x(NCH - 1, 1)
    logits(NCH - 2)
    logits(NCH - 1)

    def first(n, c, m, half):
        pe.wait_ge(s["z_gelu"], HB * n + m + 1)
        wh, wl = b.w1h[:, half, P * m:P * m + P], b.w1l[:, half, P * m:P * m + P]
        xh, xl = b.xh_all[:, bass.ds(c * CH, CH)], b.xl_all[:, bass.ds(c * CH, CH)]
        pe.matmul(bank[:, m, :], wh, xh, start=True, stop=False)
        pe.matmul(bank[:, m, :], wl, xh, start=False, stop=False)
        pe.matmul(bank[:, m, :], wh, xl, start=False, stop=True).then_inc(s["z_full"], 1)

    def second(n, parity, m, half):
        y = bank[:, MOE_Y[parity], :]
        if m == 0:
            pe.wait_ge(s["y_copied"], n + 1)
        pe.wait_ge(s["h_split"], HB * n + m + 1 + HB)
        wh, wl = b.w2h[:, half, P * m:P * m + P], b.w2l[:, half, P * m:P * m + P]
        pe.matmul(y, wh, b.h_hi[:, m, :], start=m == 0, stop=False)
        pe.matmul(y, wl, b.h_hi[:, m, :], start=False, stop=False)
        pe.matmul(y, wh, b.h_lo[:, m, :], start=False, stop=m == HB - 1).then_inc(s["h_used"], 1)

    def turn_y(n, parity):
        pe.wait_ge(s["y_copied"], n + 1 + 2)
        pe.wait_ge(s["x_added"], n + 1)
        for j in range(CT):
            mm = pe.transpose(bank[:, MOE_YT[parity], P * j:P * j + P], b.y[:, P * j:P * j + P], b.ident[:, :])
        mm.then_inc(s["yt_full"], 1)

    def step(e, c, parity, half, edge=None):
        n = NCH * e + c
        if edge == "next expert":
            pe.wait_ge(s["weights_split"], 2 * (e + 1) + 4)
        for m in range(HB):
            if edge == "next expert":
                first(n + 1, 0, m, 1 - half)
            elif edge != "last":
                first(n + 1, c + 1, m, half)
            second(n, parity, m, half)
            if m == 1 and edge != "start":
                turn_y(n - 1, 1 - parity)

    def expert(e, half, start=False, last=False):
        step(e, 0, 0, half, "start" if start else None)
        step(e, 1, 1, half)
        with pe.Fori(1, NCH // 2 - 1) as i:
            step(e, 2 * i, 0, half)
            step(e, 2 * i + 1, 1, half)
        step(e, NCH - 2, 0, half)
        step(e, NCH - 1, 1, half, "last" if last else "next expert")

    pe.wait_ge(s["x_split"], NCH + 2)
    pe.wait_ge(s["weights_split"], 4)
    for m in range(HB):
        first(0, 0, m, 0)
    expert(0, 0, start=True)
    with pe.Fori(0, NE // 2 - 1) as pair:
        expert(2 * pair + 1, 1)
        expert(2 * pair + 2, 0)
    expert(NE - 1, 1, last=True)
    turn_y(NE * NCH - 1, 1)


def moe_scalar(act, nc, b, s, layer):
    bank = b.banks
    stats_scalar(act, nc, b, s, layer)
    act.sem_inc(s["z_gelu"], HB)
    act.sem_inc(s["y_copied"], 2)
    with act.Fori(0, NCH // 2) as i:
        for parity in range(2):
            c = 2 * i + parity
            act.wait_ge(s["xt_full"], c + 1)
            act.wait_ge(s["lg_full"], c + 1)
            nc.scalar.copy(b.xT[:, :], bank[:, MOE_XT[parity], :]).then_inc(s["xt_ready"], 1)
            nc.scalar.copy(b.xh_all[:, bass.ds(c * CH, CH)], bank[:, MOE_XT[parity], :]).then_inc(s["x_hi"], 1)
    act.wait_ge(s["rt_diff"], NCH)
    nc.scalar.activation(b.rt[:, 1, :], b.rt[:, 0, :], ACT.Exp).then_inc(s["rt_exp"], 1)

    def gelu(n, e, m):
        act.wait_ge(s["z_full"], HB * n + m + 1)
        act.wait_ge(s["h_split"], HB * n + m + 1)
        act.sem_inc(s["passed"], 1)
        nc.scalar.activation(b.h_raw[:, m, :], bank[:, m, :], ACT.Gelu,
                             bias=b.b1[:, bass.ds(4 * e + m, 1)]).then_inc(s["z_gelu"], 1)

    def hi(n, m):
        act.wait_ge(s["z_gelu"], HB * n + m + 1 + HB)
        act.wait_ge(s["h_used"], HB * n + m + 1)
        act.sem_inc(s["passed"], 1)
        nc.scalar.copy(b.h_hi[:, m, :], b.h_raw[:, m, :]).then_inc(s["hi_scalar"], 1)

    def blocks(n, e):
        gelu(n, e, 0)
        gelu(n, e, 1)
        hi(n, 0)
        gelu(n, e, 2)
        hi(n, 1)
        gelu(n, e, 3)

    def y_copy(n, e, parity):
        act.wait_ge(s["h_used"], HB * n + HB + HB)
        act.wait_ge(s["yt_full"], n + 1)
        act.sem_inc(s["passed"], 1)
        nc.scalar.activation(b.y[:, :], bank[:, MOE_Y[parity], :], ACT.Identity,
                             bias=b.b2[:, bass.ds(e, 1)]).then_inc(s["y_copied"], 1)

    def expert(e, last=False):
        with act.Fori(0, NCH // 2 - 1) as i:
            for parity in range(2):
                n = NCH * e + 2 * i + parity
                blocks(n + 1, e)
                y_copy(n, e, parity)
        blocks(NCH * e + NCH - 1, e)
        y_copy(NCH * e + NCH - 2, e, 0)
        if not last:
            blocks(NCH * e + NCH, e + 1)
        y_copy(NCH * e + NCH - 1, e, 1)

    blocks(0, 0)
    with act.Fori(0, NE - 1) as e:
        expert(e)
    expert(NE - 1, last=True)


def moe_vector(v, nc, b, s, layer, stats):
    bank = b.banks
    stats_vector(v, nc, b, s, layer)
    v.sem_inc(s["h_split"], HB)
    v.sem_inc(s["x_added"], 2)
    v.sem_inc(s["x_split"], 2)
    v.sem_inc(s["lg_ready"], 1)

    def xn(c):
        if not (isinstance(c, int) and c == 0):
            v.wait_ge(s["xt_full"], c)
        for j in range(CT):
            ins = normalise(nc, b, b.xn[:, j, :], bass.ds(c * CT + j, 1))
        ins.then_inc(s["xn_ready"], 1)

    def choose(c, parity, following=None):
        v.wait_ge(s["x_hi"], c + 1)
        nc.vector.tensor_tensor(b.xl_all[:, bass.ds(c * CH, CH)], bank[:, MOE_XT[parity], :],
                                b.xh_all[:, bass.ds(c * CH, CH)].bitcast(F32), ALU.subtract).then_inc(s["x_split"], 1)
        if following is not None:
            xn(following)
        v.wait_ge(s["lg_full"], c + 2)
        nc.vector.tensor_tensor(b.lg[:, :, :], bank[:, MOE_LG, 0:CT * NE].rearrange("p (j e) -> p j e", e=NE),
                                b.br[:, None, :].to_broadcast([P, CT, NE]), ALU.add).then_inc(s["lg_ready"], 1)
        v.wait_ge(s["lg_ready"], c + 2)
        v.sem_inc(s["passed"], 1)
        for j in range(CT):
            nc.vector.max(b.top[:, j, :], b.lg[:, j, :]).then_inc(s["rt_top"], 1)
        v.wait_ge(s["rt_top"], CT * c + CT)
        nc.vector.tensor_tensor(b.rt[:, 0, bass.ds(c * CT, CT)], b.top[:, :, 1], b.top[:, :, 0],
                                ALU.subtract).then_inc(s["rt_diff"], 1)
        for j in range(CT):
            nc.vector.max_index(b.idx[:, j, :], b.top[:, j, :], b.lg[:, j, :]).then_inc(s["rt_idx"], 1)
        v.wait_ge(s["rt_idx"], CT * c + CT)
        nc.vector.tensor_copy(b.idxf[:, bass.ds(c * CT, CT), :], b.idx[:, :, 0:2]).then_inc(s["rt_place"], 1)

    def weigh():
        steps = s["rt"]
        ex, w1, w2 = (b.rt[:, k, :] for k in range(1, 4))
        all_experts = [P, TILES, NE]
        iota = b.iota8[:, None, :].to_broadcast(all_experts)
        v.wait_ge(s["rt_place"], NCH)
        for k in range(2):
            nc.vector.tensor_tensor(b.oh[:, k, :, :], iota, b.idxf[:, :, k:k + 1].to_broadcast(all_experts),
                                    ALU.is_equal).then_inc(steps, 1)
        v.wait_ge(s["rt_exp"], 1)
        nc.vector.tensor_scalar(w1, ex, 1.0, None, ALU.add).then_inc(steps, 1)
        v.wait_ge(steps, 3)
        nc.vector.reciprocal(w1, w1).then_inc(steps, 1)
        v.wait_ge(steps, 4)
        nc.vector.tensor_scalar(w1, w1, 0.5, None, ALU.mult).then_inc(steps, 1)
        v.wait_ge(steps, 5)
        nc.vector.tensor_tensor(w2, w1, ex, ALU.mult).then_inc(steps, 1)
        nc.vector.tensor_tensor(b.oh[:, 0, :, :], b.oh[:, 0, :, :], w1[:, :, None].to_broadcast(all_experts),
                                ALU.mult).then_inc(steps, 1)
        v.wait_ge(steps, 7)
        nc.vector.tensor_tensor(b.oh[:, 1, :, :], b.oh[:, 1, :, :], w2[:, :, None].to_broadcast(all_experts),
                                ALU.mult).then_inc(steps, 1)
        v.wait_ge(steps, 8)
        nc.vector.tensor_tensor(b.wf[:, :, :], b.oh[:, 0, :, :], b.oh[:, 1, :, :], ALU.add).then_inc(steps, 1)
        v.wait_ge(steps, 9)

    xn(0)
    xn(1)
    with v.Fori(0, NCH // 2 - 1) as i:
        for parity in range(2):
            choose(2 * i + parity, parity, 2 * i + parity + 2)
    choose(NCH - 2, 0)
    choose(NCH - 1, 1)

    def lo(n, m):
        if m in HI_SCALAR:
            v.wait_ge(s["hi_scalar"], 2 * n + m + 1)
        elif m == HI_VECTOR:
            v.wait_ge(s["hi_vector"], n + 1)
        else:
            v.wait_ge(s["hi_gpsimd"], n + 1)
        nc.vector.tensor_tensor(b.h_lo[:, m, :], b.h_raw[:, m, :], b.h_hi[:, m, :].bitcast(F32),
                                ALU.subtract).then_inc(s["h_split"], 1)

    def hi(n):
        v.wait_ge(s["z_gelu"], HB * n + HI_VECTOR + 1 + HB)
        v.wait_ge(s["h_used"], HB * n + HI_VECTOR + 1)
        v.sem_inc(s["passed"], 1)
        nc.vector.tensor_copy(b.h_hi[:, HI_VECTOR, :], b.h_raw[:, HI_VECTOR, :]).then_inc(s["hi_vector"], 1)

    def add(n, e, c, parity):
        v.wait_ge(s["yt_full"], n + 2)
        v.wait_ge(s["x_added"], n + 2)
        for j in range(CT):
            xs = b.x[:, bass.ds(c * CT + j, 1), :]
            ins = nc.vector.scalar_tensor_tensor(xs, bank[:, MOE_YT[parity]:MOE_YT[parity] + 1, P * j:P * j + P],
                                                 b.wfe[:, bass.ds(c * CT * NE + j * NE + e, 1)], xs,
                                                 ALU.mult, ALU.add)
        ins.then_inc(s["x_added"], 1)
        if stats and isinstance(e, int) and e == NE - 1:
            v.wait_ge(s["x_added"], n + 3)
            for j in range(CT):
                nc.vector.bn_stats(b.bn[:, bass.ds(c * CT + j, 1), :],
                                   b.x[:, bass.ds(c * CT + j, 1), :]).then_inc(b.bn_done, 1)

    def step(n, e, c, parity):
        lo(n + 1, 0)
        lo(n + 1, 1)
        if e is not None:
            add(n - 1, e, c, parity)
        hi(n + 1)
        lo(n + 1, 2)
        lo(n + 1, 3)

    def expert(e, previous):
        n = NCH * e
        step(n, previous, NCH - 1, 1)
        step(n + 1, e, 0, 0)
        with v.Fori(0, NCH // 2 - 1) as i:
            step(n + 2 * i + 2, e, 2 * i + 1, 1)
            step(n + 2 * i + 3, e, 2 * i + 2, 0)

    lo(0, 0)
    lo(0, 1)
    hi(0)
    lo(0, 2)
    lo(0, 3)
    weigh()
    expert(0, None)
    with v.Fori(0, NE - 2) as e:
        expert(e + 1, e)
    n = NCH * (NE - 1)
    step(n, NE - 2, NCH - 1, 1)
    step(n + 1, NE - 1, 0, 0)
    with v.Fori(0, NCH // 2 - 2) as i:
        step(n + 2 * i + 2, NE - 1, 2 * i + 1, 1)
        step(n + 2 * i + 3, NE - 1, 2 * i + 2, 0)
    step(n + NCH - 2, NE - 1, NCH - 3, 1)
    add(NE * NCH - 2, NE - 1, NCH - 2, 0)
    add(NE * NCH - 1, NE - 1, NCH - 1, 1)


ATT_SEMS = STATS_SEMS + ["xn_ready", "sel_own", "sel_rec", "s_full", "s_hi", "s_free", "st_full", "st_free",
                         "drafted", "staged_past", "staged_k", "staged_q", "staged_rq", "placed_past", "placed_k",
                         "placed_q", "placed_rq", "pv_done", "pv_saved", "inv", "summed", "half_bg", "kept",
                         "kept_older", "mix", "x_added"]
S_BANKS, ST_BANK, PV_BANK = (0, 1, 7), 2, 6
QK = 96
STAGE_DMAS = 3
S_SLOTS, ST_SLOTS, SAVE_SLOTS = 3, 2, 2
P_SLOTS = 6


def maxima(kind, g):
    return [("max", kind, g, h, t) for h in range(4 if kind in ("rec", "rnext") else 2) for t in range(BT)]


def step_order(own, mid, rec, prep, fin):
    kinds = (["own"] if own else []) + (["rec"] if rec else [])
    if not kinds:
        yield "flip", "rec", NG - 1, 1, 0
        yield from (("fin", kind, g, 0, 0) for kind, g in (("ctx", 0), ("gate", 0), ("mix", 0), ("mix", 1)))
        return
    pairs = [(kind, g, half) for g in range(NG) for kind in kinds for half in range(PAST if kind == "rec" else 1)]
    per_group = 2 * len(pairs) // NG
    last_at = per_group - 1

    side = {(g, at): [] for g in range(NG) for at in range(per_group)}
    tail_turn = []
    for g in range(NG):
        ahead = rec_next = turn = rec_turn = []
        if own and (g + 1 < NG or prep):
            name = ("own", g + 1) if g + 1 < NG else ("next", 0)
            ahead, turn = maxima(*name), [("turn",) + name + (0, 0)]
        if rec and g + 1 < NG or mid and g + 1 == NG:
            name = ("rec", g + 1) if g + 1 < NG else ("rnext", 0)
            rec_next, rec_turn = maxima(*name), [("turn",) + name + (0, 0)]
        if own and rec:
            rec_turn_now = [("turn", "rec", g, 0, 0)] if g > 0 else []
            side[g, 1] += ahead[0:2] + rec_turn_now + ahead[2:3]
            side[g, 2] += ahead[3:4]
            side[g, 3] += rec_next[0:2] + turn + rec_next[2:3]
            side[g, 4] += rec_next[3:4]
            side[g, 5] += rec_next[4:7]
            if g + 1 < NG:
                side[g + 1, 0] += rec_next[7:8]
        elif own:
            side[g, 0] += ahead
            side[g, 1] += rec_next[0:1] + turn + rec_next[1:7]
        else:
            for at in range(4):
                side[g, at] += rec_next[2 * at:2 * at + 2]
            if g + 1 < NG:
                side[g, 3] += rec_turn
        if g + 1 == NG and rec_next:
            tail_turn = [rec_next[7:8] if own else [], rec_turn]
    if fin:
        side[0, 0] += [("flip", "rec", NG - 1, 1, 0)]
    if mid:
        side[0, 1] += [("mid", "out", 0, 0, 0)]
    if fin:
        side[0, 1] += [("fin", "ctx", 0, 0, 0)]
        side[0, 2] += [("fin", "gate", 0, 0, 0)]
        side[1, 0] += [("fin", "mix", 0, 0, 0)]
        side[1, last_at] += [("fin", "mix", 1, 0, 0)]
    if mid or rec:
        side[1, last_at] += [("keep", "out", 0, 0, 0)]
    if prep:
        side[0, 0] += [("norm", "x", 0, 0, 0)]
        side[0, 1] += [("prep", "x", 0, 0, 0)]
        side[1, 0] += [("prep", "k", 0, 0, 0)]
        side[1, 1] += [("prep", "q", 0, 0, 0)]
    if mid:
        side[0, min(3, last_at)] += [("mid", "rq", 0, 0, 0)]
    placed = (["k", "q"] if prep else []) + (["rq"] if mid else [])
    for g in range(NG - 1):
        side[g + 1, min(3, last_at)] += [("place", kind, g, 0, 0) for kind in placed]

    for n, (kind, g, half) in enumerate(pairs):
        for u in range(2):
            if n > 1 and not u:
                yield ("save",) + pairs[n - 2] + (0,)
            yield "unit", kind, g, 2 * half + u, 0
            beside = side[g, (2 * n + u) % per_group]
            yield from beside[0:1]
            if n > 0 and u:
                yield ("pv",) + pairs[n - 1] + (0,)
                yield from beside[1:2]
                if n > 1:
                    yield ("flip",) + pairs[n - 2] + (0,)
                yield ("pv",) + pairs[n - 1] + (1,)
                yield from beside[2:]
            else:
                yield from beside[1:]
    before, last = pairs[-2], pairs[-1]
    own_ctx = [("own", "ctx", 0, 0, 0)] if own else []
    values = [("prep", "v", 0, 0, 0)] if prep else []
    last_max, last_turn = tail_turn or ([], [])
    yield from last_max
    if rec:
        yield from own_ctx
    yield ("save",) + before + (0,)
    if rec:
        yield from values
    yield ("pv",) + last + (0,)
    yield from last_turn
    yield ("pv",) + last + (1,)
    yield ("flip",) + before + (0,)
    if not rec:
        yield from values
    yield ("save",) + last + (0,)
    for kind in placed:
        yield "place", kind, NG - 1, 0, 0
    if not rec:
        yield ("flip",) + last + (0,)
        yield from own_ctx


class Counts:
    def __init__(self):
        self.base = {}
        self.n = {}
        self.mark = {}

    def add(self, key, k=1):
        self.n[key] = self.n.get(key, 0) + k

    def at(self, key):
        return self.base.get(key, 0) + self.n.get(key, 0)

    def slot(self, key, slots):
        return self.n.get(key, 0) % slots


def count_event(k, what, kind, u, t):
    if what == "max":
        k.add("s")
    elif what == "turn":
        k.add("st")
    elif what == "unit":
        k.add("st")
        k.add("unit")
        k.add("unit_pair", u % 2)
    elif what in ("pv", "save", "flip"):
        k.add(what, 1 if what != "pv" or t == 1 else 0)
        if what == "flip":
            k.add("s")
            k.add("summed", int(kind == "rec" and u == 1))
    elif what in ("keep", "norm", "place"):
        pass
    elif kind in ("k", "q", "rq"):
        k.add("s")
        k.add("split")
        k.add(what if what == "past" else kind)
    else:
        k.add("st")


STAGES = ("own", "mid", "rec", "fin", "prep")


def walk(k, stages, body, e=0):
    own, mid, rec, fin, prep = (name in stages for name in STAGES)
    k.own, k.mid, k.rec, k.fin, k.prep = own, mid, rec, fin, prep
    k.mark = {"st_start": k.at("st")}
    for what, kind, g, u, t in step_order(own, mid, rec, prep, fin):
        body(what, kind, g, u, t, e)
        count_event(k, what, kind, u, t)
    for name in STAGES:
        k.add(name, int(name in stages))


def run_steps(eng, k, body):
    walk(k, ("own", "prep"), body, 0)
    walk(k, ("own", "mid", "prep"), body, 1)
    walk(k, ("own", "mid", "rec", "prep"), body, 2)
    per = Counts()
    walk(per, STAGES, lambda *event: None)
    before = dict(k.n)
    with eng.Fori(0, BATCH - 4) as i:
        k.base = {key: i * n for key, n in per.n.items()}
        walk(k, STAGES, body, i + 3)
    k.base = {}
    k.n = {key: before.get(key, 0) + (BATCH - 4) * n for key, n in per.n.items()}
    walk(k, ("own", "mid", "rec", "fin"), body, BATCH - 1)
    walk(k, ("mid", "rec", "fin"), body, BATCH)
    walk(k, ("rec", "fin"), body, BATCH + 1)
    walk(k, ("fin",), body, BATCH + 2)


def run_prologue(k, body):
    events = [("prep", kind, 0, 0, 0) for kind in ("x", "k", "q")]
    events += [("past", "k", 0, 0, 0), ("prep", "v", 0, 0, 0), ("past", "v", 0, 0, 0)]
    events += [("place", kind, g, 0, 0) for g in range(NG) for kind in ("k", "q")]
    events += maxima("next", 0) + [("turn", "next", 0, 0, 0)]
    events += [("place", "past", g, 0, 0) for g in range(NG)]
    for event in events:
        body(*event, 0)
        count_event(k, event[0], event[1], 0, 0)
    k.add("prep")


def projection(b, what, kind):
    if what == "past":
        return b.past_split, b.brk, PAST * SEQ
    split = {"k": b.k_split, "q": b.q_split, "rq": b.rq_split}[kind]
    return split, {"k": b.bk, "q": b.bq, "rq": b.brq}[kind], SEQ


def att_tensor(pe, nc, b, s):
    bank = b.banks
    k = Counts()
    pe.sem_inc(s["pv_done"], P_SLOTS // 2)
    pe.wait_ge(b.loaded["att"], 16 * b.n_loads["att"])
    units = []
    tiles = [slice(P * j, P * j + P) for j in range(BT)]

    def body(what, kind, g, u, t, e):
        uses_s = what in ("max", "flip") or what != "place" and kind in ("k", "q", "rq")
        uses_st = what in ("turn", "unit", "prep", "own", "mid", "past", "fin") and not uses_s
        if uses_s:
            pe.wait_ge(s["s_free"], k.at("s") + 1)
            out_s = bank[:, S_BANKS[k.slot("s", S_SLOTS)], :]
        if uses_st:
            pe.wait_ge(s["st_free"], k.at("st") + 1)
            st = ST_BANK + 2 * k.slot("st", ST_SLOTS)

        if what == "max":
            first = u == 0 and t == 0
            if kind in ("own", "next"):
                if first:
                    entries = k.at("prep") - (1 if kind == "own" else 0)
                    pe.wait_ge(s["placed_k"], NG * entries + g + 1)
                    pe.wait_ge(s["placed_q"], NG * entries + g + 1)
                lhs, rhs = b.q_own[0:QK, g, tiles[t]], b.k_own[0:QK, 4 * g + 2 * u:4 * g + 2 * u + 2, :]
            else:
                if first:
                    entries = k.at("rec") + int(k.rec and kind == "rnext")
                    pe.wait_ge(s["placed_rq"], NG * entries + g + 1)
                    if not k.rec:
                        pe.wait_ge(s["placed_past"], NG)
                lhs, rhs = b.q_rec[0:QK, g, tiles[t]], b.k_rec[0:QK, 4 * g + u, :]
            pe.matmul(out_s, lhs, rhs, start=True, stop=True).then_inc(s["s_full"], 1)
            k.mark["max_" + kind] = k.at("s")
        elif what == "turn":
            pe.wait_ge(s["s_free"], k.mark["max_" + kind] + 1 + S_SLOTS)
            cols = b.m_rec if kind in ("rec", "rnext") else b.m_own
            for j in range(BT):
                mm = pe.transpose(bank[:, st, tiles[j]], cols[:, j, 32 * g:32 * g + P].bitcast(F32), b.ident[:, :])
            mm.then_inc(s["st_full"], 1)
            k.mark["turn_" + kind, g] = k.at("st")
        elif what == "unit":
            if g == 0 and u == 0:
                pe.wait_ge(s["sel_own"] if kind == "own" else s["sel_rec"], 1)
                pe.wait_ge(s["st_free"], k.mark["st_start"] + ST_SLOTS)
            elif u == 0:
                pe.wait_ge(s["st_free"], k.mark["turn_" + kind, g] + 1 + ST_SLOTS)
            for n in range(4):
                h = 4 * g + 2 * (u % 2) + n // 2
                if kind == "own":
                    lhs, rhs = b.k_own[:, h, tiles[n % 2]], b.q_own[:, g, :]
                else:
                    at = SEQ * (u // 2) + P * (n % 2)
                    lhs, rhs = b.k_rec[:, h, at:at + P], b.q_rec[:, g, :]
                mm = pe.matmul(bank[:, st + n // 2, SEQ * (n % 2):SEQ * (n % 2) + SEQ], lhs, rhs,
                               start=True, stop=True)
            mm.then_inc(s["st_full"], 1)
            units.append(k.at("st"))
        elif what == "pv":
            if t == 0:
                pe.wait_ge(s["st_free"], units[1] + 1 + ST_SLOTS)
                del units[0:2]
                if k.n.get("pv", 0) > 0:
                    pe.wait_ge(s["pv_saved"], k.at("pv"))
            first = 2 * k.n.get("pv", 0) % P_SLOTS
            for j in range(4):
                h = 4 * g + j
                val = b.v_own[:, t, h, :] if kind == "own" else b.v_rec[:, BT * u + t, h, :]
                at = ((j % 2) * BT + t) * SEQ
                mm = pe.matmul(bank[32 * j:32 * j + 32, PV_BANK, 0:SEQ], val, b.p[:, first + j // 2, at:at + SEQ],
                               start=t == 0, stop=t == BT - 1)
            if t == BT - 1:
                mm.then_inc(s["pv_done"], 1)
        elif what == "flip":
            pe.wait_ge(s["pv_saved"], k.at("flip") + 1)
            for j in range(BT):
                mm = pe.transpose(out_s[:, tiles[j]], b.pvs[:, k.slot("flip", SAVE_SLOTS), tiles[j]], b.ident[:, :])
            mm.then_inc(s["s_full"], 1)
            k.mark["flip_" + kind] = k.at("s")
        elif what == "past" and kind == "k":
            pe.matmul(out_s, b.wrk[:, :], b.pastT[:, :], start=True, stop=True).then_inc(s["s_full"], 1)
        elif what == "past":
            for n in range(PAST * BT):
                out = bank[:, st, P * n:P * n + P]
                pe.matmul(out, b.pastT[:, P * n:P * n + P], b.wrv[:, :], start=True, stop=False)
                mm = pe.matmul(out, b.ones[0:1, 0:P], b.brv[0:1, :], start=False, stop=True)
            mm.then_inc(s["st_full"], 1)
        elif what != "place" and kind in ("k", "q", "rq"):
            if kind == "rq":
                pe.wait_ge(s["st_free"], k.mark["out"] + 1 + ST_SLOTS)
            elif "xT" in k.mark:
                pe.wait_ge(s["st_free"], k.mark["xT"] + 1 + ST_SLOTS)
            w = {"k": b.wk, "q": b.wq, "rq": b.wrq}[kind]
            rhs = b.outT[:, :] if kind == "rq" else b.xT[:, 0:SEQ]
            pe.matmul(out_s[:, 0:SEQ], w[:, :], rhs, start=True, stop=True).then_inc(s["s_full"], 1)
        elif what == "prep" and kind == "x":
            pe.wait_ge(s["xn_ready"], k.at("prep") + 1)
            for j in range(BT):
                mm = pe.transpose(bank[:, st, tiles[j]], b.xn[:, j, :], b.ident[:, :])
            mm.then_inc(s["st_full"], 1)
            k.mark["xT"] = k.at("st")
        elif what == "prep" and kind == "v":
            for j in range(BT):
                mm = pe.matmul(bank[:, st, tiles[j]], b.xT[:, tiles[j]], b.wv[:, :], start=True, stop=True)
            mm.then_inc(s["st_full"], 1)
        elif what == "own" and kind == "ctx":
            pe.wait_ge(s["s_free"], k.mark["flip_own"] + 1 + S_SLOTS)
            for j in range(BT):
                mm = pe.transpose(bank[:, st, tiles[j]], b.ctx[:, j, :], b.ident[:, :])
            mm.then_inc(s["st_full"], 1)
        elif what == "mid" and kind == "out":
            pe.wait_ge(s["st_free"], k.mark["st_start"] + ST_SLOTS)
            pe.matmul(bank[:, st, 0:SEQ], b.wo[:, :], b.ctxT[:, :], start=True, stop=True).then_inc(s["st_full"], 1)
            k.mark["out"] = k.at("st")
        elif what == "fin" and kind == "ctx":
            pe.wait_ge(s["summed"], k.at("summed"))
            for j in range(BT):
                mm = pe.transpose(bank[:, st, tiles[j]], b.rctx[:, j, :], b.ident[:, :])
            mm.then_inc(s["st_full"], 1)
            k.mark["rctx"] = k.at("st")
        elif what == "fin" and kind == "gate":
            pe.wait_ge(s["kept_older"], k.at("fin") + 1)
            pe.wait_ge(s["st_free"], k.mark["rctx"] + 1 + ST_SLOTS)
            pe.matmul(bank[:, st, 0:SEQ], b.wg[:, 0, :], b.out_older[:, :], start=True, stop=False)
            pe.matmul(bank[:, st, 0:SEQ], b.wg[:, 1, :], b.rcT[:, :], start=False, stop=True).then_inc(s["st_full"], 1)
        elif what == "fin" and kind == "mix":
            pe.wait_ge(s["mix"], 3 * k.at("fin") + 3)
            pe.transpose(bank[:, st, 0:P], b.mixd[:, tiles[g]], b.ident[:, :]).then_inc(s["st_full"], 1)

    run_prologue(k, body)
    run_steps(pe, k, body)


def att_scalar(act, nc, b, s, layer):
    bank = b.banks
    stats_scalar(act, nc, b, s, layer)
    act.sem_inc(s["st_free"], ST_SLOTS)
    k = Counts()

    def body(what, kind, g, u, t, e):
        if what in ("max", "pv", "flip", "keep", "norm", "place"):
            return
        if what == "save":
            act.wait_ge(s["pv_done"], k.at("save") + 1 + P_SLOTS // 2)
            nc.scalar.copy(b.pvs[:, k.slot("save", SAVE_SLOTS), :], bank[:, PV_BANK, 0:SEQ]).then_inc(s["pv_saved"], 1)
            return
        if kind in ("k", "q", "rq"):
            act.wait_ge(s["s_full"], k.at("s") + 1)
            if what != "past" and k.n.get(kind, 0):
                act.wait_ge(s["staged_" + kind], STAGE_DMAS * 16 * k.at(kind))
            split, bias, width = projection(b, what, kind)
            nc.scalar.activation(split[:, 0, 0:width], bank[:, S_BANKS[k.slot("s", S_SLOTS)], 0:width],
                                 ACT.Identity, bias=bias[:, 0:1]).then_inc(s["s_hi"], 1)
            return
        st = ST_BANK + 2 * k.slot("st", ST_SLOTS)
        act.wait_ge(s["st_full"], k.at("st") + 1)
        if what == "turn":
            q = b.q_rec if kind in ("rec", "rnext") else b.q_own
            nc.scalar.copy(q[QK:P, g, :], bank[QK:P, st, 0:SEQ]).then_inc(s["st_free"], 1)
        elif what == "unit":
            if k.n.get("unit", 0) == P_SLOTS - 2:
                act.wait_ge(s["placed_past"], NG)
            act.wait_ge(s["pv_done"], k.at("unit_pair") + 1)
            nc.scalar.activation(b.p[:, k.slot("unit", P_SLOTS), :].rearrange("p (a n) -> p a n", a=2),
                                 bank[:, st:st + 2, :], ACT.Exp, scale=SCALE).then_inc(s["st_free"], 1)
        elif what == "past":
            nc.scalar.copy(b.v_rec[:, :, :, 0:D],
                           bank[:, st, :].rearrange("p (n h d) -> p n h d", h=NH, d=D)).then_inc(s["st_free"], 1)
        elif kind == "v":
            nc.scalar.copy(b.v_own[:, :, :, 0:D],
                           bank[:, st, 0:SEQ].rearrange("p (n h d) -> p n h d", h=NH, d=D)).then_inc(s["st_free"], 1)
        elif kind == "x":
            nc.scalar.copy(b.xT[:, 0:SEQ], bank[:, st, 0:SEQ]).then_inc(s["st_free"], 1)
        elif what == "own" and kind == "ctx":
            nc.scalar.activation(b.ctxT[:, :], bank[:, st, 0:SEQ], ACT.Identity,
                                 bias=b.bv[:, 0:1]).then_inc(s["st_free"], 1)
        elif what == "fin" and kind == "ctx":
            nc.scalar.activation(b.rcT[:, :], bank[:, st, 0:SEQ], ACT.Identity,
                                 scale=1.0 / PAST).then_inc(s["st_free"], 1)
        elif what == "fin" and kind == "mix":
            nc.scalar.copy(b.th[:, P * g:P * g + P], bank[:, st, 0:P]).then_inc(s["st_free"], 1)
        elif what == "fin" and kind == "gate":
            act.wait_ge(s["x_added"], BT * k.at("fin") + 1)
            nc.scalar.activation(b.th[:, :], bank[:, st, 0:SEQ], ACT.Tanh, bias=b.bg[:, 0:1],
                                 scale=0.5).then_inc(s["st_free"], 1)
        elif what == "mid" and kind == "out":
            if k.rec:
                act.wait_ge(s["kept"], k.at("mid"))
            nc.scalar.activation(b.outT[:, :], bank[:, st, 0:SEQ], ACT.Identity,
                                 bias=b.bo[:, 0:1]).then_inc(s["st_free"], 1)

    nc.scalar.copy(b.k_own[QK:P, :, :], b.sel[QK:P, 0:NH, None].to_broadcast([32, NH, SEQ])).then_inc(s["sel_own"], 1)
    act.wait_ge(s["half_bg"], 1)
    run_prologue(k, body)
    run_steps(act, k, body)


def att_sync(sp, nc, b, s):
    k = Counts()

    def body(what, kind, g, u, t, e):
        if what == "place" or kind not in ("k", "q", "rq"):
            return
        sp.wait_ge(s["s_free"], k.at("s") + 1 + S_SLOTS)
        name = what if what == "past" else kind
        if what != "past" and k.n.get(kind, 0):
            sp.wait_ge(s["placed_" + kind], NG * k.at(kind))
        split, _, width = projection(b, what, kind)
        dst = {"past": b.past_parts, "k": b.k_parts, "q": b.q_parts, "rq": b.rq_parts}[name]
        draft = b.drafts[name]
        sp.dma_start(draft[:, :, 0:width], split[:, :, 0:width].bitcast(F32)).then_inc(s["drafted"], 16)
        sp.wait_ge(s["drafted"], 16 * (k.at("split") + 1))
        groups = draft.rearrange("(g r) a n -> a r g n", g=NG)
        for quadrant, part in enumerate((0, 1, 0) if kind == "k" else (0, 0, 1)):
            sp.dma_start(dst[32 * quadrant:32 * quadrant + 32, :, 0:width],
                         groups[part, :, :, 0:width]).then_inc(s["staged_" + name], 16)

    run_prologue(k, body)
    run_steps(sp, k, body)


def att_gpsimd(pool, nc, b, s):
    pool.wait_ge(b.loaded["att"], 16 * b.n_loads["att"])
    k = Counts()

    def body(what, kind, g, u, t, e):
        if what == "keep":
            if k.fin:
                pool.wait_ge(s["mix"], 3 * k.at("fin") + 3)
            if k.rec:
                pool.wait_ge(s["kept"], k.at("mid"))
                pool.sem_inc(s["passed"], 1)
                nc.gpsimd.tensor_copy(b.out_older[:, :], b.out_kept[:, :]).then_inc(s["kept_older"], 1)
                pool.wait_ge(s["kept_older"], k.at("rec") + 1)
            if k.mid:
                pool.wait_ge(s["st_free"], k.mark["out"] + 1 + ST_SLOTS)
                pool.sem_inc(s["passed"], 1)
                nc.gpsimd.tensor_copy(b.out_kept[:, :], b.outT[:, :]).then_inc(s["kept"], 1)
        elif kind == "out":
            k.mark["out"] = k.at("st")
        elif what == "unit":
            k.mark["unit_" + kind, g] = k.at("st")
        elif what == "place" and kind != "past":
            count = k.at(kind)
            pool.wait_ge(s["staged_" + kind], STAGE_DMAS * 16 * count)
            reader = "rec" if kind == "rq" else "own"
            if (f"unit_{reader}", g) in k.mark:
                pool.wait_ge(s["st_full"], k.mark[f"unit_{reader}", g] + 1)
            pool.sem_inc(s["passed"], 1)
            if kind in ("q", "rq"):
                dst, src = (b.q_own, b.q_parts) if kind == "q" else (b.q_rec, b.rq_parts)
                nc.gpsimd.tensor_copy(dst[0:QK, g, :], src[:, g, :]).then_inc(s["placed_" + kind], 1)
            else:
                for h in range(4):
                    ins = nc.gpsimd.tensor_scalar(b.k_own[0:QK, 4 * g + h, :], b.k_parts[:, g, 0:SEQ],
                                                  b.headmask[0:QK, h:h + 1], 1.0, ALU.mult, ALU.mult)
                ins.then_inc(s["placed_" + kind], 1)

    run_prologue(k, body)
    run_steps(pool, k, body)


def att_vector(v, nc, b, s, layer):
    bank = b.banks
    stats_vector(v, nc, b, s, layer)
    v.sem_inc(s["s_free"], S_SLOTS)
    v.sem_inc(s["x_added"], 1)
    v.wait_ge(b.loaded["att"], 16 * b.n_loads["att"])
    nc.vector.tensor_scalar(b.bg[:, :], b.bg[:, :], 0.5, None, ALU.mult).then_inc(s["half_bg"], 1)
    k = Counts()

    def xn(entry):
        for j in range(BT):
            ins = normalise(nc, b, b.xn[:, j, :], bass.ds(entry * BT + j, 1))
        ins.then_inc(s["xn_ready"], 1)

    xn(0)

    def body(what, kind, g, u, t, e):
        src = bank[:, S_BANKS[k.slot("s", S_SLOTS)], :]
        if what == "max":
            v.wait_ge(s["s_full"], k.at("s") + 1)
            cols, at, step = (b.m_rec, 4 * u, 2) if kind in ("rec", "rnext") else (b.m_own, 8 * u, 4)
            at += QK + 32 * g
            nc.vector.reduce_max(cols[:, t, at:at + 2 * step:step], src.rearrange("p (a n) -> p a n", a=2),
                                 AX.X).then_inc(s["s_free"], 1)
        elif what == "norm":
            xn(e + 1)
        elif what == "place" and kind == "past":
            if g == 0:
                v.wait_ge(s["staged_past"], STAGE_DMAS * 16)
            for h in range(4):
                ins = nc.vector.tensor_scalar(b.k_rec[0:QK, 4 * g + h, :], b.past_parts[:, g, :],
                                              b.headmask[0:QK, h:h + 1], None, ALU.mult)
            ins.then_inc(s["placed_past"], 1)
        elif what == "own" and kind == "ctx" and not k.mid:
            nc.vector.tensor_copy(b.k_rec[QK:P, :, :].rearrange("p h (a n) -> p (h a) n", a=PAST),
                                  b.sel[QK:P, NH:NH + NH * PAST, None].to_broadcast([32, NH * PAST, SEQ])
                                  ).then_inc(s["sel_rec"], 1)
        elif what != "place" and kind in ("k", "q", "rq"):
            v.wait_ge(s["s_hi"], k.at("split") + 1)
            split, bias, width = projection(b, what, kind)
            nc.vector.scalar_tensor_tensor(split[:, 1, 0:width], src[:, 0:width], bias[:, 0:1],
                                           split[:, 0, 0:width].bitcast(F32),
                                           ALU.add, ALU.subtract).then_inc(s["s_free"], 1)
        elif what == "flip":
            n = k.at("s")
            v.wait_ge(s["s_full"], n + 1)
            acc = src[:, 0:SEQ].rearrange("p (j h w) -> p j h w", j=BT, w=VW)
            inv = b.inv[:, k.slot("flip", 2), :, :]
            nc.vector.reciprocal(inv[:, :, :, None], acc[:, :, :, D:D + 1]).then_inc(s["inv"], 1)
            v.wait_ge(s["inv"], k.at("flip") + 1)
            ctx = b.ctx if kind == "own" else b.rctx
            out = ctx[:, :, 32 * g:32 * g + 32].rearrange("p j (h d) -> p j h d", d=D)
            inv = inv[:, :, :, None].to_broadcast([P, BT, 4, D])
            if kind == "own" or u == 0:
                nc.vector.tensor_tensor(out, acc[:, :, :, 0:D], inv, ALU.mult).then_inc(s["s_free"], 1)
            else:
                nc.vector.tensor_tensor(b.rec_tmp[:, :, :, :], acc[:, :, :, 0:D], inv, ALU.mult).then_inc(s["s_free"], 1)
                v.wait_ge(s["s_free"], n + 1 + S_SLOTS)
                nc.vector.tensor_tensor(out, out, b.rec_tmp[:, :, :, :], ALU.add).then_inc(s["summed"], 1)
        elif what == "fin" and kind == "ctx":
            k.mark["rcT"] = k.at("st")
        elif what == "fin" and kind == "gate":
            n = 3 * k.at("fin")
            v.wait_ge(s["kept_older"], k.at("fin") + 1)
            v.wait_ge(s["st_free"], k.mark["rcT"] + 1 + ST_SLOTS)
            nc.vector.tensor_tensor(b.mixd[:, :], b.rcT[:, :], b.out_older[:, :], ALU.subtract).then_inc(s["mix"], 1)
            v.wait_ge(s["mix"], n + 1)
            v.wait_ge(s["st_free"], k.at("st") + 1 + ST_SLOTS)
            nc.vector.scalar_tensor_tensor(b.mixd[:, :], b.th[:, :], 1.0, b.mixd[:, :],
                                           ALU.add, ALU.mult).then_inc(s["mix"], 1)
            v.wait_ge(s["mix"], n + 2)
            nc.vector.scalar_tensor_tensor(b.mixd[:, :], b.mixd[:, :], 0.5, b.out_older[:, :],
                                           ALU.mult, ALU.add).then_inc(s["mix"], 1)
        elif what == "fin" and kind == "mix":
            v.wait_ge(s["st_free"], k.at("st") + 1 + ST_SLOTS)
            tile = (e - 3) * BT + g
            xs = b.x[:, bass.ds(tile, 1), :]
            nc.vector.tensor_tensor(xs, xs, b.th[:, None, P * g:P * g + P], ALU.add).then_inc(s["x_added"], 1)
            v.wait_ge(s["x_added"], BT * k.at("fin") + g + 2)
            nc.vector.bn_stats(b.bn[:, bass.ds(tile, 1), :], xs).then_inc(b.bn_done, 1)

    run_prologue(k, body)
    run_steps(v, k, body)


def macaron(nc, a, out):
    with ExitStack() as ctx:
        def sb(name, shape, dt=F32):
            return ctx.enter_context(nc.sbuf_tensor(name, shape, dt))

        passed = ctx.enter_context(nc.semaphore("passed"))

        def sems(prefix, names):
            return {"passed": passed, **{n: ctx.enter_context(nc.semaphore(f"{prefix}_{n}")) for n in names}}

        b = Buffers()
        b.banks = ctx.enter_context(nc.psum_tensor("banks", [P, 8, 512], F32))
        x = sb("x", [P, T])
        b.x = x[:, :].rearrange("p (t f) -> p t f", f=C)
        b.xc = x[:, :].rearrange("p (c n) -> p c n", n=CH)
        b.xb = x[:, :].rearrange("p (c n) -> p c n", n=SEQ)
        b.xn = sb("xn", [P, CT, C])
        b.xT = sb("xT", [P, CH])
        b.bn = sb("bn", [P, TILES, 6])
        b.ln = sb("ln", [P, 6, TILES])
        b.ident = sb("ident", [P, P])
        b.ones = sb("ones", [1, P])
        b.warm = sb("warm", [1, 6])
        parts = sb("parts", [P, 4 * HB * CH], F32R)
        quarter = [parts[:, HB * CH * n:HB * CH * (n + 1)].rearrange("p (k n) -> p k n", n=CH) for n in range(4)]
        b.h_hi, b.h_lo, b.g_hi, b.g_lo = quarter
        b.k_own = parts[:, 0:NH * SEQ].rearrange("p (h n) -> p h n", n=SEQ)
        wide = sb("wide", [P, 2 * T], F32R)
        b.xh_all, b.xl_all = wide[:, 0:T], wide[:, T:2 * T]
        b.k_rec = wide[:, 0:NH * PAST * SEQ].rearrange("p (h n) -> p h n", n=PAST * SEQ)
        b.y = sb("y", [P, CH])
        b.xh = sb("xh", [P, CH], F32R)
        b.xl = sb("xl", [P, CH], F32R)
        b.k0u = sb("k0u", [P, 2, 512], U8)
        b.k1u = sb("k1u", [P, HB, 512], U8)
        b.k2u = sb("k2u", [P, HB, C], U8)
        b.k0f = b.y
        b.k0 = sb("k0", [P, 512], F32R)
        b.k1 = sb("k1", [P, HB, 512], F32R)
        b.k2 = sb("k2", [P, HB, C], F32R)
        b.sc = sb("sc", [P, 16])
        b.ffn_scale = b.sc[:, 15:16]
        b.wq0 = sb("wq0", [P, C])
        b.wkv0 = sb("wkv0", [P, 2 * C])
        b.wp0 = sb("wp0", [P, C])
        b.pb0 = sb("pb0", [P, C])
        b.blockmask = sb("blockmask", [P, 2 * C])
        work = sb("work", [P, P_SLOTS * 4 * SEQ])
        b.h_raw = work[:, P_SLOTS * 4 * SEQ - HB * CH:].rearrange("p (k n) -> p k n", n=CH)
        b.kv = work[:, 0:3 * CH].rearrange("p (t n) -> p t n", t=CT)
        b.kvm = work[:, 3 * CH:4 * CH].rearrange("p (e n) -> p e n", e=2)
        b.den, b.ratio, b.qT = (work[:, n * CH:(n + 1) * CH] for n in (4, 5, 6))
        b.wr = sb("wr", [P, NE])
        b.br = sb("br", [P, NE])
        b.b1 = sb("b1", [P, NE * HB])
        b.b2 = sb("b2", [P, NE])
        b.iota8 = sb("iota8", [P, NE])
        b.w1_raw = sb("w1_raw", [P, 512])
        b.w2_raw = sb("w2_raw", [P, HB, C])
        b.w1h, b.w1l, b.w2h, b.w2l = (sb(n, [P, 2, 512], F32R) for n in ("w1h", "w1l", "w2h", "w2l"))
        b.lg = sb("lg", [P, CT, NE])
        b.top = sb("top", [P, CT, 8])
        b.idx = sb("idx", [P, CT, 8], U32)
        b.idxf = sb("idxf", [P, TILES, 2])
        b.rt = sb("rt", [P, 4, TILES])
        b.oh = work[:, 0:2 * TILES * NE].rearrange("p (k t e) -> p k t e", k=2, e=NE)
        b.wfe = sb("wfe", [P, TILES * NE])
        b.wf = b.wfe[:, :].rearrange("p (t e) -> p t e", e=NE)
        b.wq, b.wk, b.wrq, b.wrk = (sb(n, [P, C]) for n in ("wq", "wk", "wrq", "wrk"))
        b.bq, b.bk, b.brq, b.brk = (sb(n, [P, 1]) for n in ("bq", "bk", "brq", "brk"))
        b.wv, b.wrv, b.wo = (sb(n, [P, C]) for n in ("wv", "wrv", "wo"))
        b.wg = sb("wg", [P, 2, C])
        b.brv = sb("brv", [1, C])
        b.bv, b.bo, b.bg = (sb(n, [P, 1]) for n in ("bv", "bo", "bg"))
        b.pastT = sb("pastT", [P, PAST * SEQ])
        b.headmask = sb("headmask", [QK, 4])
        b.sel = sb("sel", [P, NH + NH * PAST])
        b.q_own, b.q_rec = (sb(n, [P, NG, SEQ], F32R) for n in ("q_own", "q_rec"))
        b.k_split, b.q_split, b.rq_split = b.w1h, b.w1l, b.w2h
        b.k_parts, b.q_parts, b.rq_parts = (sb(n, [QK, NG, SEQ]) for n in ("k_parts", "q_parts", "rq_parts"))
        b.past_split = b.w2l
        b.past_parts = work[0:QK, 4 * (P_SLOTS - 2) * SEQ:].rearrange("p (g n) -> p g n", g=NG)
        b.m_own, b.m_rec = (sb(n, [P, BT, QK + P], F32R) for n in ("m_own", "m_rec"))
        b.p = work[:, :].rearrange("p (k n) -> p k n", k=P_SLOTS)
        b.v_own = sb("v_own", [P, BT, NH, VW])
        b.v_rec = sb("v_rec", [P, PAST * BT, NH, VW])
        b.pvs = sb("pvs", [P, 2, SEQ])
        b.inv = sb("inv", [P, 2, BT, 4])
        b.rec_tmp = sb("rec_tmp", [P, BT, 4, D])
        b.ctx, b.rctx = (b.w1_raw[:, SEQ * n:SEQ * n + SEQ].rearrange("p (j f) -> p j f", f=C) for n in range(2))
        b.outT = b.w2_raw[:, 0:2, :].rearrange("p k c -> p (k c)")
        b.out_kept, b.out_older = b.wkv0[:, :], b.blockmask[:, :]
        b.th, b.mixd, b.ctxT = b.y[:, 0:SEQ], b.y[:, SEQ:2 * SEQ], b.xT[:, SEQ:2 * SEQ]
        b.rcT = b.xn[:, BT:2 * BT, :].rearrange("p j f -> p (j f)")

        loads = {
            "ffn": [(b.k0u[:, :, :], a["L0_ffn_k0"].rearrange("(h p) n -> p h n", p=P)),
                    (b.k1u[:, :, :], a["L0_ffn_k1"].rearrange("(k p) n -> p k n", p=P)),
                    (b.k2u[:, :, :], a["L0_ffn_k2"].rearrange("(k p) n -> p k n", p=P)),
                    (b.sc[:, 0:3], a["s_cols"]), (b.ident[:, :], a["ident"])],
            "lin": [(b.wq0[:, :], a["wqkv0_t"][:, 0:C]), (b.wkv0[:, :], a["wqkv0_t"][:, C:3 * C]),
                    (b.wp0[:, :], a["wproj0_t"]), (b.pb0[:, :], a["pb_rows"]),
                    (b.blockmask[:, :], a["blockmask"])],
            "moe": [(b.wr[:, :], a["L1_ffn_Wr"]), (b.br[:, :], a["br_rows"]),
                    (b.b1[:, :], a["b1_t"]), (b.b2[:, :], a["b2_t"]), (b.iota8[:, :], a["iota8"])],
            "att": [(b.wq[:, :], a["L1_attn_Wq"]), (b.wk[:, :], a["L1_attn_Wk"]), (b.wrq[:, :], a["L1_attn_Wrq"]),
                    (b.wrk[:, :], a["L1_attn_Wrk"]),
                    (b.wv[:, :], a["L1_attn_Wv"]), (b.wrv[:, :], a["L1_attn_Wrv"]), (b.wo[:, :], a["L1_attn_Wo"]),
                    (b.wg[:, :, :], a["L1_attn_Wg"].rearrange("(h p) n -> p h n", p=P)),
                    (b.brv[:, :], a["L1_attn_brv"].rearrange("(o f) -> o f", o=1)),
                    (b.pastT[:, :], a["past_t"]), (b.headmask[:, :], a["headmask"]),
                    (b.sel[QK:P, :], a["sel"])]
                   + [(dst[:, :], a[n].rearrange("(p o) -> p o", o=1)) for dst, n in
                      ((b.bq, "L1_attn_bq"), (b.bk, "L1_attn_bk"), (b.brq, "L1_attn_brq"), (b.brk, "L1_attn_brk"),
                       (b.bv, "L1_attn_bv"), (b.bo, "L1_attn_bo"), (b.bg, "L1_attn_bg"))],
        }
        b.n_loads = {name: len(group) for name, group in loads.items()}
        b.loaded = sems("loaded", loads)
        b.drafts = {kind: a["draft_" + kind] for kind in ("past", "k", "q", "rq")}
        b.W1, b.W2 = a["L1_ffn_W1"], a["L1_ffn_W2"]
        x_in = [ctx.enter_context(nc.semaphore(f"x_in{c}")) for c in range(NCH)]
        b.bn_done = ctx.enter_context(nc.semaphore("bn_done"))
        x_out = ctx.enter_context(nc.semaphore("x_out"))
        setup = sems("setup", ["signs", "abs", "diff", "weights", "fills"])
        layer_sems = [sems("ffn_a", FFN_SEMS), sems("lin", LIN_SEMS), sems("ffn_b", FFN_SEMS),
                      sems("moe_a", MOE_SEMS), sems("att", ATT_SEMS), sems("moe_b", MOE_SEMS)]
        ffn_a, lin, ffn_b, moe_a, att, moe_b = layer_sems
        b.weights_ready = setup["weights"]
        block = ctx.enter_context(nc.Block())
        x_dram = a["L0_attn_x"].rearrange("e (j p) f -> p (e j) f", p=P)
        out_dram = out.rearrange("e (j p) f -> p (e j) f", p=P)

        @block.sync
        def _(sp):
            for c in range(NCH):
                sp.dma_start(b.x[:, CT * c:CT * c + CT, :], x_dram[:, CT * c:CT * c + CT, :]).then_inc(x_in[c], 16)
            for name in ("lin", "moe", "att"):
                for dst, src in loads[name]:
                    sp.dma_start(dst, src).then_inc(b.loaded[name], 16)
            moe_sync(sp, nc, b, moe_a)
            sp.wait_ge(moe_a["weights_split"], 2 * NE + 2)
            att_sync(sp, nc, b, att)
            sp.wait_ge(moe_b["var"], 1)
            moe_sync(sp, nc, b, moe_b)
            for c in range(NCH):
                sp.wait_ge(moe_b["x_added"], NCH * (NE - 1) + c + 1 + 2)
                sp.dma_start(out_dram[:, CT * c:CT * c + CT, :], b.x[:, CT * c:CT * c + CT, :]).then_inc(x_out, 16)
            sp.wait_ge(x_out, 16 * NCH)

        @block.scalar
        def _(act):
            for dst, src in loads["ffn"]:
                act.dma_start(dst, src).then_inc(b.loaded["ffn"], 16)
            act.wait_ge(b.loaded["ffn"], 16 * b.n_loads["ffn"])
            ffn_scalar(act, nc, b, ffn_a, 0)
            lin_scalar(act, nc, b, lin, 1)
            ffn_scalar(act, nc, b, ffn_b, 2)
            act.wait_ge(b.loaded["moe"], 16 * b.n_loads["moe"])
            moe_scalar(act, nc, b, moe_a, 3)
            act.wait_ge(b.loaded["att"], 16 * b.n_loads["att"])
            att_scalar(act, nc, b, att, 4)
            moe_scalar(act, nc, b, moe_b, 5)

        @block.gpsimd
        def _(pool):
            pool.wait_ge(b.loaded["ffn"], 16 * b.n_loads["ffn"])
            nc.gpsimd.tensor_scalar(b.k2[:, :, :], b.k2u[:, :, :], 2.0, -1.0, ALU.mult, ALU.add).then_inc(setup["weights"], 1)
            pool.wait_ge(setup["signs"], 5)
            nc.gpsimd.tensor_scalar(b.k1[:, :, :], b.k1u[:, :, :], b.sc[:, 10:11], b.sc[:, 12:13],
                                    ALU.mult, ALU.add).then_inc(setup["weights"], 1)
            nc.gpsimd.memset(b.ones[:, :], 1.0).then_inc(setup["fills"], 1)
            nc.gpsimd.memset(b.kv[:, :, 2 * C:3 * C], 1.0).then_inc(setup["fills"], 1)
            nc.gpsimd.memset(b.v_own[:, :, :, D:D + 1], 1.0).then_inc(setup["fills"], 1)
            nc.gpsimd.memset(b.v_rec[:, :, :, D:D + 1], 1.0).then_inc(setup["fills"], 1)
            nc.gpsimd.memset(b.v_own[:, :, :, D + 1:VW], 0.0).then_inc(setup["fills"], 1)
            nc.gpsimd.memset(b.v_rec[:, :, :, D + 1:VW], 0.0).then_inc(setup["fills"], 1)
            nc.gpsimd.memset(b.m_own[:, :, :].bitcast(F32), 0.0).then_inc(setup["fills"], 1)
            nc.gpsimd.memset(b.m_rec[:, :, :].bitcast(F32), 0.0).then_inc(setup["fills"], 1)
            pool.wait_ge(b.loaded["lin"], 16 * b.n_loads["lin"])
            lin_gpsimd(pool, nc, b, lin)
            moe_gpsimd(pool, nc, b, moe_a)
            att_gpsimd(pool, nc, b, att)
            pool.wait_ge(moe_b["var"], 1)
            moe_gpsimd(pool, nc, b, moe_b)

        @block.tensor
        def _(pe):
            pe.wait_ge(b.loaded["ffn"], 16 * b.n_loads["ffn"])
            pe.wait_ge(setup["weights"], 1)
            ffn_tensor(pe, nc, b, ffn_a)
            pe.wait_ge(b.loaded["lin"], 16 * b.n_loads["lin"])
            pe.wait_ge(setup["fills"], 8)
            lin_tensor(pe, nc, b, lin)
            ffn_tensor(pe, nc, b, ffn_b)
            pe.wait_ge(b.loaded["moe"], 16 * b.n_loads["moe"])
            moe_tensor(pe, nc, b, moe_a)
            att_tensor(pe, nc, b, att)
            moe_tensor(pe, nc, b, moe_b)

        @block.vector
        def _(v):
            for c in range(NCH):
                v.wait_ge(x_in[c], 16)
                for t in range(CT * c, CT * c + CT):
                    nc.vector.bn_stats(b.bn[:, t, :], b.x[:, t, :]).then_inc(b.bn_done, 1)
            v.wait_ge(b.loaded["ffn"], 16 * b.n_loads["ffn"])
            pos, neg, sign, twice, minus = (b.sc[:, n:n + 2] for n in (3, 5, 7, 9, 11))
            s01 = b.sc[:, 0:2]
            nc.vector.tensor_scalar(pos, s01, 0.0, None, ALU.is_gt).then_inc(setup["signs"], 1)
            nc.vector.tensor_scalar(neg, s01, 0.0, None, ALU.is_lt).then_inc(setup["signs"], 1)
            v.wait_ge(setup["signs"], 2)
            nc.vector.tensor_tensor(sign, pos, neg, ALU.subtract).then_inc(setup["signs"], 1)
            v.wait_ge(setup["signs"], 3)
            nc.vector.tensor_scalar(twice, sign, 2.0, None, ALU.mult).then_inc(setup["signs"], 1)
            nc.vector.tensor_scalar(minus, sign, -1.0, None, ALU.mult).then_inc(setup["signs"], 1)
            nc.vector.tensor_tensor(b.sc[:, 13:15], s01, sign, ALU.mult).then_inc(setup["abs"], 1)
            nc.vector.tensor_tensor(b.k0f[:, :], b.k0u[:, 0, :], b.k0u[:, 1, :], ALU.subtract).then_inc(setup["diff"], 1)
            v.wait_ge(setup["signs"], 5)
            v.wait_ge(setup["abs"], 1)
            nc.vector.scalar_tensor_tensor(b.sc[:, 13:14], b.sc[:, 13:14], 2.0, b.sc[:, 14:15],
                                           ALU.mult, ALU.mult).then_inc(setup["abs"], 1)
            v.wait_ge(setup["abs"], 2)
            nc.vector.tensor_tensor(b.ffn_scale, b.sc[:, 13:14], b.sc[:, 2:3], ALU.mult).then_inc(setup["abs"], 1)
            v.wait_ge(setup["diff"], 1)
            nc.vector.tensor_scalar(b.k0[:, :], b.k0f[:, :], twice[:, 0:1], None, ALU.mult).then_inc(setup["weights"], 1)
            ffn_vector(v, nc, b, ffn_a, 0)
            v.wait_ge(b.loaded["lin"], 16 * b.n_loads["lin"])
            lin_vector(v, nc, b, lin, 1)
            ffn_vector(v, nc, b, ffn_b, 2)
            v.wait_ge(b.loaded["moe"], 16 * b.n_loads["moe"])
            moe_vector(v, nc, b, moe_a, 3, stats=True)
            v.wait_ge(setup["fills"], 8)
            att_vector(v, nc, b, att, 4)
            moe_vector(v, nc, b, moe_b, 5, stats=False)


def kernel(**inputs):
    import numpy as np
    import concourse.bacc as bacc
    from concourse.bass_utils import run_bass_kernel_spmd

    given = {n: np.asarray(v) for n, v in inputs.items()}
    arrays = {n: given[n] for n in (
        "L0_attn_x", "L0_ffn_k0", "L0_ffn_k1", "L0_ffn_k2", "L1_attn_Wv", "L1_attn_bv",
        "L1_attn_Wq", "L1_attn_bq", "L1_attn_Wk", "L1_attn_bk", "L1_attn_Wrq", "L1_attn_brq", "L1_attn_Wrk", "L1_attn_brk",
        "L1_attn_Wo", "L1_attn_bo", "L1_attn_Wrv", "L1_attn_brv", "L1_attn_Wg", "L1_attn_bg", "L1_ffn_Wr",
        "L1_ffn_W1", "L1_ffn_W2")}
    arrays["wqkv0_t"] = given["L0_attn_qkv_weight"].T
    arrays["wproj0_t"] = given["L0_attn_proj_weight"].T
    arrays["s_cols"] = np.tile(np.stack([given["L0_ffn_s0"], given["L0_ffn_s1"], given["L0_ffn_s2"]]).reshape(1, 3), (P, 1))
    arrays["pb_rows"] = np.tile(given["L0_attn_proj_bias"], (P, 1))
    arrays["br_rows"] = np.tile(given["L1_ffn_br"], (P, 1))
    arrays["b1_t"] = given["L1_ffn_b1"].reshape(NE * HB, P).T
    arrays["b2_t"] = given["L1_ffn_b2"].T
    arrays["past_t"] = given["L1_attn_past_states"].reshape(PAST * SEQ, C).T
    f = np.arange(P)
    arrays["ident"] = np.eye(P, dtype=np.float32)
    mask = (f[:, None] // 4 == f[None, :] // 4).astype(np.float32)
    arrays["blockmask"] = np.concatenate([mask, mask], axis=1)
    arrays["iota8"] = np.tile(np.arange(NE, dtype=np.float32), (P, 1))
    arrays["headmask"] = (f[:QK, None] % 32 // D == np.arange(4)[None, :]).astype(np.float32)
    sel = np.zeros((32, NH + NH * PAST), np.float32)
    for h in range(NH):
        for a in range(PAST):
            rows = slice(4 * (h % 4) + 2 * a, 4 * (h % 4) + 2 * a + 2)
            if a == 0:
                sel[rows, h] = -1.0
            sel[rows, NH + h * PAST + a] = -1.0
    arrays["sel"] = sel

    nc = bacc.Bacc("TRN2", target_bir_lowering=False, num_devices=1)
    feed, args = {}, {}
    for name, arr in arrays.items():
        arr = np.ascontiguousarray(arr)
        feed[f"in_{name}"] = arr
        args[name] = nc.dram_tensor(f"in_{name}", arr.shape, mybir.dt.from_np(arr.dtype), kind="ExternalInput").ap()
    for kind, width in (("past", PAST * SEQ), ("k", SEQ), ("q", SEQ), ("rq", SEQ)):
        args["draft_" + kind] = nc.dram_tensor("draft_" + kind, (P, 2, width), F32, kind="Internal").ap()
    out = nc.dram_tensor("out_x", (BATCH, SEQ, C), F32, kind="ExternalOutput").ap()
    macaron(nc, args, out)
    result = run_bass_kernel_spmd(nc, [feed], core_ids=[0])
    return result.results[0]["out_x"]
```
